# Optimizing a Trainium2 kernel written in Bass

```python
import numpy as np
import jax
import jax.numpy as jnp

def _softmax(x, axis=-1):
    return jax.nn.softmax(x, axis=axis)

def _gelu(x):
    return jax.nn.gelu(x, approximate=True)

def _silu(x):
    return jax.nn.silu(x)

def _sigmoid(x):
    return jax.nn.sigmoid(x)

def _layernorm(x, axis=-1, eps=1e-05):
    m = jnp.mean(x, axis=axis, keepdims=True)
    v = jnp.var(x, axis=axis, keepdims=True)
    return (x - m) / jnp.sqrt(v + eps)

def _scatter_add(tgt, idx, src, axis=0):
    return tgt.at[idx].add(src)

def _segment_sum(src, seg, n):
    return jax.ops.segment_sum(src, seg, n)
kernel_name = 'mk_audio_tower_d2_tok_audfeat512_r4_2d0ece'

def setup_inputs(seed: int=0):
    np.random.seed(seed)
    _w = jnp.asarray

    def _rec_inputs():
        import jax
        import jax.numpy as jnp
        _rk = jax.random.key(seed)
        x = -0.000356955 + 1 * jax.random.normal(jax.random.fold_in(_rk, 1), (64, 196, 96), jnp.float32)
        return x
    x = _rec_inputs()

    def _L0_tok_setup():
        import jax, jax.numpy as jnp
        import numpy as np
        import itertools
        B, RES, RES_, STRIDE = (64, 14, 7, 2)
        N, N_ = (RES * RES, RES_ * RES_)
        IN_DIM, OUT_DIM = (96, 128)
        H, KD, AR = (12, 32, 2)
        D = AR * KD
        DH = D * H
        NH_KD = KD * H
        KV_H = DH + NH_KD
        EPS = 1e-05

        def _bias_idxs():
            points = list(itertools.product(range(RES), range(RES)))
            points_ = list(itertools.product(range(RES_), range(RES_)))
            offsets, idxs = ({}, [])
            for p1 in points_:
                for p2 in points:
                    off = (abs(p1[0] * STRIDE - p2[0]), abs(p1[1] * STRIDE - p2[1]))
                    if off not in offsets:
                        offsets[off] = len(offsets)
                    idxs.append(offsets[off])
            return (np.array(idxs, dtype=np.int32).reshape(N_, N), len(offsets))

        def linear_bn(x, w, gamma, beta, mean, var):
            s = gamma / jnp.sqrt(var + EPS)
            return jnp.matmul(x, w.T) * s + (beta - mean * s)
        key = jax.random.key(seed)
        ks = jax.random.split(key, 12)
        idxs_np, n_off = _bias_idxs()

        def bn_params(k, dim):
            k1, k2, k3, k4 = jax.random.split(k, 4)
            return (jax.random.normal(k1, (dim,)) * 0.1 + 1.0, jax.random.normal(k2, (dim,)) * 0.1, jax.random.normal(k3, (dim,)) * 0.1, jax.random.uniform(k4, (dim,), minval=0.5, maxval=1.5))
        kv_g, kv_b, kv_m, kv_v = bn_params(ks[1], KV_H)
        q_g, q_b, q_m, q_v = bn_params(ks[3], NH_KD)
        pr_g, pr_b, pr_m, pr_v = bn_params(ks[5], OUT_DIM)
        return {'x': jax.random.normal(ks[0], (B, N, IN_DIM), dtype=jnp.float32), 'kv_w': jax.random.normal(ks[6], (KV_H, IN_DIM), dtype=jnp.float32) * IN_DIM ** (-0.5), 'kv_g': kv_g, 'kv_b': kv_b, 'kv_m': kv_m, 'kv_v': kv_v, 'q_w': jax.random.normal(ks[7], (NH_KD, IN_DIM), dtype=jnp.float32) * IN_DIM ** (-0.5), 'q_g': q_g, 'q_b': q_b, 'q_m': q_m, 'q_v': q_v, 'proj_w': jax.random.normal(ks[8], (OUT_DIM, DH), dtype=jnp.float32) * DH ** (-0.5), 'proj_g': pr_g, 'proj_b': pr_b, 'proj_m': pr_m, 'proj_v': pr_v, 'attention_biases': jax.random.normal(ks[9], (H, n_off), dtype=jnp.float32) * 0.02, 'bias_idxs': jnp.asarray(idxs_np)}
    _L0_tok_all = _L0_tok_setup()
    _L0_tok_in = {k: v for k, v in _L0_tok_all.items() if k in ('kv_w', 'kv_g', 'kv_b', 'kv_m', 'kv_v', 'q_w', 'q_g', 'q_b', 'q_m', 'q_v', 'proj_w', 'proj_g', 'proj_b', 'proj_m', 'proj_v', 'attention_biases', 'bias_idxs')}
    del _L0_tok_all

    def _L0_attn_setup():
        import jax, jax.numpy as jnp
        import numpy as np
        B, M, D = (4, 1024, 128)
        BAND = D // 4

        def _rot_tables(m, d):
            half = jnp.arange(d // 2, dtype=jnp.float32)
            theta = jnp.float32(10000.0) ** (-2.0 * (half - 1.0) / d)
            ang = jnp.arange(m, dtype=jnp.float32)[:, None] * theta[None, :]
            return (jnp.cos(ang), jnp.sin(ang))

        def _apply_R(t, cos, sin):
            te, to = (t[..., 0::2], t[..., 1::2])
            oe = te * cos + to * sin
            oo = -te * sin + to * cos
            return jnp.stack([oe, oo], axis=-1).reshape(t.shape)
        key = jax.random.key(seed)
        k0, k1, k2, k3, k4 = jax.random.split(key, 5)
        x = jax.random.normal(k0, (B, M, D), dtype=jnp.float32)
        idx = jnp.arange(D)
        diff = idx[:, None] - idx[None, :]
        band_mask = ((diff >= 0) & (diff <= BAND + 1)).astype(jnp.float32)
        W_q = jax.random.normal(k1, (D, D), dtype=jnp.float32) * 0.02 * band_mask
        W_k = jax.random.normal(k2, (D, D), dtype=jnp.float32) * 0.02 * band_mask
        u_v = jax.random.normal(k3, (D, 1), dtype=jnp.float32) * 0.02
        v_v = jax.random.normal(k4, (1, D), dtype=jnp.float32) * 0.02
        return {'x': x, 'W_q': W_q, 'W_k': W_k, 'u_v': u_v, 'v_v': v_v}
    _L0_attn_all = _L0_attn_setup()
    _L0_attn_in = {k: v for k, v in _L0_attn_all.items() if k in ('W_q', 'W_k', 'u_v', 'v_v')}
    del _L0_attn_all

    def _L0_ffn_setup():
        import jax, jax.numpy as jnp
        import numpy as np
        MARK_AX, OP_ADD, OP_SUB = (0, 1, 2)
        ALU_LO, ALU_HI = (16, 32)
        AX_CARRY_LO, AX_CARRY_HI = (48, 64)
        OPCODE_BASE = 80
        OUTPUT_LO, OUTPUT_HI, CARRY = (128, 144, 160)
        NIB_A, NIB_B, OP_START = (0, 1, 10)
        RESULT, CARRY_OUT = (100, 101)
        GE_POS, GE_DIM = (8, 160)
        OPC_ADD, OPC_SUB = (25, 26)
        B, S, D = (8, 1024, 128)

        def _decode_nibble(x, base):
            return jnp.argmax(x[..., base:base + 16] > 0.5, axis=-1).astype(x.dtype)

        def _pipeline(h, W, b):
            for i in range(3):
                h = jnp.einsum('bspd,od->bspo', h, W[i]) + b[i]
                if i < 2:
                    h = jax.nn.relu(h)
            return h
        key = jax.random.key(seed)
        kx, k1, k2, k3, k4 = jax.random.split(key, 5)
        x_bd = jax.random.uniform(kx, (B, S, D), dtype=jnp.float32)
        Wa = jax.random.normal(k1, (3, GE_DIM, GE_DIM), dtype=jnp.float32) * 0.05
        ba = jax.random.normal(k2, (3, GE_DIM), dtype=jnp.float32) * 0.05
        Ws = jax.random.normal(k3, (3, GE_DIM, GE_DIM), dtype=jnp.float32) * 0.05
        bs = jax.random.normal(k4, (3, GE_DIM), dtype=jnp.float32) * 0.05
        return {'x_bd': x_bd, 'Wa': Wa, 'ba': ba, 'Ws': Ws, 'bs': bs}
    _L0_ffn_all = _L0_ffn_setup()
    _L0_ffn_in = {k: v for k, v in _L0_ffn_all.items() if k in ('Wa', 'ba', 'Ws', 'bs')}
    del _L0_ffn_all

    def _L1_attn_setup():
        import jax, jax.numpy as jnp
        import numpy as np
        D_MODEL, N_HEADS, D_KEYS, D_LLM = (128, 8, 16, 1024)
        B, L, S = (32, 256, 250)
        HE = N_HEADS * D_KEYS
        key = jax.random.key(seed)
        ks = jax.random.split(key, 11)
        s = 0.02
        return {'target_embedding': jax.random.normal(ks[0], (B, L, D_MODEL), jnp.float32), 'source_embedding': jax.random.normal(ks[1], (S, D_LLM), jnp.float32), 'value_embedding': jax.random.normal(ks[2], (S, D_LLM), jnp.float32), 'Wq': jax.random.normal(ks[3], (D_MODEL, HE), jnp.float32) * s, 'bq': jnp.zeros((HE,), jnp.float32), 'Wk': jax.random.normal(ks[4], (D_LLM, HE), jnp.float32) * s, 'bk': jnp.zeros((HE,), jnp.float32), 'Wv': jax.random.normal(ks[5], (D_LLM, HE), jnp.float32) * s, 'bv': jnp.zeros((HE,), jnp.float32), 'Wo': jax.random.normal(ks[6], (HE, D_MODEL), jnp.float32) * s, 'bo': jnp.zeros((D_MODEL,), jnp.float32)}
    _L1_attn_all = _L1_attn_setup()
    _L1_attn_in = {k: v for k, v in _L1_attn_all.items() if k in ('source_embedding', 'value_embedding', 'Wq', 'bq', 'Wk', 'bk', 'Wv', 'bv', 'Wo', 'bo')}
    del _L1_attn_all

    def _L1_ffn_setup():
        import jax, jax.numpy as jnp
        import numpy as np
        NUM_TILES = 64
        TPC = 8
        GRID = 16
        EPS = 1e-05
        key = jax.random.key(seed)
        ks = jax.random.split(key, 6)
        B, S, D, T, DH, G = (2, 256, 128, NUM_TILES, 128, GRID)
        x = jax.random.normal(ks[0], (B, S, D), dtype=jnp.float32)
        gamma = jnp.ones((D,), jnp.float32)
        beta = jnp.zeros((D,), jnp.float32)
        Wd = jax.random.normal(ks[1], (T, DH, D), dtype=jnp.float32) * 0.02
        spline_bases = jax.random.normal(ks[2], (T, DH, G), dtype=jnp.float32) * 0.1
        spline_slopes = jax.random.normal(ks[3], (T, DH, G), dtype=jnp.float32) * 0.1
        Wu = jax.random.normal(ks[4], (T, D, DH), dtype=jnp.float32) * 0.02
        scale = jnp.full((T,), 0.1, jnp.float32)
        return {'x': x, 'gamma': gamma, 'beta': beta, 'Wd': Wd, 'spline_bases': spline_bases, 'spline_slopes': spline_slopes, 'Wu': Wu, 'scale': scale}
    _L1_ffn_all = _L1_ffn_setup()
    _L1_ffn_in = {k: v for k, v in _L1_ffn_all.items() if k in ('gamma', 'beta', 'Wd', 'spline_bases', 'spline_slopes', 'Wu', 'scale')}
    del _L1_ffn_all
    return {'x': x, 'L0_tok_kv_w': _L0_tok_in['kv_w'], 'L0_tok_kv_g': _L0_tok_in['kv_g'], 'L0_tok_kv_b': _L0_tok_in['kv_b'], 'L0_tok_kv_m': _L0_tok_in['kv_m'], 'L0_tok_kv_v': _L0_tok_in['kv_v'], 'L0_tok_q_w': _L0_tok_in['q_w'], 'L0_tok_q_g': _L0_tok_in['q_g'], 'L0_tok_q_b': _L0_tok_in['q_b'], 'L0_tok_q_m': _L0_tok_in['q_m'], 'L0_tok_q_v': _L0_tok_in['q_v'], 'L0_tok_proj_w': _L0_tok_in['proj_w'], 'L0_tok_proj_g': _L0_tok_in['proj_g'], 'L0_tok_proj_b': _L0_tok_in['proj_b'], 'L0_tok_proj_m': _L0_tok_in['proj_m'], 'L0_tok_proj_v': _L0_tok_in['proj_v'], 'L0_tok_attention_biases': _L0_tok_in['attention_biases'], 'L0_tok_bias_idxs': _L0_tok_in['bias_idxs'], 'L0_attn_W_q': _L0_attn_in['W_q'], 'L0_attn_W_k': _L0_attn_in['W_k'], 'L0_attn_u_v': _L0_attn_in['u_v'], 'L0_attn_v_v': _L0_attn_in['v_v'], 'L0_ffn_Wa': _L0_ffn_in['Wa'], 'L0_ffn_ba': _L0_ffn_in['ba'], 'L0_ffn_Ws': _L0_ffn_in['Ws'], 'L0_ffn_bs': _L0_ffn_in['bs'], 'L1_attn_source_embedding': _L1_attn_in['source_embedding'], 'L1_attn_value_embedding': _L1_attn_in['value_embedding'], 'L1_attn_Wq': _L1_attn_in['Wq'], 'L1_attn_bq': _L1_attn_in['bq'], 'L1_attn_Wk': _L1_attn_in['Wk'], 'L1_attn_bk': _L1_attn_in['bk'], 'L1_attn_Wv': _L1_attn_in['Wv'], 'L1_attn_bv': _L1_attn_in['bv'], 'L1_attn_Wo': _L1_attn_in['Wo'], 'L1_attn_bo': _L1_attn_in['bo'], 'L1_ffn_gamma': _L1_ffn_in['gamma'], 'L1_ffn_beta': _L1_ffn_in['beta'], 'L1_ffn_Wd': _L1_ffn_in['Wd'], 'L1_ffn_spline_bases': _L1_ffn_in['spline_bases'], 'L1_ffn_spline_slopes': _L1_ffn_in['spline_slopes'], 'L1_ffn_Wu': _L1_ffn_in['Wu'], 'L1_ffn_scale': _L1_ffn_in['scale']}

def reference(x, L0_tok_kv_w, L0_tok_kv_g, L0_tok_kv_b, L0_tok_kv_m, L0_tok_kv_v, L0_tok_q_w, L0_tok_q_g, L0_tok_q_b, L0_tok_q_m, L0_tok_q_v, L0_tok_proj_w, L0_tok_proj_g, L0_tok_proj_b, L0_tok_proj_m, L0_tok_proj_v, L0_tok_attention_biases, L0_tok_bias_idxs, L0_attn_W_q, L0_attn_W_k, L0_attn_u_v, L0_attn_v_v, L0_ffn_Wa, L0_ffn_ba, L0_ffn_Ws, L0_ffn_bs, L1_attn_source_embedding, L1_attn_value_embedding, L1_attn_Wq, L1_attn_bq, L1_attn_Wk, L1_attn_bk, L1_attn_Wv, L1_attn_bv, L1_attn_Wo, L1_attn_bo, L1_ffn_gamma, L1_ffn_beta, L1_ffn_Wd, L1_ffn_spline_bases, L1_ffn_spline_slopes, L1_ffn_Wu, L1_ffn_scale):
    import jax
    import jax.numpy as jnp

    def _L0_tok_ref(x, kv_w, kv_g, kv_b, kv_m, kv_v, q_w, q_g, q_b, q_m, q_v, proj_w, proj_g, proj_b, proj_m, proj_v, attention_biases, bias_idxs):
        import jax, jax.numpy as jnp
        import numpy as np
        import itertools
        B, RES, RES_, STRIDE = (64, 14, 7, 2)
        N, N_ = (RES * RES, RES_ * RES_)
        IN_DIM, OUT_DIM = (96, 128)
        H, KD, AR = (12, 32, 2)
        D = AR * KD
        DH = D * H
        NH_KD = KD * H
        KV_H = DH + NH_KD
        EPS = 1e-05

        def _bias_idxs():
            points = list(itertools.product(range(RES), range(RES)))
            points_ = list(itertools.product(range(RES_), range(RES_)))
            offsets, idxs = ({}, [])
            for p1 in points_:
                for p2 in points:
                    off = (abs(p1[0] * STRIDE - p2[0]), abs(p1[1] * STRIDE - p2[1]))
                    if off not in offsets:
                        offsets[off] = len(offsets)
                    idxs.append(offsets[off])
            return (np.array(idxs, dtype=np.int32).reshape(N_, N), len(offsets))

        def linear_bn(x, w, gamma, beta, mean, var):
            s = gamma / jnp.sqrt(var + EPS)
            return jnp.matmul(x, w.T) * s + (beta - mean * s)
        Bsz = x.shape[0]
        scale = KD ** (-0.5)
        kv = linear_bn(x, kv_w, kv_g, kv_b, kv_m, kv_v).reshape(Bsz, N, H, KD + D)
        k, v = (kv[..., :KD], kv[..., KD:])
        xs = x.reshape(Bsz, RES, RES, IN_DIM)[:, ::STRIDE, ::STRIDE].reshape(Bsz, N_, IN_DIM)
        q = linear_bn(xs, q_w, q_g, q_b, q_m, q_v).reshape(Bsz, N_, H, KD)
        bias = attention_biases[:, bias_idxs]
        attn = jnp.einsum('bqhd,bkhd->bhqk', q, k) * scale + bias
        attn = jax.nn.softmax(attn, axis=-1)
        out = jnp.einsum('bhqk,bkhd->bqhd', attn, v).reshape(Bsz, N_, DH)
        out = jax.nn.hard_swish(out)
        return linear_bn(out, proj_w, proj_g, proj_b, proj_m, proj_v)

    def _L0_attn_ref(x, W_q, W_k, u_v, v_v):
        import jax, jax.numpy as jnp
        import numpy as np
        B, M, D = (4, 1024, 128)
        BAND = D // 4

        def _rot_tables(m, d):
            half = jnp.arange(d // 2, dtype=jnp.float32)
            theta = jnp.float32(10000.0) ** (-2.0 * (half - 1.0) / d)
            ang = jnp.arange(m, dtype=jnp.float32)[:, None] * theta[None, :]
            return (jnp.cos(ang), jnp.sin(ang))

        def _apply_R(t, cos, sin):
            te, to = (t[..., 0::2], t[..., 1::2])
            oe = te * cos + to * sin
            oo = -te * sin + to * cos
            return jnp.stack([oe, oo], axis=-1).reshape(t.shape)
        b, m, d = x.shape
        q = x @ W_q
        k = x @ W_k
        v = x @ u_v @ v_v
        cos, sin = _rot_tables(m, d)
        qr = _apply_R(q, cos, sin)
        kr = _apply_R(k, cos, sin)
        scores = jnp.einsum('bqd,bkd->bqk', qr, kr) / jnp.sqrt(jnp.float32(d))
        causal = jnp.tril(jnp.ones((m, m), dtype=bool))
        scores = jnp.where(causal, scores, jnp.float32(-jnp.inf))
        attn = jax.nn.softmax(scores, axis=-1)
        return attn @ v

    def _L0_ffn_ref(x_bd, Wa, ba, Ws, bs):
        import jax, jax.numpy as jnp
        import numpy as np
        MARK_AX, OP_ADD, OP_SUB = (0, 1, 2)
        ALU_LO, ALU_HI = (16, 32)
        AX_CARRY_LO, AX_CARRY_HI = (48, 64)
        OPCODE_BASE = 80
        OUTPUT_LO, OUTPUT_HI, CARRY = (128, 144, 160)
        NIB_A, NIB_B, OP_START = (0, 1, 10)
        RESULT, CARRY_OUT = (100, 101)
        GE_POS, GE_DIM = (8, 160)
        OPC_ADD, OPC_SUB = (25, 26)
        B, S, D = (8, 1024, 128)

        def _decode_nibble(x, base):
            return jnp.argmax(x[..., base:base + 16] > 0.5, axis=-1).astype(x.dtype)

        def _pipeline(h, W, b):
            for i in range(3):
                h = jnp.einsum('bspd,od->bspo', h, W[i]) + b[i]
                if i < 2:
                    h = jax.nn.relu(h)
            return h
        x = x_bd
        Bsz, seq, _ = x.shape
        x_ge = jnp.zeros((Bsz, seq, GE_POS, GE_DIM), dtype=x.dtype)
        x_ge = x_ge.at[..., 0, NIB_A].set(_decode_nibble(x, ALU_LO))
        x_ge = x_ge.at[..., 1, NIB_A].set(_decode_nibble(x, ALU_HI))
        x_ge = x_ge.at[..., 0, NIB_B].set(_decode_nibble(x, AX_CARRY_LO))
        x_ge = x_ge.at[..., 1, NIB_B].set(_decode_nibble(x, AX_CARRY_HI))
        x_ge = x_ge.at[..., :, OP_START + OPC_ADD].set(x[..., OPCODE_BASE + OPC_ADD][..., None])
        x_ge = x_ge.at[..., :, OP_START + OPC_SUB].set(x[..., OPCODE_BASE + OPC_SUB][..., None])
        mark = x[..., MARK_AX] > 0.5
        m_add = mark & (x[..., OP_ADD] > 0.5)
        m_sub = mark & ~(x[..., OP_ADD] > 0.5) & (x[..., OP_SUB] > 0.5)
        active = (m_add | m_sub).astype(x.dtype)
        y_add = _pipeline(x_ge, Wa, ba)
        y_sub = _pipeline(x_ge, Ws, bs)
        y = jnp.where(m_add[..., None, None], y_add, jnp.where(m_sub[..., None, None], y_sub, x_ge))
        res_lo = jnp.clip(jnp.round(y[..., 0, RESULT]), 0, 15).astype(jnp.int32)
        res_hi = jnp.clip(jnp.round(y[..., 1, RESULT]), 0, 15).astype(jnp.int32)
        oh_lo = jax.nn.one_hot(res_lo, 16, dtype=x.dtype) * active[..., None]
        oh_hi = jax.nn.one_hot(res_hi, 16, dtype=x.dtype) * active[..., None]
        carry = (jnp.round(y[..., 1, CARRY_OUT]) > 0.5).astype(x.dtype) * active
        out = x
        out = out.at[..., OUTPUT_LO:OUTPUT_LO + 16].add(2.0 * oh_lo)
        out = out.at[..., OUTPUT_HI:OUTPUT_HI + 16].add(2.0 * oh_hi)
        out = out.at[..., CARRY].add(carry)
        return out

    def _L1_attn_ref(target_embedding, source_embedding, value_embedding, Wq, bq, Wk, bk, Wv, bv, Wo, bo):
        import jax, jax.numpy as jnp
        import numpy as np
        D_MODEL, N_HEADS, D_KEYS, D_LLM = (128, 8, 16, 1024)
        B, L, S = (32, 256, 250)
        HE = N_HEADS * D_KEYS
        H, E = (N_HEADS, D_KEYS)
        Bb, Ll, _ = target_embedding.shape
        Ss = source_embedding.shape[0]
        q = (target_embedding @ Wq + bq).reshape(Bb, Ll, H, E)
        k = (source_embedding @ Wk + bk).reshape(Ss, H, E)
        v = (value_embedding @ Wv + bv).reshape(Ss, H, E)
        scale = 1.0 / jnp.sqrt(jnp.asarray(E, q.dtype))
        scores = jnp.einsum('blhe,she->bhls', q, k)
        attn = jax.nn.softmax(scale * scores, axis=-1)
        out = jnp.einsum('bhls,she->blhe', attn, v).reshape(Bb, Ll, H * E)
        return out @ Wo + bo

    def _L1_ffn_ref(x, gamma, beta, Wd, spline_bases, spline_slopes, Wu, scale):
        import jax, jax.numpy as jnp
        import numpy as np
        NUM_TILES = 64
        TPC = 8
        GRID = 16
        EPS = 1e-05
        B, S, D = x.shape
        T, DH, _ = Wd.shape
        C = T // TPC
        N = B * S
        mu = x.mean(-1, keepdims=True)
        var = ((x - mu) ** 2).mean(-1, keepdims=True)
        xn = (x - mu) * jax.lax.rsqrt(var + EPS) * gamma + beta
        xf = xn.reshape(N, D)
        tile_sigs = jnp.sign(Wd.mean(axis=1))
        cluster_sigs = jnp.sign(tile_sigs.reshape(C, TPC, D).mean(1))
        in_sigs = jnp.sign(xf)
        best_c = jnp.argmax(in_sigs @ cluster_sigs.T, axis=-1)
        tile_scores = (in_sigs @ tile_sigs.T).reshape(N, C, TPC)
        sc = jnp.take_along_axis(tile_scores, best_c[:, None, None], axis=1)[:, 0, :]
        local_best = jnp.argmax(sc, axis=-1)
        tidx = best_c * TPC + local_best
        h = jnp.einsum('nd,nhd->nh', xf, Wd[tidx])
        hn = jax.nn.sigmoid(h)
        idx = jnp.clip((hn * GRID).astype(jnp.int32), 0, GRID - 1)
        base = jnp.take_along_axis(spline_bases[tidx], idx[..., None], axis=-1)[..., 0]
        slope = jnp.take_along_axis(spline_slopes[tidx], idx[..., None], axis=-1)[..., 0]
        local_pos = hn * GRID - idx.astype(h.dtype)
        hs = base + slope * local_pos
        y = jnp.einsum('nh,ndh->nd', hs, Wu[tidx]) * scale[tidx][:, None]
        return x + y.reshape(B, S, D)
    h = _L0_tok_ref(x, L0_tok_kv_w, L0_tok_kv_g, L0_tok_kv_b, L0_tok_kv_m, L0_tok_kv_v, L0_tok_q_w, L0_tok_q_g, L0_tok_q_b, L0_tok_q_m, L0_tok_q_v, L0_tok_proj_w, L0_tok_proj_g, L0_tok_proj_b, L0_tok_proj_m, L0_tok_proj_v, L0_tok_attention_biases, L0_tok_bias_idxs)
    h = h + _L0_attn_ref(_layernorm(h, axis=-1), L0_attn_W_q, L0_attn_W_k, L0_attn_u_v, L0_attn_v_v)
    h = h + _L0_ffn_ref(_layernorm(h, axis=-1), L0_ffn_Wa, L0_ffn_ba, L0_ffn_Ws, L0_ffn_bs)
    h = h + _L1_attn_ref(_layernorm(h, axis=-1), L1_attn_source_embedding, L1_attn_value_embedding, L1_attn_Wq, L1_attn_bq, L1_attn_Wk, L1_attn_bk, L1_attn_Wv, L1_attn_bv, L1_attn_Wo, L1_attn_bo)
    h = h + _L1_ffn_ref(_layernorm(h, axis=-1), L1_ffn_gamma, L1_ffn_beta, L1_ffn_Wd, L1_ffn_spline_bases, L1_ffn_spline_slopes, L1_ffn_Wu, L1_ffn_scale)
    return h

_drawn_inputs = setup_inputs


def setup_inputs(seed=0):
    import zlib

    import numpy as np

    out = dict(_drawn_inputs(seed))
    spreads = {'L1_attn_bq': (0.0, 0.8),
     'L1_attn_bk': (0.0, 2.0),
     'L1_attn_bv': (0.0, 2.0),
     'L1_attn_bo': (0.0, 0.8),
     'L1_ffn_gamma': (1.0, 0.6),
     'L1_ffn_beta': (0.0, 2.0),
     'L1_ffn_scale': (0.10000000149011612, 0.6)}
    factors = {'L0_tok_attention_biases': 7.983,
     'L0_attn_W_q': 8.0,
     'L0_attn_W_k': 8.0,
     'L0_attn_v_v': 2.767,
     'L1_attn_source_embedding': 8.0,
     'L1_attn_value_embedding': 7.35,
     'L1_attn_Wq': 8.0,
     'L1_attn_Wk': 8.0,
     'L1_attn_Wv': 7.65,
     'L1_attn_Wo': 2.694,
     'L1_ffn_Wd': 31.771,
     'L1_ffn_spline_bases': 30.536,
     'L1_ffn_spline_slopes': 51.269,
     'L1_ffn_Wu': 26.116}
    for name, (base, spread) in spreads.items():
        noise = np.random.default_rng([zlib.crc32(name.encode()), seed]).standard_normal(out[name].shape)
        drawn = base * np.exp(spread * noise) if base else spread * noise
        out[name] = jnp.asarray(drawn.astype(out[name].dtype))
    for name, factor in factors.items():
        out[name] = (out[name] * factor).astype(out[name].dtype)
    return out
```

```python
from contextlib import ExitStack

import concourse.bass as bass
from concourse import mybir

ALU = mybir.AluOpType
ACT = mybir.ActivationFunctionType
AX_X = mybir.AxisListType.X
F32 = mybir.dt.float32
BF16 = mybir.dt.bfloat16
I32 = mybir.dt.int32
U16 = mybir.dt.uint16
U32 = mybir.dt.uint32

EPS = 1e-5
BATCH, RES, RESQ, DIM_IN, DIM = 64, 14, 7, 96, 128
KEYS, QUERIES = RES * RES, RESQ * RESQ
HEADS, KD, VD = 12, 32, 64
AUG = DIM_IN + 1
TOKENS = BATCH * QUERIES
ROWS = 2 * QUERIES
TILES = TOKENS // ROWS
KHALF = KEYS // 2
GROUP = 4
GROUPS = BATCH // GROUP
GTOK = GROUP * QUERIES
HQ = HEADS * QUERIES
CH = 118
CHUNKS = 5
CHUNK_AT = [0, CH, 2 * CH, 3 * CH, HQ - CH]
PIECES = [(0, 1), (2, 3), (4,)]


def at_least(eng, sem, count):
    if isinstance(count, int) and count <= 0:
        return
    eng.wait_ge(sem, count)


def carry_waits(eng, tally):
    eng.sem_inc(tally, 1)


class Stage(ExitStack):

    def __init__(self, nc):
        super().__init__()
        self.nc, self.sems = nc, []

    def semaphore(self, name):
        self.sems.append(self.nc.alloc_semaphore(name))
        return self.sems[-1]

    def __exit__(self, *error):
        handled = super().__exit__(*error)
        if error[0] is None:
            self.nc.clear_and_free_semaphores(self.sems)
            self.nc.all_engine_barrier(sem_only=True)
        return handled


def bc(ap, shape):
    return ap.to_broadcast(shape)


def setup_stage(nc, a, k, outer):
    with Stage(nc) as ctx:
        sb = lambda n, s, d=F32: ctx.enter_context(nc.sbuf_tensor(n, s, d))
        sem = lambda n: ctx.semaphore(n)
        qw, kw = sb("qw", [KD, HEADS, DIM_IN]), sb("kw", [KD, HEADS, DIM_IN])
        vw = sb("vw", [VD, HEADS, DIM_IN])
        qp, kp, vp = sb("qp", [KD, 4, HEADS]), sb("kp", [KD, 4, HEADS]), sb("vp", [VD, 4, HEADS])
        pp = sb("pp", [128, 4, DIM])
        qaug, kaug, vaug = sb("qaug", [KD, HEADS, AUG]), sb("kaug", [KD, HEADS, AUG]), sb("vaug", [VD, HEADS, AUG])
        rt_q, rt_k, rt_v, rt_p = sb("rt_q", [KD, HEADS]), sb("rt_k", [KD, HEADS]), sb("rt_v", [VD, HEADS]), sb("rt_p", [128, DIM])
        sc_q, sc_k, sc_v, sc_p = sb("sc_q", [KD, HEADS]), sb("sc_k", [KD, HEADS]), sb("sc_v", [VD, HEADS]), sb("sc_p", [128, DIM])
        tm_q, tm_k, tm_v, tm_p = sb("tm_q", [KD, HEADS]), sb("tm_k", [KD, HEADS]), sb("tm_v", [VD, HEADS]), sb("tm_p", [128, DIM])
        PIECE = KEYS * QUERIES // 7
        STRIP = PIECE // 4
        idx = sb("idx", [KHALF, 2, PIECE], I32)
        onehot = sb("onehot", [KHALF, 2, 2, PIECE])
        ab = sb("ab", [KHALF, 2, HEADS])
        off_col = sb("off_col", [KHALF, 2])
        brow = sb("brow", [HEADS, 2, PIECE])

        loaded, idx_in = sem("loaded"), [sem("idx_in0"), sem("idx_in1")]
        chain, root, ready, m_full, m_out = sem("chain"), sem("root"), sem("ready"), sem("m_full"), sem("m_out")
        hot, b_full, b_out, v_full, table_in = sem("hot"), sem("b_full"), sem("b_out"), sem("v_full"), sem("table_in")
        b_stored = [sem("b_stored0"), sem("b_stored1")]
        bank = k.banks
        idx_src = a["bias_idx"]
        sets = [(qw, qp, qaug, rt_q, sc_q, tm_q), (kw, kp, kaug, rt_k, sc_k, tm_k), (vw, vp, vaug, rt_v, sc_v, tm_v)]
        LOADS = 11
        block = ctx.enter_context(nc.Block())

        @block.sync
        def _(sp):
            for dst, src in ((qw, "q_w"), (kw, "k_w"), (vw, "v_w"), (qp, "q_bn"), (kp, "k_bn"), (vp, "v_bn"),
                             (k.pw, "proj_w"), (k.ident, "ident"), (ab, "bias_t"), (off_col, "off_col")):
                sp.dma_start(dst[:], a[src]).then_inc(loaded, 16)
            sp.dma_start(pp[:], a["proj_bn"].partition_broadcast(128)).then_inc(loaded, 16)
            for p in range(7):
                if p >= 2:
                    sp.wait_ge(hot, 2 * (p - 1))
                sp.dma_start(idx[:, p % 2, :], idx_src[p * PIECE:(p + 1) * PIECE].partition_broadcast(KHALF)).then_inc(idx_in[p % 2], 16)
                if p >= 1:
                    sp.wait_ge(b_out, 4 * p)
                    sp.dma_start(k.bias_dram[:, (p - 1) * PIECE:p * PIECE], brow[:, (p - 1) % 2, :]).then_inc(b_stored[(p - 1) % 2], 16)
            sp.wait_ge(b_out, 28)
            sp.dma_start(k.bias_dram[:, 6 * PIECE:], brow[:, 0, :]).then_inc(b_stored[0], 16)
            sp.wait_ge(b_stored[0], 16 * 4)
            sp.wait_ge(b_stored[1], 16 * 3)
            flat = k.bias_dram.rearrange("h (q n) -> (h q) n", n=KEYS)
            sp.dma_start(k.bias[:, 0:4, :], flat[0:4 * CH, :].rearrange("(c r) n -> r c n", c=4)).then_inc(table_in, 16)
            sp.dma_start(k.bias[:, 4, :], flat[HQ - CH:HQ, :]).then_inc(table_in, 16)
            sp.wait_ge(table_in, 32)

        @block.vector
        def _(dve):
            n = [0]

            def link(ins):
                n[0] += 1
                ins.then_inc(chain, 1)
                dve.wait_ge(chain, n[0])

            for u in range(2):
                nc.vector.memset(k.xT[DIM_IN:AUG, u, :], 1.0)
                nc.vector.memset(k.xn[:, u, :, :, DIM_IN:AUG], 1.0)
            nc.vector.memset(k.three[:], 3.0)
            dve.wait_ge(loaded, 16 * LOADS)
            for i, (w, p, aug, rt, sc, tm) in enumerate(sets):
                nc.vector.tensor_scalar(rt[:], p[:, 3, :], EPS, None, ALU.add).then_inc(ready, 1)
            nc.vector.tensor_scalar(rt_p[:], pp[:, 3, :], EPS, None, ALU.add).then_inc(ready, 1)
            dve.wait_ge(root, 4)
            for i, (w, p, aug, rt, sc, tm) in enumerate(sets):
                link(nc.vector.reciprocal(tm[:], rt[:]))
                link(nc.vector.tensor_tensor(sc[:], tm[:], p[:, 0, :], ALU.mult))
                link(nc.vector.tensor_tensor(tm[:], p[:, 2, :], sc[:], ALU.mult))
                link(nc.vector.tensor_tensor(aug[:, :, DIM_IN], p[:, 1, :], tm[:], ALU.subtract))
                link(nc.vector.tensor_tensor(aug[:, :, 0:DIM_IN], w[:], bc(sc[:].unsqueeze(2), list(w.shape)), ALU.mult))
            nc.vector.tensor_copy(tm_q[:], sc_q[:]).then_inc(ready, 1)
            link(nc.vector.reciprocal(tm_p[:], rt_p[:]))
            link(nc.vector.tensor_tensor(sc_p[:], tm_p[:], pp[:, 0, :], ALU.mult))
            link(nc.vector.tensor_tensor(tm_p[:], pp[:, 2, :], sc_p[:], ALU.mult))
            link(nc.vector.tensor_tensor(k.prow[:], pp[:, 1, :], tm_p[:], ALU.subtract))
            link(nc.vector.tensor_scalar(sc_p[:], sc_p[:], 1.0 / 6.0, None, ALU.mult))
            link(nc.vector.tensor_tensor(k.pw[:], k.pw[:], bc(sc_p[:].unsqueeze(1), [128, 6, DIM]), ALU.mult))
            for j in range(3):
                dve.wait_ge(m_full, j + 1)
                nc.vector.tensor_copy(k.mh[:, 4 * j:4 * j + 4, :],
                                      bank[j][0:AUG, 0:4 * AUG].rearrange("p (h r) -> p h r", h=4))
            for j in range(2):
                dve.wait_ge(v_full, j + 1)
                nc.vector.tensor_copy(k.wv[:, 6 * j:6 * j + 6, :],
                                      bank[3 + j][0:AUG, 0:6 * VD].rearrange("p (h r) -> p h r", h=6))
            for p in range(7):
                dve.wait_ge(idx_in[p % 2], 16 * (p // 2 + 1))
                if p >= 2:
                    dve.wait_ge(b_full, 4 * (p - 1))
                for c in range(2):
                    nc.vector.tensor_scalar(onehot[:, p % 2, c, :], idx[:, p % 2, :], off_col[:, c:c + 1], None,
                                            ALU.is_equal).then_inc(hot, 1)

        @block.scalar
        def _(act):
            act.wait_ge(ready, 4)
            for rt in (rt_q, rt_k, rt_v, rt_p):
                nc.scalar.activation(rt[:], rt[:], ACT.Sqrt).then_inc(root, 1)
            for p in range(7):
                if p >= 2:
                    act.wait_ge(b_stored[p % 2], 16 * (p // 2))
                for t in range(4):
                    act.wait_ge(b_full, 4 * p + t + 1)
                    nc.scalar.activation(brow[:, p % 2, t * STRIP:(t + 1) * STRIP],
                                         bank[5 + (4 * p + t) % 3][0:HEADS, 0:STRIP], ACT.Copy).then_inc(b_out, 1)

        @block.tensor
        def _(pe):
            pe.wait_ge(ready, 5)
            for h in range(HEADS):
                mm = nc.tensor.matmul(bank[h // 4][0:AUG, (h % 4) * AUG:(h % 4 + 1) * AUG], qaug[:, h, :], kaug[:, h, :],
                                      start=True, stop=True)
                if h % 4 == 3:
                    mm.then_inc(m_full, 1)
            for h in range(HEADS):
                mm = nc.tensor.transpose(bank[3 + h // 6][0:AUG, (h % 6) * VD:(h % 6 + 1) * VD], vaug[:, h, :],
                                         k.ident[0:VD, 0:VD])
                if h % 6 == 5:
                    mm.then_inc(v_full, 1)
            for p in range(7):
                pe.wait_ge(hot, 2 * (p + 1))
                for t in range(4):
                    if 4 * p + t >= 3:
                        pe.wait_ge(b_out, 4 * p + t - 2)
                    for c in range(2):
                        mm = nc.tensor.matmul(bank[5 + (4 * p + t) % 3][0:HEADS, 0:STRIP], ab[:, c, :],
                                              onehot[:, p % 2, c, t * STRIP:(t + 1) * STRIP],
                                              start=(c == 0), stop=(c == 1))
                    mm.then_inc(b_full, 1)


def token_stage(nc, a, k):
    with Stage(nc) as ctx:
        sb = lambda n, s, d=F32: ctx.enter_context(nc.sbuf_tensor(n, s, d))
        sem = lambda n: ctx.semaphore(n)
        qt = sb("qt", [AUG, 2, GROUP, HQ])
        sbias = sb("sbias", [CH, 2, CHUNKS, KEYS])
        prob = sb("prob", [CH, 2, CHUNKS, KEYS])
        low = sb("low", [CH, 2, CHUNKS])
        tally = sem("tally")
        total = sb("total", [CH, 2, CHUNKS])
        inv = sb("inv", [CH, 2, CHUNKS])
        pt = sb("pt", [KHALF, 2, 2, HQ])
        px = sb("px", [AUG, 2, HEADS, GTOK])
        shifted = sb("shifted", [128, 2, 2, GTOK])
        hs = sb("hs", [128, 2, 6, GTOK])
        xT_in, xn_in = [sem("xT_in0"), sem("xT_in1")], [sem("xn_in0"), sem("xn_in1")]
        s_full, s_max, p_exp, inv_done, p_norm = sem("s_full"), sem("s_max"), sem("p_exp"), sem("inv_done"), sem("p_norm")
        t_full, t_out, px_full, px_out = sem("t_full"), sem("t_out"), sem("px_full"), sem("px_out")
        q_full, q_out, o_full, o_relu, o_hs = sem("q_full"), sem("q_out"), sem("o_full"), sem("o_relu"), sem("o_hs")
        h_full, h_out = sem("h_full"), sem("h_out")
        s_bank, t_bank, px_bank, m_bank = k.banks[0:3], k.banks[3:5], k.banks[5:7], k.banks[7]
        BODY = 2 * GROUP
        STEPS = BATCH // BODY

        def run(eng, slot):
            slot_range = range(BODY)
            for j in slot_range:
                slot(0, j)
            with eng.Fori(1, STEPS - 1) as it:
                for j in slot_range:
                    slot(it, j)
            for it in (STEPS - 1, STEPS):
                for j in slot_range:
                    slot(it, j)
            slot(STEPS + 1, 0)

        def live(it, j, back, count=BATCH):
            return not isinstance(it, int) or 0 <= BODY * it + j - back < count

        def group_live(it, u, back):
            return not isinstance(it, int) or 0 <= 2 * it + u - back < GROUPS

        SHARED = [[("h", 0)], [("q", 0), ("q", 1), ("q", 2)], [("q", 3), ("q", 4), ("o", 0)], [("q", 5), ("o", 1), ("o", 2)]]
        BACK = {"q": -1, "h": 2, "o": 1}
        PER = {"q": 6, "h": 1, "o": 3}

        def shared_before(it, u, i, n):
            seen = {"q": 0, "h": 0, "o": 0}
            for ii in range(i + 1):
                for nn, (kind, _) in enumerate(SHARED[ii]):
                    if (ii, nn) < (i, n):
                        seen[kind] += 1
            out = {}
            for kind, c in seen.items():
                count = PER[kind] * (2 * it + u - BACK[kind]) + c
                if isinstance(it, int):
                    count = min(max(count, 0), PER[kind] * GROUPS)
                out[kind] = count
            return out

        order = [x for row in SHARED for x in row]

        @(block := ctx.enter_context(nc.Block())).sync
        def _(sp):
            def load_keys(g, u):
                sp.dma_start(k.xT[0:DIM_IN, u, :], a["xT"][:, bass.ds(g * GROUP * KEYS, GROUP * KEYS)]).then_inc(xT_in[u], 16)

            def load_rows(g, u):
                sp.dma_start(k.xn[:, u, :, :, 0:DIM_IN].rearrange("p b c i -> p (b c) i"),
                             a["xn"][:, bass.ds(g * GROUP * 2, GROUP * 2), :]).then_inc(xn_in[u], 16)

            for u in range(2):
                load_keys(u, u)
                load_rows(u, u)
            with sp.Fori(0, STEPS - 1) as it:
                for u in range(2):
                    sp.wait_ge(s_full, 3 * (BODY * it + GROUP * (u + 1)))
                    load_keys(2 * it + 2 + u, u)
                    sp.wait_ge(px_full, 2 * (BODY * it + GROUP * (u + 1)))
                    load_rows(2 * it + 2 + u, u)

        def rolled(j):
            return j // GROUP, j % GROUP

        @block.tensor
        def _(pe):
            def shared(it, u, i, n, kind, m):
                if not group_live(it, u, BACK[kind]):
                    return
                done = {"q": q_out, "h": h_out, "o": o_hs}
                before = shared_before(it, u, i, n)
                if isinstance(it, int):
                    for name, c in before.items():
                        at_least(pe, done[name], c)
                else:
                    prev = order[order.index((kind, m)) - 1][0]
                    at_least(pe, done[prev], before[prev])
                par = (u - BACK[kind]) % 2
                if kind == "q":
                    if m == 0:
                        pe.wait_ge(xT_in[par], 16 * (it + (1 if u == 0 else 2)))
                    for hh in range(2):
                        src = k.xT[:, par, :].rearrange("p (b r s c t) -> p b r s c t", b=GROUP, r=RESQ, s=2, c=RESQ)[:, :, :, 0, :, 0]
                        mm = nc.tensor.matmul(m_bank[0:AUG, hh * GTOK:(hh + 1) * GTOK], k.mh[:, 2 * m + hh, :],
                                              src, start=True, stop=True)
                    mm.then_inc(q_full, 1)
                elif kind == "o":
                    if m == 0:
                        at_least(pe, px_out, 2 * GROUP * (2 * it + u))
                    for jj in range(2):
                        for hh in range(2):
                            mm = nc.tensor.matmul(m_bank[64 * hh:64 * hh + 64, jj * GTOK:(jj + 1) * GTOK],
                                                  k.wv[:, 4 * m + 2 * jj + hh, :], px[:, par, 4 * m + 2 * jj + hh, :],
                                                  start=True, stop=True)
                    mm.then_inc(o_full, 1)
                else:
                    at_least(pe, o_hs, 3 * (2 * it + u - 1))
                    for t in range(2):
                        for j in range(6):
                            mm = nc.tensor.matmul(m_bank[0:ROWS, t * DIM:(t + 1) * DIM],
                                                  hs[:, par, j, t * ROWS:(t + 1) * ROWS], k.pw[:, j, :],
                                                  start=(j == 0), stop=(j == 5))
                    mm.then_inc(h_full, 1)

            def slot(it, j):
                u, i = rolled(j)
                s = BODY * it + j
                if live(it, j, 0):
                    if i == 0:
                        at_least(pe, q_out, 6 * (2 * it + u + 1))
                    for p, chunks in enumerate(PIECES):
                        if live(it, j, 1):
                            pe.wait_ge(s_max, 5 * (s - 1) + chunks[-1] + 1)
                        for n, c in enumerate(chunks):
                            mm = nc.tensor.matmul(s_bank[p][0:CH, n * KEYS:(n + 1) * KEYS],
                                                  qt[:, u, i, CHUNK_AT[c]:CHUNK_AT[c] + CH],
                                                  k.xT[:, u, i * KEYS:(i + 1) * KEYS], start=True, stop=True)
                        mm.then_inc(s_full, 1)
                def turn_piece(p, chunks):
                    if not live(it, j, 1):
                        return
                    par = (j - 1) % 2
                    pe.wait_ge(p_norm, 3 * (s - 1) + p + 1)
                    at_least(pe, t_out, 3 * (s - 1) + p - 1)
                    for n, c in enumerate(chunks):
                        for kc in range(2):
                            mm = nc.tensor.transpose(
                                t_bank[(3 * (j - 1) + p) % 2][0:KHALF, (2 * n + kc) * CH:(2 * n + kc + 1) * CH],
                                prob[:, par, c, kc * KHALF:(kc + 1) * KHALF], k.ident[0:CH, 0:CH])
                    mm.then_inc(t_full, 1)

                def weigh(half):
                    if not live(it, j, 2):
                        return
                    bu, bi = rolled((j - 2) % BODY)
                    if half == 0:
                        if bi == 0:
                            pe.wait_ge(xn_in[bu], 16 * (it + 1))
                        pe.wait_ge(t_out, 3 * (s - 1))
                    at_least(pe, px_out, 2 * (s - 3) + half + 1)
                    for kc in range(2):
                        mm = nc.tensor.matmul(px_bank[half][0:AUG, 0:HQ // 2], k.xn[:, bu, bi, kc, :],
                                              pt[:, j % 2, kc, half * (HQ // 2):(half + 1) * (HQ // 2)],
                                              start=(kc == 0), stop=(kc == 1))
                    mm.then_inc(px_full, 1)

                weigh(0)
                for n in range(3):
                    if n < len(SHARED[i]):
                        shared(it, u, i, n, *SHARED[i][n])
                    if n == 0:
                        weigh(1)
                    turn_piece(n, PIECES[n])

            pe.wait_ge(xT_in[0], 16)
            for m in range(6):
                at_least(pe, q_out, m)
                for hh in range(2):
                    src = k.xT[:, 0, :].rearrange("p (b r s c t) -> p b r s c t", b=GROUP, r=RESQ, s=2, c=RESQ)[:, :, :, 0, :, 0]
                    mm = nc.tensor.matmul(m_bank[0:AUG, hh * GTOK:(hh + 1) * GTOK], k.mh[:, 2 * m + hh, :], src,
                                          start=True, stop=True)
                mm.then_inc(q_full, 1)
            run(pe, slot)

        @block.vector
        def _(dve):
            def slot(it, j):
                u, i = rolled(j)
                s = BODY * it + j
                if live(it, j, 1):
                    par = (j - 1) % 2
                    dve.wait_ge(p_exp, s)
                    nc.vector.reciprocal(inv[:, par, :], total[:, par, :]).then_inc(inv_done, 1)
                    dve.wait_ge(inv_done, s)
                    for p, chunks in enumerate(PIECES):
                        for c in chunks:
                            ins = nc.vector.tensor_scalar(prob[:, par, c, :], prob[:, par, c, :], inv[:, par, c:c + 1], None, ALU.mult)
                        ins.then_inc(p_norm, 1)
                if live(it, j, 0):
                    par = j % 2
                    for p, chunks in enumerate(PIECES):
                        dve.wait_ge(s_full, 3 * s + p + 1)
                        if p == 0 and live(it, j, 2):
                            dve.wait_ge(p_exp, s - 1)
                        carry_waits(dve, tally)
                        for n, c in enumerate(chunks):
                            nc.vector.tensor_tensor_reduce(
                                sbias[:, par, c, :], s_bank[p][0:CH, n * KEYS:(n + 1) * KEYS], k.bias[:, c, :],
                                -1.0, 3e38, ALU.add, ALU.min, low[:, par, c:c + 1]).then_inc(s_max, 1)
                if live(it, j, 2):
                    bu, bi = rolled((j - 2) % BODY)
                    if bi == 0:
                        at_least(dve, o_full, 3 * ((2 * it + (u if i >= 2 else u - 1)) - 1))
                    for half in range(2):
                        dve.wait_ge(px_full, 2 * (s - 2) + half + 1)
                        nc.vector.tensor_copy(px[:, bu, 6 * half:6 * half + 6, bi * QUERIES:(bi + 1) * QUERIES],
                                                    px_bank[half][0:AUG, 0:HQ // 2].rearrange("p (h q) -> p h q", h=6)).then_inc(px_out, 1)
                for kind, m in SHARED[i]:
                    if kind == "h" and group_live(it, u, 2):
                        dve.wait_ge(h_full, 2 * it + u - 1)
                        nc.vector.tensor_tensor(k.h[:, bass.ds(4 * it + 2 * u - 4, 2), :],
                                                m_bank[0:ROWS, 0:2 * DIM].rearrange("p (t d) -> p t d", t=2),
                                                bc(k.prow[0:ROWS, :].unsqueeze(1), [ROWS, 2, DIM]), ALU.add).then_inc(h_out, 1)
                    if kind == "o" and group_live(it, u, 1):
                        par = (u - 1) % 2
                        n = (3 * par + m) % 2
                        if m == 0:
                            at_least(dve, h_full, 2 * it + u - 1)
                        dve.wait_ge(o_relu, 3 * (2 * it + u - 1) + m + 1)
                        nc.vector.scalar_tensor_tensor(hs[:, par, 2 * m:2 * m + 2, :], shifted[:, n, :, :], 6.0,
                                                       m_bank[:, 0:2 * GTOK].rearrange("p (t d) -> p t d", t=2),
                                                       ALU.min, ALU.mult).then_inc(o_hs, 1)

            run(dve, slot)
            dve.wait_ge(h_out, GROUPS)

        @block.scalar
        def _(act):
            def evacuate_q(it, u, m, par):
                dst = qt[:, par, :, :].rearrange("p b (h q) -> p h b q", h=HEADS)
                for hh in range(2):
                    ins = nc.scalar.activation(dst[:, 2 * m + hh, :, :],
                                               m_bank[0:AUG, hh * GTOK:(hh + 1) * GTOK].rearrange("p (b q) -> p b q", b=GROUP),
                                               ACT.Copy, scale=KD ** -0.5)
                ins.then_inc(q_out, 1)

            def slot(it, j):
                u, i = rolled(j)
                s = BODY * it + j
                if live(it, j, 0):
                    par = j % 2
                    if live(it, j, 2):
                        act.wait_ge(t_full, 3 * (s - 1))
                    for c in range(CHUNKS):
                        act.wait_ge(s_max, 5 * s + c + 1)
                        ins = nc.scalar.activation(prob[:, par, c, :], sbias[:, par, c, :], ACT.Exp, bias=low[:, par, c:c + 1],
                                                   scale=-1.0, accum_out=total[:, par, c:c + 1])
                    ins.then_inc(p_exp, 1)
                def leave_shared(kind, m):
                    if kind == "q" and group_live(it, u, -1):
                        if m == 0:
                            at_least(act, s_full, 3 * GROUP * (2 * it + u))
                        act.wait_ge(q_full, 6 * (2 * it + u + 1) + m + 1)
                        evacuate_q(it, u, m, (u + 1) % 2)
                    if kind == "o" and group_live(it, u, 1):
                        par = (u - 1) % 2
                        n = (3 * par + m) % 2
                        at_least(act, o_hs, 3 * (2 * it + u - 1) + m - 1)
                        act.wait_ge(o_full, 3 * (2 * it + u - 1) + m + 1)
                        nc.scalar.activation(shifted[:, n, :, :], m_bank[:, 0:2 * GTOK].rearrange("p (t d) -> p t d", t=2),
                                             ACT.Relu, bias=k.three[:, 0:1]).then_inc(o_relu, 1)

                def leave_turned(p, chunks):
                    par = (j - 1) % 2
                    if p == 0 and live(it, j, 3):
                        act.wait_ge(px_full, 2 * (s - 2))
                    act.wait_ge(t_full, 3 * (s - 1) + p + 1)
                    src = t_bank[(3 * (j - 1) + p) % 2][0:KHALF, 0:2 * CH * len(chunks)].rearrange(
                        "p (n c r) -> p c n r", n=len(chunks), c=2)
                    at = CHUNK_AT[chunks[0]]
                    if p == 2:
                        act.wait_ge(t_out, 3 * (s - 1) + p)
                    nc.scalar.activation(pt[:, par, :, at:at + CH * len(chunks)].rearrange("p c (n r) -> p c n r", r=CH), src,
                                         ACT.Copy).then_inc(t_out, 1)

                for n in range(3):
                    if n < len(SHARED[i]):
                        leave_shared(*SHARED[i][n])
                    if live(it, j, 1):
                        leave_turned(n, PIECES[n])

            for m in range(6):
                act.wait_ge(q_full, m + 1)
                evacuate_q(0, 0, m, 0)
            run(act, slot)


def peeled(eng, steps, body):
    body(0)
    with eng.Fori(1, steps) as it:
        body(it)


class Norm:

    def __init__(self, nc, ctx, name):
        sb = lambda n, s: ctx.enter_context(nc.sbuf_tensor(f"{name}_{n}", s, F32))
        self.nc = nc
        self.raw = sb("raw", [ROWS, TILES, 6])
        self.mean, self.var, self.rstd = sb("mean", [ROWS, TILES]), sb("var", [ROWS, TILES]), sb("rstd", [ROWS, TILES])
        self.half, self.gap = sb("half", [ROWS, TILES]), sb("gap", [ROWS, TILES])
        self.rows_seen, self.chain, self.var_ready, self.root_done, self.rstd_ready = (
            ctx.semaphore(f"{name}_{n}") for n in ("rows_seen", "chain", "var_ready", "root_done", "rstd_ready"))

    def vector_part(self, dve, x):
        nc, n = self.nc, [0]

        def link(ins):
            n[0] += 1
            ins.then_inc(self.chain, 1)
            dve.wait_ge(self.chain, n[0])

        with dve.Fori(0, TILES // 4) as it:
            for t in range(4):
                nc.vector.bn_stats(self.raw[:, 4 * it + t, :], x[:, 4 * it + t, :]).then_inc(self.rows_seen, 1)
        dve.wait_ge(self.rows_seen, TILES)
        m0, c0, m1, c1 = self.raw[:, :, 1], self.raw[:, :, 2], self.raw[:, :, 4], self.raw[:, :, 5]
        link(nc.vector.tensor_tensor(self.half[:], m0, m1, ALU.add))
        link(nc.vector.tensor_scalar(self.mean[:], self.half[:], 0.5, None, ALU.mult))
        link(nc.vector.tensor_tensor(self.gap[:], m0, m1, ALU.subtract))
        link(nc.vector.tensor_tensor(self.gap[:], self.gap[:], self.gap[:], ALU.mult))
        link(nc.vector.tensor_tensor(self.half[:], c0, c1, ALU.add))
        link(nc.vector.tensor_scalar(self.half[:], self.half[:], 1.0 / DIM, EPS, ALU.mult, ALU.add))
        nc.vector.scalar_tensor_tensor(self.var[:], self.gap[:], 0.25, self.half[:], ALU.mult, ALU.add).then_inc(self.var_ready, 1)
        dve.wait_ge(self.root_done, 1)
        nc.vector.reciprocal(self.rstd[:], self.var[:]).then_inc(self.rstd_ready, 1)
        dve.wait_ge(self.rstd_ready, 1)

    def scalar_part(self, act):
        act.wait_ge(self.var_ready, 1)
        self.nc.scalar.activation(self.var[:], self.var[:], ACT.Sqrt).then_inc(self.root_done, 1)


BT = 4
BTOK = BT * ROWS


def band_stage(nc, a, k):
    with Stage(nc) as ctx:
        sb = lambda n, s, d=F32: ctx.enter_context(nc.sbuf_tensor(n, s, d))
        sem = lambda n: ctx.semaphore(n)
        norm_a, norm_b = Norm(nc, ctx, "band"), Norm(nc, ctx, "ffn")
        w = sb("band_w", [DIM, 4, DIM])
        uv = sb("uv", [DIM, 1])
        vv = sb("vv", [ROWS, DIM])
        trig = sb("trig", [DIM, 2, QUERIES])
        mask = sb("mask", [ROWS, ROWS])
        rows = sb("rows", [ROWS, 2, BT, DIM])
        xt = sb("xt", [DIM, 2, BTOK])
        turn = sb("turn", [DIM, 2, 4, BTOK])
        rot = sb("rot", [DIM, 2, 2, BTOK])
        sval = sb("sval", [DIM, 2, BTOK])
        smask = sb("smask", [ROWS, 2, BT, ROWS])
        prob = sb("bprob", [ROWS, 2, BT, ROWS])
        junk = sb("junk", [ROWS, 2, BT, ROWS])
        low, den, num = sb("blow", [ROWS, 2, BT]), sb("bden", [ROWS, 2, BT]), sb("bnum", [ROWS, 2, BT])
        tally = sem("b_tally")
        yrow = sb("yrow", [ROWS, 4, DIM])
        names = ("w_in", "rows_done", "tr", "xt_out", "proj", "s_out", "turned", "rotated", "s_full", "s_low", "p_exp",
                 "num_done", "inv_done", "ratio", "h_done", "y_done", "sum_done")
        (w_in, rows_done, tr, xt_out, proj, s_out, turned, rotated, s_full, s_low, p_exp, num_done, inv_done, ratio,
         h_done, y_done, sum_done) = (sem("b_" + n) for n in names)
        xt_bank, s_bank, v_bank, q_banks = k.banks[0], k.banks[6:8], k.banks[5], k.banks[1:5]
        STEPS = TILES // BT // 2
        block = ctx.enter_context(nc.Block())

        @block.sync
        def _(sp):
            sp.dma_start(w[:], a["band_w"]).then_inc(w_in, 16)
            sp.dma_start(uv[:], a["u_v"]).then_inc(w_in, 16)
            sp.dma_start(vv[:], a["v_v"].partition_broadcast(ROWS)).then_inc(w_in, 16)
            sp.dma_start(trig[:], a["trig"]).then_inc(w_in, 16)
            sp.dma_start(mask[:], a["band_mask"]).then_inc(w_in, 16)

        @block.vector
        def _(dve):
            norm_a.vector_part(dve, k.h)
            dve.wait_ge(w_in, 16 * 5)

            def make_rows(it, u):
                g = 2 * it + u
                at_least(dve, tr, g - 1)
                for t in range(BT):
                    tile = 4 * g + t
                    ins = nc.vector.tensor_scalar(rows[:, u, t, :], k.h[:, tile, :], norm_a.mean[:, bass.ds(tile, 1)],
                                                  norm_a.rstd[:, bass.ds(tile, 1)], ALU.subtract, ALU.mult)
                ins.then_inc(rows_done, 1)

            def rotate(it, u):
                g = 2 * it + u
                dve.wait_ge(proj, g + 1)
                at_least(dve, s_full, g - 1)
                for i in range(4):
                    ins = nc.vector.tensor_tensor(turn[:, u, i, :].rearrange("p (b q) -> p b q", q=QUERIES),
                                                  q_banks[i][:, 0:BTOK].rearrange("p (b q) -> p b q", q=QUERIES),
                                                  bc(trig[:, i % 2, :].unsqueeze(1), [DIM, BTOK // QUERIES, QUERIES]), ALU.mult)
                ins.then_inc(turned, 1)
                dve.wait_ge(turned, g + 1)
                for i in range(2):
                    ins = nc.vector.tensor_tensor(rot[:, u, i, :], turn[:, u, 2 * i, :], turn[:, u, 2 * i + 1, :], ALU.add)
                ins.then_inc(rotated, 1)

            def lowest(it, u):
                g = 2 * it + u
                dve.wait_ge(s_full, g + 1)
                at_least(dve, p_exp, g - 1)
                carry_waits(dve, tally)
                for t in range(BT):
                    ins = nc.vector.tensor_tensor_reduce(smask[:, u, t, :], s_bank[u][0:ROWS, t * ROWS:(t + 1) * ROWS], mask[:],
                                                         -(DIM ** -0.5), 3e38, ALU.add, ALU.min, low[:, u, t:t + 1])
                ins.then_inc(s_low, 1)

            def add_rows(it, u):
                g = 2 * it + u
                dve.wait_ge(p_exp, g + 1)
                dve.wait_ge(s_out, g + 1)
                for t in range(BT):
                    ins = nc.vector.tensor_tensor_reduce(junk[:, u, t, :], prob[:, u, t, :], sval[0:ROWS, u, t * ROWS:(t + 1) * ROWS],
                                                         1.0, 0.0, ALU.mult, ALU.add, num[:, u, t:t + 1])
                ins.then_inc(num_done, 1)
                nc.vector.reciprocal(den[:, u, :], den[:, u, :]).then_inc(inv_done, 1)
                dve.wait_ge(num_done, g + 1)
                dve.wait_ge(inv_done, g + 1)
                nc.vector.tensor_tensor(num[:, u, :], num[:, u, :], den[:, u, :], ALU.mult).then_inc(ratio, 1)
                dve.wait_ge(ratio, g + 1)
                for t in range(BT):
                    tile = 4 * g + t
                    ins = nc.vector.scalar_tensor_tensor(k.h[:, tile, :], vv[:], num[:, u, t:t + 1], k.h[:, tile, :],
                                                         ALU.mult, ALU.add)
                ins.then_inc(h_done, 1)

            def body(it):
                make_rows(it, 0)
                make_rows(it, 1)
                rotate(it, 0)
                lowest(it, 0)
                rotate(it, 1)
                add_rows(it, 0)
                lowest(it, 1)
                add_rows(it, 1)

            peeled(dve, STEPS, body)
            dve.wait_ge(h_done, 2 * STEPS)
            norm_b.vector_part(dve, k.h)

            def add_norm(it):
                at_least(dve, sum_done, it)
                for t in range(4):
                    tile = 4 * it + t
                    ins = nc.vector.tensor_scalar(yrow[:, t, :], k.h[:, tile, :], norm_b.mean[:, bass.ds(tile, 1)],
                                                  norm_b.rstd[:, bass.ds(tile, 1)], ALU.subtract, ALU.mult)
                ins.then_inc(y_done, 1)
                dve.wait_ge(y_done, it + 1)
                nc.vector.tensor_tensor(k.h[:, bass.ds(4 * it, 4), :], k.h[:, bass.ds(4 * it, 4), :], yrow[:], ALU.add).then_inc(sum_done, 1)

            peeled(dve, TILES // 4, add_norm)
            dve.wait_ge(sum_done, TILES // 4)

        @block.tensor
        def _(pe):
            pe.wait_ge(w_in, 16 * 5)

            def turn_rows(it, u):
                g = 2 * it + u
                pe.wait_ge(rows_done, g + 1)
                at_least(pe, xt_out, g)
                for t in range(BT):
                    mm = nc.tensor.transpose(xt_bank[:, t * ROWS:(t + 1) * ROWS], rows[:, u, t, :], k.ident[0:ROWS, 0:ROWS])
                mm.then_inc(tr, 1)

            def project(it, u):
                g = 2 * it + u
                pe.wait_ge(xt_out, g + 1)
                at_least(pe, turned, g)
                at_least(pe, s_out, g)
                for i in range(4):
                    nc.tensor.matmul(q_banks[i][:, 0:BTOK], w[:, i, :], xt[:, u, :], start=True, stop=True)
                nc.tensor.matmul(v_bank[:, 0:BTOK], bc(uv[:, 0:1], [DIM, DIM]), xt[:, u, :], start=True, stop=True).then_inc(proj, 1)

            def scores(it, u):
                g = 2 * it + u
                pe.wait_ge(rotated, g + 1)
                at_least(pe, s_low, g - 1)
                for t in range(BT):
                    mm = nc.tensor.matmul(s_bank[u][0:ROWS, t * ROWS:(t + 1) * ROWS], rot[:, u, 0, t * ROWS:(t + 1) * ROWS],
                                          rot[:, u, 1, t * ROWS:(t + 1) * ROWS], start=True, stop=True)
                mm.then_inc(s_full, 1)

            def body(it):
                turn_rows(it, 0)
                project(it, 0)
                turn_rows(it, 1)
                project(it, 1)
                scores(it, 0)
                scores(it, 1)

            peeled(pe, STEPS, body)

        @block.scalar
        def _(act):
            norm_a.scalar_part(act)

            def copy_x(it, u):
                g = 2 * it + u
                act.wait_ge(tr, g + 1)
                at_least(act, proj, g - 1)
                nc.scalar.activation(xt[:, u, :], xt_bank[:, 0:BTOK], ACT.Copy).then_inc(xt_out, 1)

            def copy_s(it, u):
                g = 2 * it + u
                act.wait_ge(proj, g + 1)
                at_least(act, num_done, g - 1)
                nc.scalar.activation(sval[:, u, :], v_bank[:, 0:BTOK], ACT.Copy).then_inc(s_out, 1)

            def expo(it, u):
                g = 2 * it + u
                act.wait_ge(s_low, g + 1)
                at_least(act, ratio, g - 1)
                for t in range(BT):
                    ins = nc.scalar.activation(prob[:, u, t, :], smask[:, u, t, :], ACT.Exp, bias=low[:, u, t:t + 1], scale=-1.0,
                                               accum_out=den[:, u, t:t + 1])
                ins.then_inc(p_exp, 1)

            def body(it):
                copy_x(it, 0)
                copy_s(it, 0)
                copy_x(it, 1)
                copy_s(it, 1)
                expo(it, 0)
                expo(it, 1)

            peeled(act, STEPS, body)
            norm_b.scalar_part(act)


XH, XE, SRC, LLM = 8, 16, 250, 1024
SHALF = SRC // 2
LCH = LLM // 128


def cross_stage(nc, a, k):
    with Stage(nc) as ctx:
        sb = lambda n, s, d=F32: ctx.enter_context(nc.sbuf_tensor(n, s, d))
        sem = lambda n: ctx.semaphore("c_" + n)
        norm = Norm(nc, ctx, "cross")
        srcT, valT = sb("srcT", [128, LCH, SRC]), sb("valT", [128, LCH, SRC])
        wk, wv = sb("cwk", [128, LCH, 2, 128]), sb("cwv", [128, LCH, DIM])
        wq, wo = sb("cwq", [DIM, 2, 128]), sb("cwo", [DIM, DIM])
        bq, bk = sb("cbq", [128, 2]), sb("cbk", [128, 2])
        bv, bo, ones = sb("cbv", [SHALF, DIM]), sb("cbo", [1, DIM]), sb("cones", [1, ROWS])
        kT = sb("kT", [128, 2, SRC])
        v = sb("cv", [SHALF, 2, DIM])
        rows, xt = sb("crows", [ROWS, 4, DIM]), sb("cxt", [DIM, BTOK])
        qT = sb("qT", [128, 2, BTOK])
        prob = sb("cprob", [ROWS, 2, XH, SRC])
        low, total, inv = sb("clow", [ROWS, 2, XH]), sb("ctotal", [ROWS, 2, XH]), sb("cinv", [ROWS, 2, XH])
        pt = sb("cpt", [SHALF, 2, XH, 2, ROWS])
        orow, ot = sb("corow", [ROWS, 2, DIM]), sb("cot", [DIM, 2, ROWS])
        names = ("w_in", "kv_full", "kv_out", "bias_done", "rows_done", "tr", "xt_out", "q_full", "q_out", "s_full", "s_low",
                 "p_exp", "t_full", "t_out", "t_last", "inv_done", "pv_full", "o_done", "ot_full", "ot_out", "wo_full", "h_done")
        (w_in, kv_full, kv_out, bias_done, rows_done, tr, xt_out, q_full, q_out, s_full, s_low,
         p_exp, t_full, t_out, t_last, inv_done, pv_full, o_done, ot_full, ot_out, wo_full, h_done) = (sem(n) for n in names)
        s_bank, t_bank, pv_bank, m_bank = k.banks[0:4], k.banks[4:6], k.banks[6], k.banks[7]
        STEPS = TILES // 4
        LOADS = 10
        table, gslope, cell = sb("table", [128, 4096]), sb("gslope", [128, 16, 128]), sb("cell", [128, 16])
        zeros = sb("zeros", [128, SLOTS // 512 * DIM])
        table_in, moe_in, zeroed, split = sem("table_in"), sem("moe_in"), sem("zeroed"), sem("split")

        def run(eng, slot):
            for j in range(4):
                slot(0, j)
            with eng.Fori(1, STEPS - 1) as it:
                for j in range(4):
                    slot(it, j)
            for it in (STEPS - 1, STEPS):
                for j in range(4):
                    slot(it, j)

        def live(it, j, back):
            return not isinstance(it, int) or 0 <= 4 * it + j - back < TILES

        block = ctx.enter_context(nc.Block())

        @block.sync
        def _(sp):
            for dst, src in ((srcT, "srcT"), (wk, "x_wk"), (valT, "valT"), (wv, "x_wv"), (wq, "x_wq"), (wo, "x_wo"),
                             (bq, "x_bq"), (bk, "x_bk"), (bo, "x_bo")):
                sp.dma_start(dst[:], a[src]).then_inc(w_in, 16)
            sp.dma_start(bv[:], a["x_bv"].partition_broadcast(SHALF)).then_inc(w_in, 16)
            sp.dma_start(table[:], a["spline"]).then_inc(table_in, 16)
            sp.dma_start(cell[:], a["cell"].partition_broadcast(128)).then_inc(table_in, 16)
            sp.dma_start(k.wd[:], a["wd"]).then_inc(moe_in, 16)
            sp.dma_start(k.wu[:], a["wu"]).then_inc(moe_in, 16)
            sp.wait_ge(zeroed, 1)
            slots = k.x_slots.rearrange("(n p r) d -> n p (r d)", n=4, p=128)
            for i in range(4):
                sp.dma_start(slots[i], zeros[:]).then_inc(moe_in, 16)
            sp.wait_ge(moe_in, 16 * 6)

        @block.gpsimd
        def _(pool):
            nc.gpsimd.memset(zeros[:], 0.0).then_inc(zeroed, 1)
            pool.wait_ge(zeroed, 1)
            nc.gpsimd.memset(k.lines_lo[EXPERTS:128, :], 0.0).then_inc(zeroed, 1)
            pool.wait_ge(zeroed, 2)
            pool.wait_ge(table_in, 32)
            tv = table[:].rearrange("p (g c h) -> p g c h", g=16, c=2)
            shape = [128, 16, 128]
            nc.gpsimd.tensor_tensor(gslope[:], tv[:, :, 1, :], bc(cell[:].unsqueeze(2), shape), ALU.mult).then_inc(split, 1)
            pool.wait_ge(split, 1)
            nc.gpsimd.tensor_tensor(tv[:, :, 0, :], tv[:, :, 0, :], gslope[:], ALU.subtract).then_inc(split, 1)
            pool.wait_ge(split, 2)
            nc.gpsimd.tensor_copy(k.lines_hi[:], table[:]).then_inc(split, 1)
            pool.wait_ge(split, 3)
            nc.gpsimd.tensor_tensor(table[:], table[:], k.lines_hi[:], ALU.subtract).then_inc(split, 1)
            pool.wait_ge(split, 4)
            nc.gpsimd.tensor_copy(k.lines_hi[64:128, :], table[64:128, :]).then_inc(split, 1)
            pool.wait_ge(split, 5)
            nc.gpsimd.tensor_copy(k.lines_lo[0:64, :], table[0:64, :]).then_inc(split, 1)
            pool.wait_ge(split, 6)
            nc.gpsimd.tensor_tensor(table[0:64, :], table[0:64, :], k.lines_lo[0:64, :], ALU.subtract).then_inc(split, 1)
            pool.wait_ge(split, 7)
            nc.gpsimd.tensor_copy(k.lines_lo[0:64, :], table[0:64, :]).then_inc(split, 1)


        @block.tensor
        def _(pe):
            pe.wait_ge(w_in, 16 * LOADS)
            for half in range(2):
                for c in range(LCH):
                    mm = nc.tensor.matmul(s_bank[half][:, 0:SRC], wk[:, c, half, :], srcT[:, c, :], start=(c == 0), stop=(c == LCH - 1))
                mm.then_inc(kv_full, 1)
            for kc in range(2):
                for c in range(LCH):
                    mm = nc.tensor.matmul(s_bank[2 + kc][0:SHALF, 0:DIM], valT[:, c, kc * SHALF:(kc + 1) * SHALF], wv[:, c, :],
                                          start=(c == 0), stop=(c == LCH - 1))
                mm.then_inc(kv_full, 1)

            def prepare(it):
                pe.wait_ge(rows_done, it + 1)
                at_least(pe, h_done, 4 * it - 4)
                for t in range(4):
                    mm = nc.tensor.transpose(m_bank[:, t * ROWS:(t + 1) * ROWS], rows[:, t, :], k.ident[0:ROWS, 0:ROWS])
                mm.then_inc(tr, 1)
                for half in range(2):
                    pe.wait_ge(xt_out, it + 1)
                    at_least(pe, q_out, 2 * it + half)
                    nc.tensor.matmul(m_bank[:, 0:BTOK], wq[:, half, :], xt[:], start=True, stop=True).then_inc(q_full, 1)

            def slot(it, j):
                t = 4 * it + j
                if live(it, j, 0):
                    if j == 0:
                        at_least(pe, q_out, 2 * it + 2)
                    for b in range(4):
                        if live(it, j, 1):
                            pe.wait_ge(p_exp, 4 * (t - 1) + b + 1)
                        elif b == 0:
                            pe.wait_ge(kv_out, 4)
                        for n in range(2):
                            mm = nc.tensor.matmul(s_bank[b][0:ROWS, n * SRC:(n + 1) * SRC],
                                                  qT[32 * b:32 * b + 32, n, j * ROWS:(j + 1) * ROWS],
                                                  kT[32 * b:32 * b + 32, n, :], start=True, stop=True)
                        mm.then_inc(s_full, 1)
                if j == 0:
                    at_least(pe, q_out, 2 * min(it + 1, STEPS) if isinstance(it, int) else 2 * it + 2)
                if live(it, j, 3):
                    par = (j - 3) % 2
                    pe.wait_ge(o_done, t - 2)
                    at_least(pe, h_done, t - 3)
                    nc.tensor.transpose(m_bank[:, 0:ROWS], orow[:, par, :], k.ident[0:ROWS, 0:ROWS]).then_inc(ot_full, 1)
                if live(it, j, 1):
                    par = (j - 1) % 2
                    for b in range(4):
                        pe.wait_ge(p_exp, 4 * (t - 1) + b + 1)
                        if b == 1:
                            at_least(pe, t_last, t - 1)
                        else:
                            at_least(pe, t_out, 3 * (t - 1) + max(b - 1, 0))
                        for n in range(2):
                            for kc in range(2):
                                mm = nc.tensor.transpose(t_bank[b % 2][0:SHALF, (2 * n + kc) * ROWS:(2 * n + kc + 1) * ROWS],
                                                         prob[:, par, 2 * b + n, kc * SHALF:(kc + 1) * SHALF], k.ident[0:ROWS, 0:ROWS])
                        mm.then_inc(t_full, 1)
                if live(it, j, 3):
                    par = (j - 3) % 2
                    pe.wait_ge(ot_out, t - 2)
                    nc.tensor.matmul(m_bank[0:ROWS, 0:DIM], ot[:, par, :], wo[:], start=True, stop=False)
                    nc.tensor.matmul(m_bank[0:ROWS, 0:DIM], ones[:], bo[:], start=False, stop=True).then_inc(wo_full, 1)
                if live(it, j, 2):
                    par = (j - 2) % 2
                    pe.wait_ge(t_out, 3 * (t - 1))
                    pe.wait_ge(t_last, t - 1)
                    at_least(pe, o_done, t - 2)
                    for h in range(XH):
                        for kc in range(2):
                            mm = nc.tensor.matmul(pv_bank[0:ROWS, h * XE:(h + 1) * XE], pt[:, par, 2 * (h % 4) + h // 4, kc, :],
                                                  v[:, kc, h * XE:(h + 1) * XE], start=(kc == 0), stop=(kc == 1))
                    mm.then_inc(pv_full, 1)
                if j == 3 and live(it, 0, -4):
                    at_least(pe, h_done, t - 2)
                    prepare(it + 1)

            prepare(0)
            run(pe, slot)

        @block.vector
        def _(dve):
            nc.vector.memset(ones[:], 1.0)
            norm.vector_part(dve, k.h)
            dve.wait_ge(w_in, 16 * LOADS)
            nc.vector.tensor_scalar(bq[:], bq[:], XE ** -0.5, None, ALU.mult).then_inc(bias_done, 1)
            for kc in range(2):
                dve.wait_ge(kv_full, 3 + kc)
                nc.vector.tensor_tensor(v[:, kc, :], s_bank[2 + kc][0:SHALF, 0:DIM], bv[:], ALU.add).then_inc(kv_out, 1)

            def make_rows(it):
                at_least(dve, tr, it)
                for t in range(4):
                    tile = 4 * it + t
                    ins = nc.vector.tensor_scalar(rows[:, t, :], k.h[:, tile, :], norm.mean[:, bass.ds(tile, 1)],
                                                  norm.rstd[:, bass.ds(tile, 1)], ALU.subtract, ALU.mult)
                ins.then_inc(rows_done, 1)

            def slot(it, j):
                t = 4 * it + j
                if live(it, j, 0):
                    par = j % 2
                    for b in range(4):
                        dve.wait_ge(s_full, 4 * t + b + 1)
                        if b == 0 and live(it, j, 2):
                            dve.wait_ge(p_exp, 4 * (t - 1))
                        nc.vector.tensor_reduce(low[:, par, 2 * b:2 * b + 2],
                                                s_bank[b][0:ROWS, 0:2 * SRC].rearrange("p (h s) -> p h s", h=2),
                                                AX_X, ALU.max, negate=True).then_inc(s_low, 1)
                if live(it, j, 1):
                    par = (j - 1) % 2
                    dve.wait_ge(p_exp, 4 * t)
                    if live(it, j, 3):
                        dve.wait_ge(o_done, t - 2)
                    nc.vector.reciprocal(inv[:, par, :], total[:, par, :]).then_inc(inv_done, 1)
                    if live(it, j, 3):
                        dve.wait_ge(pv_full, t - 2)
                    for b in range(3):
                        dve.wait_ge(t_full, 4 * (t - 1) + b + 1)
                        nc.vector.tensor_copy(pt[:, par, 2 * b:2 * b + 2, :, :].rearrange("p h c r -> p (h c r)"),
                                              t_bank[b % 2][0:SHALF, 0:4 * ROWS]).then_inc(t_out, 1)
                if live(it, j, 3):
                    par = (j - 3) % 2
                    dve.wait_ge(wo_full, t - 2)
                    tile = t - 3
                    nc.vector.tensor_tensor(k.h[:, bass.ds(tile, 1), :], m_bank[0:ROWS, 0:DIM].unsqueeze(1),
                                            k.h[:, bass.ds(tile, 1), :], ALU.add).then_inc(h_done, 1)
                if live(it, j, 2):
                    par = (j - 2) % 2
                    dve.wait_ge(inv_done, t - 1)
                    dve.wait_ge(pv_full, t - 1)
                    if live(it, j, 4):
                        dve.wait_ge(ot_full, t - 3)
                    nc.vector.tensor_tensor(orow[:, par, :].rearrange("p (n b e) -> p n b e", n=2, b=4),
                                            pv_bank[0:ROWS, 0:DIM].rearrange("p (n b e) -> p n b e", n=2, b=4),
                                            bc(inv[:, par, :].rearrange("p (b n) -> p n b", n=2).unsqueeze(3), [ROWS, 2, 4, XE]),
                                            ALU.mult).then_inc(o_done, 1)
                if j == 3 and live(it, 0, -4):
                    make_rows(it + 1)

            make_rows(0)
            run(dve, slot)
            dve.wait_ge(h_done, TILES)

        @block.scalar
        def _(act):
            norm.scalar_part(act)
            act.wait_ge(w_in, 16 * LOADS)
            for half in range(2):
                act.wait_ge(kv_full, half + 1)
                nc.scalar.activation(kT[:, half, :], s_bank[half][:, 0:SRC], ACT.Identity, bias=bk[:, half:half + 1]).then_inc(kv_out, 1)
            act.wait_ge(bias_done, 1)

            def prepare(it):
                act.wait_ge(tr, it + 1)
                at_least(act, q_full, 2 * it)
                nc.scalar.activation(xt[:], m_bank[:, 0:BTOK], ACT.Copy).then_inc(xt_out, 1)
                at_least(act, s_full, 16 * it)
                for half in range(2):
                    act.wait_ge(q_full, 2 * it + half + 1)
                    nc.scalar.activation(qT[:, half, :], m_bank[:, 0:BTOK], ACT.Identity, bias=bq[:, half:half + 1],
                                         scale=XE ** -0.5).then_inc(q_out, 1)

            def slot(it, j):
                t = 4 * it + j
                if live(it, j, 0):
                    par = j % 2
                    if live(it, j, 2):
                        act.wait_ge(t_full, 4 * (t - 1))
                        act.wait_ge(inv_done, t - 1)
                    for b in range(4):
                        act.wait_ge(s_low, 4 * t + b + 1)
                        for n in range(2):
                            h = 2 * b + n
                            ins = nc.scalar.activation(prob[:, par, h, :], s_bank[b][0:ROWS, n * SRC:(n + 1) * SRC], ACT.Exp,
                                                       bias=low[:, par, h:h + 1], accum_out=total[:, par, h:h + 1])
                        ins.then_inc(p_exp, 1)
                if live(it, j, 3):
                    par = (j - 3) % 2
                    act.wait_ge(ot_full, t - 2)
                    if live(it, j, 4):
                        act.wait_ge(wo_full, t - 3)
                    nc.scalar.activation(ot[:, par, :], m_bank[:, 0:ROWS], ACT.Copy).then_inc(ot_out, 1)
                if live(it, j, 1):
                    par = (j - 1) % 2
                    if live(it, j, 3):
                        act.wait_ge(pv_full, t - 2)
                    act.wait_ge(t_full, 4 * (t - 1) + 4)
                    nc.scalar.activation(pt[:, par, 6:8, :, :].rearrange("p h c r -> p (h c r)"),
                                         t_bank[1][0:SHALF, 0:4 * ROWS], ACT.Copy).then_inc(t_last, 1)
                if j == 3 and live(it, 0, -4):
                    prepare(it + 1)

            prepare(0)
            run(act, slot)


EXPERTS, CLUSTERS, GRID = 64, 8, 16
PER_CLUSTER = EXPERTS // CLUSTERS
SLOT = 64
BLOCKS = (TOKENS + EXPERTS * (SLOT - 1)) // SLOT
SLOTS = BLOCKS * SLOT
LOAD = 8


def route_stage(nc, a, k):
    with Stage(nc) as ctx:
        sb = lambda n, s, d=F32: ctx.enter_context(nc.sbuf_tensor(n, s, d))
        sem = lambda n: ctx.semaphore("r_" + n)
        norm_x, norm_f = Norm(nc, ctx, "outer"), Norm(nc, ctx, "inner")
        gamma, beta, scale_row = sb("gamma", [ROWS, DIM]), sb("beta", [ROWS, DIM]), sb("scale_row", [ROWS, EXPERTS])
        tie = sb("tie", [ROWS, CLUSTERS + EXPERTS])
        tri, all_one, ident16 = sb("tri", [ROWS, ROWS], BF16), sb("all_one", [ROWS, BLOCKS], BF16), sb("ident16", [ROWS, ROWS], BF16)
        tri32, ident32, block_col = sb("tri32", [ROWS, ROWS]), sb("ident32", [ROWS, ROWS]), sb("block_col", [BLOCKS, 1])
        x5 = sb("x5", [ROWS, TILES, DIM])
        sgn = sb("sgn", [ROWS, TILES, DIM], BF16)
        sgT = sb("sgT", [DIM, TILES, ROWS], BF16)
        sums, csum = sb("sums", [DIM, EXPERTS]), sb("csum", [DIM, CLUSTERS])
        sneg, cneg = sb("sneg", [DIM, EXPERTS]), sb("cneg", [DIM, CLUSTERS])
        sig = sb("sig", [DIM, CLUSTERS + EXPERTS], BF16)
        keys = sb("keys", [ROWS, TILES, CLUSTERS + EXPERTS])
        cmax, tmax = sb("cmax", [ROWS, TILES]), sb("tmax", [ROWS, TILES])
        pen = sb("pen", [ROWS, TILES, CLUSTERS])
        tkey = sb("tkey", [ROWS, TILES, EXPERTS])
        oh = sb("oh", [ROWS, TILES, 2, EXPERTS], BF16)
        cum = sb("cum", [ROWS, TILES + 1, EXPERTS], BF16)
        count_i, nb_i = sb("count_i", [BLOCKS, EXPERTS], I32), sb("nb_i", [BLOCKS, EXPERTS], I32)
        nb, upto, start = sb("nb", [BLOCKS, EXPERTS]), sb("upto", [BLOCKS, EXPERTS]), sb("start", [BLOCKS, EXPERTS])
        one_row = sb("one_row", [BLOCKS, EXPERTS])
        owner, owner_i = sb("owner", [BLOCKS, 1]), sb("owner_i", [BLOCKS, 1], I32)
        posf = sb("posf", [ROWS, TILES])
        names = ("w_in", "link", "x_done", "f_done", "sgn_done", "sT", "sT_out", "sig_done", "sc_full", "key_done", "oh_done",
                 "cum_done", "pre_full", "oT", "oT_out", "owner_done", "owner_out", "owner_in", "pos_done", "scattered", "consts")
        (w_in, chain, x_done, f_done, sgn_done, sT, sT_out, sig_done, sc_full, key_done, oh_done, cum_done, pre_full, oT,
         oT_out, owner_done, owner_out, owner_in, pos_done, scattered, consts) = (sem(n) for n in names)
        block = ctx.enter_context(nc.Block())
        tb = [k.banks[6][:].bitcast(BF16), k.banks[7][:].bitcast(BF16)]
        LOADS = 7

        @block.sync
        def _(sp):
            for dst, name, p in ((gamma, "gamma", ROWS), (beta, "beta", ROWS), (scale_row, "scale", ROWS), (tie, "tie", ROWS)):
                sp.dma_start(dst[:], a[name].partition_broadcast(p)).then_inc(w_in, 16)
            for dst, name in ((tri32, "tri"), (ident32, "ident98"), (block_col, "block_col")):
                sp.dma_start(dst[:], a[name]).then_inc(w_in, 16)
            sp.wait_ge(owner_done, 1)
            sp.dma_start(k.owner_dram, owner_i[:]).then_inc(owner_out, 16)
            sp.wait_ge(owner_out, 16)
            sp.dma_start(k.owner_row[:], k.owner_dram.rearrange("b o -> o b")).then_inc(owner_in, 16)
            sp.wait_ge(owner_in, 16)

        @block.vector
        def _(dve):
            n = [0]

            def link(ins):
                n[0] += 1
                ins.then_inc(chain, 1)
                dve.wait_ge(chain, n[0])

            def sign(out, x, below, done=None):
                link(nc.vector.tensor_scalar(below, x, 0.0, None, ALU.is_lt))
                return nc.vector.scalar_tensor_tensor(out, x, 0.0, below, ALU.is_gt, ALU.subtract)

            link(nc.vector.tensor_reduce(sums[:], k.wd[:].rearrange("p (e h) -> p e h", e=EXPERTS), AX_X, ALU.add))
            link(sign(sig[:, CLUSTERS:], sums[:], sneg[:]))
            link(nc.vector.tensor_reduce(csum[:], sig[:, CLUSTERS:].rearrange("p (c t) -> p c t", c=CLUSTERS), AX_X, ALU.add))
            sign(sig[:, 0:CLUSTERS], csum[:], cneg[:]).then_inc(sig_done, 1)
            link(nc.vector.memset(all_one[:], 1.0))
            link(nc.vector.memset(one_row[:], 1.0))
            link(nc.vector.memset(cum[:, 0, :], 0.0))
            norm_x.vector_part(dve, k.h)
            dve.wait_ge(w_in, 16 * LOADS)
            link(nc.vector.tensor_copy(tri[:], tri32[:]))
            nc.vector.tensor_copy(ident16[:], ident32[:]).then_inc(consts, 1)

            def outer(it):
                for t in range(4):
                    tile = 4 * it + t
                    nc.vector.tensor_scalar(x5[:, tile, :], k.h[:, tile, :], norm_x.mean[:, bass.ds(tile, 1)],
                                            norm_x.rstd[:, bass.ds(tile, 1)], ALU.subtract, ALU.mult).then_inc(x_done, 1)

            def inner(it):
                for t in range(4):
                    tile = 4 * it + t
                    nc.vector.tensor_scalar(k.xf[:, tile, :], x5[:, tile, :], norm_f.mean[:, bass.ds(tile, 1)],
                                            norm_f.rstd[:, bass.ds(tile, 1)], ALU.subtract, ALU.mult).then_inc(f_done, 1)

            with dve.Fori(0, TILES // 4) as it:
                outer(it)
            dve.wait_ge(x_done, TILES)
            norm_f.vector_part(dve, x5)
            with dve.Fori(0, TILES // 4) as it:
                inner(it)
            dve.wait_ge(f_done, TILES)
            wide = [ROWS, TILES, DIM]
            link(nc.vector.tensor_tensor(k.xf[:], k.xf[:], bc(gamma[:].unsqueeze(1), wide), ALU.mult))
            link(nc.vector.tensor_tensor(k.xf[:], k.xf[:], bc(beta[:].unsqueeze(1), wide), ALU.add))
            sign(sgn[:], k.xf[:], tkey[:].rearrange("p t e -> p (t e)").bitcast(BF16)).then_inc(sgn_done, 1)
            dve.wait_ge(sgn_done, 1)
            link(nc.vector.tensor_tensor(k.h[:], k.h[:], x5[:], ALU.add))
            for g in range(TILES // 4):
                dve.wait_ge(sc_full, g + 1)
                nc.vector.scalar_tensor_tensor(keys[:, 4 * g:4 * g + 4, :],
                                               k.banks[g % 4][0:ROWS, 0:4 * 72].rearrange("p (t e) -> p t e", t=4), 16.0,
                                               bc(tie[:].unsqueeze(1), [ROWS, 4, 72]), ALU.mult, ALU.add).then_inc(key_done, 1)
            dve.wait_ge(key_done, TILES // 4)
            ck = keys[:, :, 0:CLUSTERS]
            link(nc.vector.tensor_reduce(cmax[:], ck, AX_X, ALU.max))
            link(nc.vector.tensor_tensor(pen[:], ck, bc(cmax[:].unsqueeze(2), [ROWS, TILES, CLUSTERS]), ALU.is_equal))
            link(nc.vector.tensor_scalar(pen[:], pen[:], -1.0, 1e5, ALU.add, ALU.mult))
            link(nc.vector.tensor_tensor(tkey[:].rearrange("p t (c j) -> p t c j", c=CLUSTERS),
                                         keys[:, :, CLUSTERS:].rearrange("p t (c j) -> p t c j", c=CLUSTERS),
                                         bc(pen[:].unsqueeze(3), [ROWS, TILES, CLUSTERS, PER_CLUSTER]), ALU.add))
            link(nc.vector.tensor_reduce(tmax[:], tkey[:], AX_X, ALU.max))
            for half in range(2):
                ins = nc.vector.tensor_tensor(oh[:, :, half, :], tkey[:], bc(tmax[:].unsqueeze(2), [ROWS, TILES, EXPERTS]), ALU.is_equal)
                ins.then_inc(oh_done, 1)
            dve.wait_ge(oh_done, 2)
            for t in range(TILES):
                link(nc.vector.tensor_tensor(cum[:, t + 1, :], cum[:, t, :], oh[:, t, 0, :], ALU.add))
            nc.vector.tensor_copy(one_row[:], one_row[:]).then_inc(cum_done, 1)
            dve.wait_ge(pre_full, 1)
            link(nc.vector.tensor_scalar(count_i[:], k.banks[4][0:BLOCKS, 0:EXPERTS], float(SLOT - 1), None, ALU.add))
            link(nc.vector.tensor_scalar(nb_i[:], count_i[:], SLOT.bit_length() - 1, None, ALU.arith_shift_right))
            link(nc.vector.tensor_copy(nb[:], nb_i[:]))
            link(nc.vector.tensor_tensor_scan(upto[:], one_row[:], nb[:], 0.0, ALU.mult, ALU.add))
            link(nc.vector.tensor_tensor(start[:], upto[:], nb[:], ALU.subtract))
            link(nc.vector.tensor_scalar(start[:], start[:], float(SLOT), None, ALU.mult))
            link(nc.vector.tensor_scalar(nb[:], upto[:], block_col[:, 0:1], None, ALU.is_le))
            link(nc.vector.tensor_reduce(owner[:], nb[:], AX_X, ALU.add))
            nc.vector.tensor_scalar(owner_i[:], owner[:], float(EXPERTS - 1), None, ALU.min).then_inc(owner_done, 1)
            for g in range(4):
                link(nc.vector.tensor_tensor(tkey[:, 8 * g:8 * g + 8, :], k.banks[g][0:ROWS, :].rearrange("p (t e) -> p t e", t=8),
                                             bc(start[0:ROWS, :].unsqueeze(1), [ROWS, 8, EXPERTS]), ALU.add))
            link(nc.vector.tensor_tensor(tkey[:], tkey[:], oh[:, :, 0, :], ALU.mult))
            link(nc.vector.tensor_reduce(posf[:], tkey[:], AX_X, ALU.add))
            nc.vector.tensor_copy(k.pos[:], posf[:]).then_inc(pos_done, 1)
            link(nc.vector.tensor_tensor(x5[:, :, 0:EXPERTS], oh[:, :, 0, :], bc(scale_row[:].unsqueeze(1), [ROWS, TILES, EXPERTS]), ALU.mult))
            link(nc.vector.tensor_reduce(k.scale[:], x5[:, :, 0:EXPERTS], AX_X, ALU.add))

        @block.scalar
        def _(act):
            norm_x.scalar_part(act)
            norm_f.scalar_part(act)
            for g in range(TILES // 4):
                act.wait_ge(sT, g + 1)
                nc.scalar.activation(sgT[:, 4 * g:4 * g + 4, :], tb[g % 2][:, 0:4 * ROWS].rearrange("p (t r) -> p t r", t=4),
                                     ACT.Copy).then_inc(sT_out, 1)
            for g in range(TILES // 4):
                act.wait_ge(oT, g + 1)
                nc.scalar.activation(k.ohT[:, 4 * g:4 * g + 4, :], tb[g % 2][:, 0:4 * ROWS].rearrange("p (t r) -> p t r", t=4),
                                     ACT.Copy).then_inc(oT_out, 1)

        def score(pe, g):
            pe.wait_ge(sT_out, g + 1)
            if g >= 4:
                pe.wait_ge(key_done, g - 3)
            for t in range(4):
                mm = nc.tensor.matmul(k.banks[g % 4][0:ROWS, 72 * t:72 * t + 72], sgT[:, 4 * g + t, :], sig[:], start=True, stop=True)
            mm.then_inc(sc_full, 1)

        @block.tensor
        def _(pe):
            pe.wait_ge(sgn_done, 1)
            pe.wait_ge(consts, 1)
            pe.wait_ge(sig_done, 1)
            for g in range(TILES // 4):
                if g >= 2:
                    pe.wait_ge(sT_out, g - 1)
                for t in range(4):
                    mm = nc.tensor.transpose(tb[g % 2][:, t * ROWS:(t + 1) * ROWS], sgn[:, 4 * g + t, :], ident16[:])
                mm.then_inc(sT, 1)
                if g >= 1:
                    score(pe, g - 1)
            score(pe, TILES // 4 - 1)
            pe.wait_ge(cum_done, 1)
            for g in range(4):
                nc.tensor.matmul(k.banks[g][0:ROWS, :], tri[:], oh[:, 8 * g:8 * g + 8, 0, :], start=True, stop=False)
                nc.tensor.matmul(k.banks[g][0:ROWS, :], all_one[:, 0:ROWS], cum[:, 8 * g:8 * g + 8, :], start=False, stop=True)
            nc.tensor.matmul(k.banks[4][0:BLOCKS, 0:EXPERTS], all_one[:], cum[:, TILES, :], start=True, stop=True).then_inc(pre_full, 1)
            pe.wait_ge(sT_out, TILES // 4)
            for g in range(TILES // 4):
                if g >= 2:
                    pe.wait_ge(oT_out, g - 1)
                for t in range(4):
                    mm = nc.tensor.transpose(tb[g % 2][:, t * ROWS:(t + 1) * ROWS], oh[:, 4 * g + t, :, :].rearrange("p a e -> p (a e)"),
                                             ident16[:])
                mm.then_inc(oT, 1)

        @block.gpsimd
        def _(pool):
            pool.wait_ge(pos_done, 1)
            for t in range(TILES):
                nc.gpsimd.indirect_dma_start(out=k.x_slots, out_offset=bass.IndirectOffsetOnAxis(ap=k.pos[:, t:t + 1], axis=0),
                                             in_=k.xf[:, t, :], in_offset=None).then_inc(scattered, 16)
            pool.wait_ge(scattered, 16 * TILES)


def expert_stage(nc, k, name, weights, src, dst):
    with Stage(nc) as ctx:
        sb = lambda n, s, d=F32: ctx.enter_context(nc.sbuf_tensor(f"{name}_{n}", s, d))
        sem = lambda n: ctx.semaphore(f"{name}_{n}")
        rows, out = sb("rows", [SLOT, 2, LOAD, DIM]), sb("out", [SLOT, 2, LOAD, DIM])
        xt = sb("xt", [DIM, 2, 4 * SLOT])
        rows_in, stored = [sem("rows_in0"), sem("rows_in1")], [sem("stored0"), sem("stored1")]
        t_full, t_out, y_full, y_out = sem("t_full"), sem("t_out"), sem("y_full"), sem("y_out")
        t_bank, y_bank = k.banks[0:2], k.banks[2:4]
        tally = sem("tally")
        STEPS = BLOCKS // LOAD // 2
        src_v = src.rearrange("(b s) d -> s b d", s=SLOT)
        dst_v = dst.rearrange("(b s) d -> s b d", s=SLOT)
        block = ctx.enter_context(nc.Block())

        @block.sync
        def _(sp):
            def body(it):
                for u in range(2):
                    at_least(sp, t_full, 4 * it + 2 * u - 2)
                    sp.dma_start(rows[:, u, :, :], src_v[:, bass.ds((2 * it + u) * LOAD, LOAD), :]).then_inc(rows_in[u], 16)
            peeled(sp, STEPS, body)

        @block.tensor
        def _(pe):
            def turn(it, v):
                u = v // 2
                if v % 2 == 0:
                    pe.wait_ge(rows_in[u], 16 * (it + 1))
                at_least(pe, t_out, 4 * it + v - 1)
                carry_waits(pe, tally)
                for b in range(4):
                    mm = nc.tensor.transpose(t_bank[v % 2][:, b * SLOT:(b + 1) * SLOT], rows[:, u, 4 * (v % 2) + b, :],
                                             k.ident[0:SLOT, 0:SLOT])
                mm.then_inc(t_full, 1)

            def product(it, v):
                pe.wait_ge(t_out, 4 * it + v + 1)
                at_least(pe, y_out, 4 * it + v - 1)
                for b in range(4):
                    e = nc.tensor.value_load(k.owner_row[0:1, bass.ds(16 * it + 4 * v + b, 1)], min_val=0, max_val=EXPERTS - 1)
                    mm = nc.tensor.matmul(y_bank[v % 2][0:SLOT, b * DIM:(b + 1) * DIM], xt[:, v % 2, b * SLOT:(b + 1) * SLOT],
                                          weights[:, bass.ds(e * DIM, DIM)], start=True, stop=True)
                mm.then_inc(y_full, 1)

            def body(it):
                turn(it, 0)
                for v in range(4):
                    if v < 3:
                        turn(it, v + 1)
                    product(it, v)

            peeled(pe, STEPS, body)

        @block.vector
        def _(dve):
            def body(it):
                for v in range(4):
                    dve.wait_ge(t_full, 4 * it + v + 1)
                    at_least(dve, y_full, 4 * it + v - 1)
                    nc.vector.tensor_copy(xt[:, v % 2, :], t_bank[v % 2][:, 0:4 * SLOT]).then_inc(t_out, 1)
            peeled(dve, STEPS, body)

        @block.scalar
        def _(act):
            def body(it):
                for v in range(4):
                    act.wait_ge(y_full, 4 * it + v + 1)
                    if v % 2 == 0:
                        at_least(act, stored[v // 2], 16 * it)
                    nc.scalar.activation(out[:, v // 2, 4 * (v % 2):4 * (v % 2) + 4, :].rearrange("p b d -> p (b d)"),
                                         y_bank[v % 2][0:SLOT, :], ACT.Copy).then_inc(y_out, 1)
                    if v % 2 == 1:
                        act.wait_ge(y_out, 4 * it + v + 1)
                        act.dma_start(dst_v[:, bass.ds((2 * it + v // 2) * LOAD, LOAD), :], out[:, v // 2, :, :]).then_inc(stored[v // 2], 16)
            peeled(act, STEPS, body)
            for u in range(2):
                act.wait_ge(stored[u], 16 * STEPS)


def spline_stage(nc, a, k):
    with Stage(nc) as ctx:
        sb = lambda n, s, d=F32: ctx.enter_context(nc.sbuf_tensor(n, s, d))
        sem = lambda n: ctx.semaphore("s_" + n)
        edge = sb("edge", [ROWS, GRID])
        below = sb("below", [ROWS, 2, GRID, 2, DIM], BF16)
        line = sb("line", [ROWS, 2, 2, 2, DIM])
        hn = sb("hn", [ROWS, TILES, DIM])
        slope_u = sb("slope_u", [ROWS, 2, 2, DIM])
        gathered = [sem(f"gathered{i}") for i in range(4)]
        edge_in, sig_done, mask_done, tab_full, pick, mul_done, hs_done, scattered = (
            sem(n) for n in ("edge_in", "sig_done", "mask_done", "tab_full", "pick", "mul_done", "hs_done", "scattered"))
        PAIRS = TILES // 2
        tally = sem("tally")
        block = ctx.enter_context(nc.Block())

        @block.sync
        def _(sp):
            sp.dma_start(edge[:], a["edge"].partition_broadcast(ROWS)).then_inc(edge_in, 16)

        @block.gpsimd
        def _(pool):
            for t in range(TILES):
                nc.gpsimd.indirect_dma_start(out=k.xf[:, t, :], out_offset=None, in_=k.y_slots,
                                             in_offset=bass.IndirectOffsetOnAxis(ap=k.pos[:, t:t + 1], axis=0)).then_inc(gathered[t // 8], 16)
            for t in range(TILES):
                pool.wait_ge(hs_done, t + 1)
                nc.gpsimd.indirect_dma_start(out=k.x_slots, out_offset=bass.IndirectOffsetOnAxis(ap=k.pos[:, t:t + 1], axis=0),
                                             in_=k.xf[:, t, :], in_offset=None).then_inc(scattered, 16)
            pool.wait_ge(scattered, 16 * TILES)

        @block.scalar
        def _(act):
            for q in range(4):
                act.wait_ge(gathered[q], 16 * 8)
                nc.scalar.activation(hn[:, 8 * q:8 * q + 8, :], k.xf[:, 8 * q:8 * q + 8, :], ACT.Sigmoid).then_inc(sig_done, 1)
            act.wait_ge(sig_done, 4)
            act.wait_ge(edge_in, 16)

            def body(it):
                for v in range(2):
                    at_least(act, pick, 32 * (2 * it + v - 1))
                    for i in range(1, GRID):
                        ins = nc.scalar.activation(below[:, v, i, :, :], hn[:, bass.ds(4 * it + 2 * v, 2), :], ACT.Relu,
                                                   bias=edge[:, i:i + 1], scale=-float(GRID))
                    ins.then_inc(mask_done, 1)
            peeled(act, PAIRS // 2, body)

        @block.tensor
        def _(pe):
            def body(it):
                for v in range(2):
                    for p in range(8):
                        for t in range(2):
                            n = (2 * p + t) % 8
                            at_least(pe, pick, 32 * (2 * it + v) + 4 * (p - 4) + 3 + t)
                            lhs = k.ohT[:, bass.ds(4 * it + 2 * v + t, 1), :].rearrange("p a r -> p (a r)")
                            nc.tensor.matmul(k.banks[n][0:ROWS, :], lhs, k.lines_hi[:, 512 * p:512 * (p + 1)], start=True, stop=False)
                            nc.tensor.matmul(k.banks[n][0:ROWS, :], lhs, k.lines_lo[:, 512 * p:512 * (p + 1)], start=False, stop=True).then_inc(tab_full, 1)
            peeled(pe, PAIRS // 2, body)

        @block.vector
        def _(dve):
            def body(it):
                for v in range(2):
                    base = 32 * (2 * it + v)
                    dve.wait_ge(mask_done, 2 * it + v + 1)
                    for p in range(8):
                        for n in range(2):
                            i = 2 * p + n
                            for t in range(2):
                                src = k.banks[(2 * p + t) % 8][0:ROWS, 256 * n:256 * n + 256].rearrange("p (c d) -> p c d", c=2)
                                if n == 0:
                                    dve.wait_ge(tab_full, 16 * (2 * it + v) + 2 * p + t + 1)
                                if i == 0:
                                    at_least(dve, hs_done, 2 * (2 * it + v) - 2)
                                    ins = nc.vector.tensor_copy(line[:, v, t, :, :], src)
                                else:
                                    dve.wait_ge(pick, base + 2 * i + t - 1)
                                    carry_waits(dve, tally)
                                    ins = nc.vector.copy_predicated(line[:, v, t, :, :],
                                                                    bc(below[:, v, i, t, :].bitcast(U16).unsqueeze(1), [ROWS, 2, DIM]), src)
                                ins.then_inc(pick, 1)
                    dve.wait_ge(pick, base + 32)
                    tile = 4 * it + 2 * v
                    nc.vector.scalar_tensor_tensor(slope_u[:, v, :, :], hn[:, bass.ds(tile, 2), :], float(GRID), line[:, v, :, 1, :],
                                                   ALU.mult, ALU.mult).then_inc(mul_done, 1)
                    dve.wait_ge(mul_done, 2 * it + v + 1)
                    for t in range(2):
                        nc.vector.tensor_tensor(k.xf[:, bass.ds(tile + t, 1), :], slope_u[:, v, t, :].unsqueeze(1), line[:, v, t, 0, :].unsqueeze(1),
                                                ALU.add).then_inc(hs_done, 1)
            peeled(dve, PAIRS // 2, body)


def final_stage(nc, k, out):
    with Stage(nc) as ctx:
        sem = lambda n: ctx.semaphore("f_" + n)
        gathered = [sem(f"gathered{i}") for i in range(8)]
        done, stored = sem("done"), sem("stored")
        out_v = out.rearrange("b q d -> (b q) d").rearrange("(t r) d -> r t d", r=ROWS)
        block = ctx.enter_context(nc.Block())

        @block.gpsimd
        def _(pool):
            for t in range(TILES):
                nc.gpsimd.indirect_dma_start(out=k.xf[:, t, :], out_offset=None, in_=k.y_slots,
                                             in_offset=bass.IndirectOffsetOnAxis(ap=k.pos[:, t:t + 1], axis=0)).then_inc(gathered[t // 4], 16)

        @block.vector
        def _(dve):
            for g in range(8):
                dve.wait_ge(gathered[g], 16 * 4)
                for t in range(4 * g, 4 * g + 4):
                    ins = nc.vector.scalar_tensor_tensor(k.h[:, t, :], k.xf[:, t, :], k.scale[:, t:t + 1], k.h[:, t, :], ALU.mult, ALU.add)
                    ins.then_inc(done, 1)

        @block.sync
        def _(sp):
            for g in range(8):
                sp.wait_ge(done, 4 * g + 4)
                sp.dma_start(out_v[:, 4 * g:4 * g + 4, :], k.h[:, 4 * g:4 * g + 4, :]).then_inc(stored, 16)
            sp.wait_ge(stored, 16 * 8)


class Store:
    pass


def tower_program(nc, a, out, stop=None, dbg=None):
    with ExitStack() as ctx:
        sb = lambda n, s, d=F32: ctx.enter_context(nc.sbuf_tensor(n, s, d))
        k = Store()
        k.banks = [ctx.enter_context(nc.psum_tensor(f"bank{i}", [128, 512], F32)) for i in range(8)]
        k.ident = sb("ident", [128, 128])
        k.h = sb("h", [ROWS, TILES, DIM])
        k.bias_dram = nc.dram_tensor("bias_dram", (HEADS, QUERIES * KEYS), F32, kind="Internal").ap()
        k.three = sb("three", [128, 1])
        with ExitStack() as first:
            sb1 = lambda n, s, d=F32: first.enter_context(nc.sbuf_tensor(n, s, d))
            k.mh = sb1("mh", [AUG, HEADS, AUG])
            k.wv = sb1("wv", [AUG, HEADS, VD])
            k.pw = sb1("pw", [128, 6, DIM])
            k.prow = sb1("prow", [128, DIM])
            k.bias = sb1("bias", [CH, CHUNKS, KEYS])
            k.xT = sb1("xT", [AUG, 2, GROUP * KEYS])
            k.xn = sb1("xn", [KHALF, 2, GROUP, 2, AUG])
            setup_stage(nc, a, k, ctx)
            token_stage(nc, a, k)
        if stop == "token":
            return dump(nc, k.h, dbg)
        band_stage(nc, a, k)
        if stop == "band":
            return dump(nc, k.h, dbg)
        k.wd = sb("wd", [DIM, EXPERTS * DIM])
        k.wu = sb("wu", [DIM, EXPERTS * DIM])
        k.lines_hi, k.lines_lo = sb("lines_hi", [128, 4096], BF16), sb("lines_lo", [128, 4096], BF16)
        k.x_slots = nc.dram_tensor("x_slots", (SLOTS, DIM), F32, kind="Internal").ap()
        k.y_slots = nc.dram_tensor("y_slots", (SLOTS, DIM), F32, kind="Internal").ap()
        k.owner_dram = nc.dram_tensor("owner_dram", (BLOCKS, 1), I32, kind="Internal").ap()
        cross_stage(nc, a, k)
        if stop == "cross":
            return dump(nc, k.h, dbg)
        k.owner_row = sb("owner_row", [1, BLOCKS], I32)
        k.pos = sb("pos", [ROWS, TILES], I32)
        k.scale = sb("scale", [ROWS, TILES])
        k.ohT = sb("ohT", [128, TILES, ROWS], BF16)
        k.xf = sb("xf", [ROWS, TILES, DIM])
        route_stage(nc, a, k)
        if stop == "route":
            return dump(nc, k.xf, dbg)
        expert_stage(nc, k, "down", k.wd[:], k.x_slots, k.y_slots)
        spline_stage(nc, a, k)
        if stop == "spline":
            return dump(nc, k.xf, dbg)
        expert_stage(nc, k, "up", k.wu[:], k.x_slots, k.y_slots)
        final_stage(nc, k, out)


def dump(nc, buf, dbg):
    with nc.semaphore("dumped") as dumped, nc.Block() as block:
        @block.sync
        def _(sp):
            sp.dma_start(dbg, buf[:]).then_inc(dumped, 16)
            sp.wait_ge(dumped, 16)


def layouts(i):
    import numpy as np
    f = {n: np.asarray(v) for n, v in i.items()}
    x = f["x"]
    kvw = f["L0_tok_kv_w"].reshape(HEADS, KD + VD, DIM_IN)
    kv_bn = np.stack([f[f"L0_tok_kv_{c}"] for c in "gbmv"]).reshape(4, HEADS, KD + VD)
    o = {
        "xT": x.transpose(2, 0, 1).reshape(DIM_IN, BATCH * KEYS),
        "xn": x.reshape(BATCH, 2, KHALF, DIM_IN).transpose(2, 0, 1, 3).reshape(KHALF, BATCH * 2, DIM_IN),
        "q_w": f["L0_tok_q_w"].reshape(HEADS, KD, DIM_IN).transpose(1, 0, 2),
        "k_w": kvw[:, :KD].transpose(1, 0, 2),
        "v_w": kvw[:, KD:].transpose(1, 0, 2),
        "q_bn": np.stack([f[f"L0_tok_q_{c}"] for c in "gbmv"]).reshape(4, HEADS, KD).transpose(2, 0, 1),
        "k_bn": kv_bn[:, :, :KD].transpose(2, 0, 1),
        "v_bn": kv_bn[:, :, KD:].transpose(2, 0, 1),
        "proj_w": f["L0_tok_proj_w"].T.reshape(6, 128, DIM).transpose(1, 0, 2),
        "proj_bn": np.stack([f[f"L0_tok_proj_{c}"] for c in "gbmv"]),
        "bias_t": f["L0_tok_attention_biases"].T.reshape(2, KHALF, HEADS).transpose(1, 0, 2),
        "bias_idx": f["L0_tok_bias_idxs"].reshape(-1),
        "off_col": (np.arange(KHALF)[:, None] + KHALF * np.arange(2)[None, :]).astype(np.float32),
        "ident": np.eye(128, dtype=np.float32),
    }
    half = np.arange(DIM // 2, dtype=np.float32)
    theta = np.float32(10000.0) ** (np.float32(-2.0) * (half - np.float32(1.0)) / np.float32(DIM))
    angle = np.arange(QUERIES, dtype=np.float32)[:, None] * theta[None, :]
    cos, sin = np.repeat(np.cos(angle).T, 2, axis=0), np.repeat(np.sin(angle).T, 2, axis=0)
    sin[1::2] *= -1.0
    swap = np.arange(DIM) ^ 1
    q, kk = np.arange(ROWS)[:, None], np.arange(ROWS)[None, :]
    wq, wk = f["L0_attn_W_q"], f["L0_attn_W_k"]
    o |= {
        "band_w": np.stack([wq, wq[:, swap], wk, wk[:, swap]], axis=1),
        "u_v": f["L0_attn_u_v"],
        "v_v": f["L0_attn_v_v"].reshape(DIM),
        "trig": np.stack([cos, sin], axis=1).astype(np.float32),
        "band_mask": np.where((kk <= q) & (kk // QUERIES == q // QUERIES), 0.0, -1e30).astype(np.float32),
    }

    def padded(w):
        out = np.zeros((w.shape[0], 2, 4, 32), w.dtype)
        out[..., :XE] = w.reshape(w.shape[0], 2, 4, XE)
        return out.reshape(w.shape[0], 2, 128)

    g = lambda n: f["L1_attn_" + n]
    o |= {
        "srcT": g("source_embedding").T.reshape(LCH, 128, SRC).transpose(1, 0, 2),
        "valT": g("value_embedding").T.reshape(LCH, 128, SRC).transpose(1, 0, 2),
        "x_wk": padded(g("Wk")).reshape(LCH, 128, 2, 128).transpose(1, 0, 2, 3),
        "x_wv": g("Wv").reshape(LCH, 128, DIM).transpose(1, 0, 2),
        "x_wq": padded(g("Wq")),
        "x_wo": g("Wo"),
        "x_bq": padded(g("bq")[None])[0].T,
        "x_bk": padded(g("bk")[None])[0].T,
        "x_bv": g("bv"),
        "x_bo": g("bo")[None],
    }
    g = lambda n: f["L1_ffn_" + n]
    cells = np.arange(GRID - 1, -1, -1)
    lines = np.stack([g("spline_bases"), g("spline_slopes")], axis=3)[:, :, cells]
    lines = lines.transpose(0, 2, 3, 1).reshape(EXPERTS, 4096)
    o |= {
        "gamma": g("gamma"), "beta": g("beta"), "scale": g("scale"),
        "wd": g("Wd").transpose(2, 0, 1).reshape(DIM, EXPERTS * DIM),
        "wu": g("Wu").transpose(2, 0, 1).reshape(DIM, EXPERTS * DIM),
        "spline": np.concatenate([lines, lines]),
        "cell": cells.astype(np.float32),
        "edge": (GRID - np.arange(GRID)).astype(np.float32),
        "tie": -np.concatenate([np.arange(CLUSTERS), np.arange(EXPERTS) % PER_CLUSTER]).astype(np.float32),
        "tri": np.triu(np.ones((ROWS, ROWS), np.float32), 1),
        "ident98": np.eye(ROWS, dtype=np.float32),
        "block_col": np.arange(BLOCKS, dtype=np.float32)[:, None],
    }
    return {n: np.ascontiguousarray(v) for n, v in o.items()}


def kernel(**inputs):
    import numpy as np
    import concourse.bacc as bacc
    from concourse.bass_utils import run_bass_kernel_spmd

    arrays = {f"in_{n}": v for n, v in layouts(inputs).items()}
    nc = bacc.Bacc("TRN2", target_bir_lowering=False, num_devices=1)
    a = {n[3:]: nc.dram_tensor(n, v.shape, mybir.dt.from_np(v.dtype), kind="ExternalInput").ap() for n, v in arrays.items()}
    out = nc.dram_tensor("out", (BATCH, QUERIES, DIM), F32, kind="ExternalOutput").ap()
    tower_program(nc, a, out)
    r = run_bass_kernel_spmd(nc, [arrays], core_ids=[0])
    return np.asarray(r.results[0]["out"])
```

```python
from contextlib import ExitStack

import concourse.bass as bass
from concourse import mybir

ALU = mybir.AluOpType
ACT = mybir.ActivationFunctionType
AX_X = mybir.AxisListType.X
F32 = mybir.dt.float32
BF16 = mybir.dt.bfloat16
I32 = mybir.dt.int32
U16 = mybir.dt.uint16
U32 = mybir.dt.uint32

EPS = 1e-5
BATCH, RES, RESQ, DIM_IN, DIM = 64, 14, 7, 96, 128
KEYS, QUERIES = RES * RES, RESQ * RESQ
HEADS, KD, VD = 12, 32, 64
AUG = DIM_IN + 1
TOKENS = BATCH * QUERIES
ROWS = 2 * QUERIES
TILES = TOKENS // ROWS
KHALF = KEYS // 2
GROUP = 4
GROUPS = BATCH // GROUP
GTOK = GROUP * QUERIES
HQ = HEADS * QUERIES
CH = 118
CHUNKS = 5
CHUNK_AT = [0, CH, 2 * CH, 3 * CH, HQ - CH]
PIECES = [(0, 1), (2, 3), (4,)]


def at_least(eng, sem, count):
    if isinstance(count, int) and count <= 0:
        return
    eng.wait_ge(sem, count)


def carry_waits(eng, tally):
    eng.sem_inc(tally, 1)


class Stage(ExitStack):

    def __init__(self, nc):
        super().__init__()
        self.nc, self.sems = nc, []

    def semaphore(self, name):
        self.sems.append(self.nc.alloc_semaphore(name))
        return self.sems[-1]

    def __exit__(self, *error):
        handled = super().__exit__(*error)
        if error[0] is None:
            self.nc.clear_and_free_semaphores(self.sems)
            self.nc.all_engine_barrier(sem_only=True)
        return handled


def bc(ap, shape):
    return ap.to_broadcast(shape)


def setup_stage(nc, a, k, outer):
    with Stage(nc) as ctx:
        sb = lambda n, s, d=F32: ctx.enter_context(nc.sbuf_tensor(n, s, d))
        sem = lambda n: ctx.semaphore(n)
        qw, kw = sb("qw", [KD, HEADS, DIM_IN]), sb("kw", [KD, HEADS, DIM_IN])
        vw = sb("vw", [VD, HEADS, DIM_IN])
        qp, kp, vp = sb("qp", [KD, 4, HEADS]), sb("kp", [KD, 4, HEADS]), sb("vp", [VD, 4, HEADS])
        pp = sb("pp", [128, 4, DIM])
        qaug, kaug, vaug = sb("qaug", [KD, HEADS, AUG]), sb("kaug", [KD, HEADS, AUG]), sb("vaug", [VD, HEADS, AUG])
        rt_q, rt_k, rt_v, rt_p = sb("rt_q", [KD, HEADS]), sb("rt_k", [KD, HEADS]), sb("rt_v", [VD, HEADS]), sb("rt_p", [128, DIM])
        sc_q, sc_k, sc_v, sc_p = sb("sc_q", [KD, HEADS]), sb("sc_k", [KD, HEADS]), sb("sc_v", [VD, HEADS]), sb("sc_p", [128, DIM])
        tm_q, tm_k, tm_v, tm_p = sb("tm_q", [KD, HEADS]), sb("tm_k", [KD, HEADS]), sb("tm_v", [VD, HEADS]), sb("tm_p", [128, DIM])
        PIECE = KEYS * QUERIES // 7
        STRIP = PIECE // 4
        idx = sb("idx", [KHALF, 2, PIECE], I32)
        onehot = sb("onehot", [KHALF, 2, 2, PIECE])
        ab = sb("ab", [KHALF, 2, HEADS])
        off_col = sb("off_col", [KHALF, 2])
        brow = sb("brow", [HEADS, 2, PIECE])

        loaded, idx_in = sem("loaded"), [sem("idx_in0"), sem("idx_in1")]
        chain, root, ready, m_full, m_out = sem("chain"), sem("root"), sem("ready"), sem("m_full"), sem("m_out")
        hot, b_full, b_out, v_full, table_in = sem("hot"), sem("b_full"), sem("b_out"), sem("v_full"), sem("table_in")
        b_stored = [sem("b_stored0"), sem("b_stored1")]
        bank = k.banks
        idx_src = a["bias_idx"]
        sets = [(qw, qp, qaug, rt_q, sc_q, tm_q), (kw, kp, kaug, rt_k, sc_k, tm_k), (vw, vp, vaug, rt_v, sc_v, tm_v)]
        LOADS = 11
        block = ctx.enter_context(nc.Block())

        @block.sync
        def _(sp):
            for dst, src in ((qw, "q_w"), (kw, "k_w"), (vw, "v_w"), (qp, "q_bn"), (kp, "k_bn"), (vp, "v_bn"),
                             (k.pw, "proj_w"), (k.ident, "ident"), (ab, "bias_t"), (off_col, "off_col")):
                sp.dma_start(dst[:], a[src]).then_inc(loaded, 16)
            sp.dma_start(pp[:], a["proj_bn"].partition_broadcast(128)).then_inc(loaded, 16)
            for p in range(7):
                if p >= 2:
                    sp.wait_ge(hot, 2 * (p - 1))
                sp.dma_start(idx[:, p % 2, :], idx_src[p * PIECE:(p + 1) * PIECE].partition_broadcast(KHALF)).then_inc(idx_in[p % 2], 16)
                if p >= 1:
                    sp.wait_ge(b_out, 4 * p)
                    sp.dma_start(k.bias_dram[:, (p - 1) * PIECE:p * PIECE], brow[:, (p - 1) % 2, :]).then_inc(b_stored[(p - 1) % 2], 16)
            sp.wait_ge(b_out, 28)
            sp.dma_start(k.bias_dram[:, 6 * PIECE:], brow[:, 0, :]).then_inc(b_stored[0], 16)
            sp.wait_ge(b_stored[0], 16 * 4)
            sp.wait_ge(b_stored[1], 16 * 3)
            flat = k.bias_dram.rearrange("h (q n) -> (h q) n", n=KEYS)
            sp.dma_start(k.bias[:, 0:4, :], flat[0:4 * CH, :].rearrange("(c r) n -> r c n", c=4)).then_inc(table_in, 16)
            sp.dma_start(k.bias[:, 4, :], flat[HQ - CH:HQ, :]).then_inc(table_in, 16)
            sp.wait_ge(table_in, 32)

        @block.vector
        def _(dve):
            n = [0]

            def link(ins):
                n[0] += 1
                ins.then_inc(chain, 1)
                dve.wait_ge(chain, n[0])

            for u in range(2):
                nc.vector.memset(k.xT[DIM_IN:AUG, u, :], 1.0)
                nc.vector.memset(k.xn[:, u, :, :, DIM_IN:AUG], 1.0)
            nc.vector.memset(k.three[:], 3.0)
            dve.wait_ge(loaded, 16 * LOADS)
            for i, (w, p, aug, rt, sc, tm) in enumerate(sets):
                nc.vector.tensor_scalar(rt[:], p[:, 3, :], EPS, None, ALU.add).then_inc(ready, 1)
            nc.vector.tensor_scalar(rt_p[:], pp[:, 3, :], EPS, None, ALU.add).then_inc(ready, 1)
            dve.wait_ge(root, 4)
            for i, (w, p, aug, rt, sc, tm) in enumerate(sets):
                link(nc.vector.reciprocal(tm[:], rt[:]))
                link(nc.vector.tensor_tensor(sc[:], tm[:], p[:, 0, :], ALU.mult))
                link(nc.vector.tensor_tensor(tm[:], p[:, 2, :], sc[:], ALU.mult))
                link(nc.vector.tensor_tensor(aug[:, :, DIM_IN], p[:, 1, :], tm[:], ALU.subtract))
                link(nc.vector.tensor_tensor(aug[:, :, 0:DIM_IN], w[:], bc(sc[:].unsqueeze(2), list(w.shape)), ALU.mult))
            nc.vector.tensor_copy(tm_q[:], sc_q[:]).then_inc(ready, 1)
            link(nc.vector.reciprocal(tm_p[:], rt_p[:]))
            link(nc.vector.tensor_tensor(sc_p[:], tm_p[:], pp[:, 0, :], ALU.mult))
            link(nc.vector.tensor_tensor(tm_p[:], pp[:, 2, :], sc_p[:], ALU.mult))
            link(nc.vector.tensor_tensor(k.prow[:], pp[:, 1, :], tm_p[:], ALU.subtract))
            link(nc.vector.tensor_scalar(sc_p[:], sc_p[:], 1.0 / 6.0, None, ALU.mult))
            link(nc.vector.tensor_tensor(k.pw[:], k.pw[:], bc(sc_p[:].unsqueeze(1), [128, 6, DIM]), ALU.mult))
            for j in range(3):
                dve.wait_ge(m_full, j + 1)
                nc.vector.tensor_copy(k.mh[:, 4 * j:4 * j + 4, :],
                                      bank[j][0:AUG, 0:4 * AUG].rearrange("p (h r) -> p h r", h=4))
            for j in range(2):
                dve.wait_ge(v_full, j + 1)
                nc.vector.tensor_copy(k.wv[:, 6 * j:6 * j + 6, :],
                                      bank[3 + j][0:AUG, 0:6 * VD].rearrange("p (h r) -> p h r", h=6))
            for p in range(7):
                dve.wait_ge(idx_in[p % 2], 16 * (p // 2 + 1))
                if p >= 2:
                    dve.wait_ge(b_full, 4 * (p - 1))
                for c in range(2):
                    nc.vector.tensor_scalar(onehot[:, p % 2, c, :], idx[:, p % 2, :], off_col[:, c:c + 1], None,
                                            ALU.is_equal).then_inc(hot, 1)

        @block.scalar
        def _(act):
            act.wait_ge(ready, 4)
            for rt in (rt_q, rt_k, rt_v, rt_p):
                nc.scalar.activation(rt[:], rt[:], ACT.Sqrt).then_inc(root, 1)
            for p in range(7):
                if p >= 2:
                    act.wait_ge(b_stored[p % 2], 16 * (p // 2))
                for t in range(4):
                    act.wait_ge(b_full, 4 * p + t + 1)
                    nc.scalar.activation(brow[:, p % 2, t * STRIP:(t + 1) * STRIP],
                                         bank[5 + (4 * p + t) % 3][0:HEADS, 0:STRIP], ACT.Copy).then_inc(b_out, 1)

        @block.tensor
        def _(pe):
            pe.wait_ge(ready, 5)
            for h in range(HEADS):
                mm = nc.tensor.matmul(bank[h // 4][0:AUG, (h % 4) * AUG:(h % 4 + 1) * AUG], qaug[:, h, :], kaug[:, h, :],
                                      start=True, stop=True)
                if h % 4 == 3:
                    mm.then_inc(m_full, 1)
            for h in range(HEADS):
                mm = nc.tensor.transpose(bank[3 + h // 6][0:AUG, (h % 6) * VD:(h % 6 + 1) * VD], vaug[:, h, :],
                                         k.ident[0:VD, 0:VD])
                if h % 6 == 5:
                    mm.then_inc(v_full, 1)
            for p in range(7):
                pe.wait_ge(hot, 2 * (p + 1))
                for t in range(4):
                    if 4 * p + t >= 3:
                        pe.wait_ge(b_out, 4 * p + t - 2)
                    for c in range(2):
                        mm = nc.tensor.matmul(bank[5 + (4 * p + t) % 3][0:HEADS, 0:STRIP], ab[:, c, :],
                                              onehot[:, p % 2, c, t * STRIP:(t + 1) * STRIP],
                                              start=(c == 0), stop=(c == 1))
                    mm.then_inc(b_full, 1)


def token_stage(nc, a, k):
    with Stage(nc) as ctx:
        sb = lambda n, s, d=F32: ctx.enter_context(nc.sbuf_tensor(n, s, d))
        sem = lambda n: ctx.semaphore(n)
        qt = sb("qt", [AUG, 2, GROUP, HQ])
        sbias = sb("sbias", [CH, 2, CHUNKS, KEYS])
        prob = sb("prob", [CH, 2, CHUNKS, KEYS])
        low = sb("low", [CH, 2, CHUNKS])
        tally = sem("tally")
        total = sb("total", [CH, 2, CHUNKS])
        inv = sb("inv", [CH, 2, CHUNKS])
        pt = sb("pt", [KHALF, 2, 2, HQ])
        px = sb("px", [AUG, 2, HEADS, GTOK])
        shifted = sb("shifted", [128, 2, 2, GTOK])
        hs = sb("hs", [128, 2, 6, GTOK])
        xT_in, xn_in = [sem("xT_in0"), sem("xT_in1")], [sem("xn_in0"), sem("xn_in1")]
        s_full, s_max, p_exp, inv_done, p_norm = sem("s_full"), sem("s_max"), sem("p_exp"), sem("inv_done"), sem("p_norm")
        t_full, t_out, px_full, px_out = sem("t_full"), sem("t_out"), sem("px_full"), sem("px_out")
        q_full, q_out, o_full, o_relu, o_hs = sem("q_full"), sem("q_out"), sem("o_full"), sem("o_relu"), sem("o_hs")
        h_full, h_out = sem("h_full"), sem("h_out")
        s_bank, t_bank, px_bank, m_bank = k.banks[0:3], k.banks[3:5], k.banks[5:7], k.banks[7]
        BODY = 2 * GROUP
        STEPS = BATCH // BODY

        def run(eng, slot):
            slot_range = range(BODY)
            for j in slot_range:
                slot(0, j)
            with eng.Fori(1, STEPS - 1) as it:
                for j in slot_range:
                    slot(it, j)
            for it in (STEPS - 1, STEPS):
                for j in slot_range:
                    slot(it, j)
            slot(STEPS + 1, 0)

        def live(it, j, back, count=BATCH):
            return not isinstance(it, int) or 0 <= BODY * it + j - back < count

        def group_live(it, u, back):
            return not isinstance(it, int) or 0 <= 2 * it + u - back < GROUPS

        SHARED = [[("h", 0)], [("q", 0), ("q", 1), ("q", 2)], [("q", 3), ("q", 4), ("o", 0)], [("q", 5), ("o", 1), ("o", 2)]]
        BACK = {"q": -1, "h": 2, "o": 1}
        PER = {"q": 6, "h": 1, "o": 3}

        def shared_before(it, u, i, n):
            seen = {"q": 0, "h": 0, "o": 0}
            for ii in range(i + 1):
                for nn, (kind, _) in enumerate(SHARED[ii]):
                    if (ii, nn) < (i, n):
                        seen[kind] += 1
            out = {}
            for kind, c in seen.items():
                count = PER[kind] * (2 * it + u - BACK[kind]) + c
                if isinstance(it, int):
                    count = min(max(count, 0), PER[kind] * GROUPS)
                out[kind] = count
            return out

        order = [x for row in SHARED for x in row]

        @(block := ctx.enter_context(nc.Block())).sync
        def _(sp):
            def load_keys(g, u):
                sp.dma_start(k.xT[0:DIM_IN, u, :], a["xT"][:, bass.ds(g * GROUP * KEYS, GROUP * KEYS)]).then_inc(xT_in[u], 16)

            def load_rows(g, u):
                sp.dma_start(k.xn[:, u, :, :, 0:DIM_IN].rearrange("p b c i -> p (b c) i"),
                             a["xn"][:, bass.ds(g * GROUP * 2, GROUP * 2), :]).then_inc(xn_in[u], 16)

            for u in range(2):
                load_keys(u, u)
                load_rows(u, u)
            with sp.Fori(0, STEPS - 1) as it:
                for u in range(2):
                    sp.wait_ge(s_full, 3 * (BODY * it + GROUP * (u + 1)))
                    load_keys(2 * it + 2 + u, u)
                    sp.wait_ge(px_full, 2 * (BODY * it + GROUP * (u + 1)))
                    load_rows(2 * it + 2 + u, u)

        def rolled(j):
            return j // GROUP, j % GROUP

        @block.tensor
        def _(pe):
            def shared(it, u, i, n, kind, m):
                if not group_live(it, u, BACK[kind]):
                    return
                done = {"q": q_out, "h": h_out, "o": o_hs}
                before = shared_before(it, u, i, n)
                if isinstance(it, int):
                    for name, c in before.items():
                        at_least(pe, done[name], c)
                else:
                    prev = order[order.index((kind, m)) - 1][0]
                    at_least(pe, done[prev], before[prev])
                par = (u - BACK[kind]) % 2
                if kind == "q":
                    if m == 0:
                        pe.wait_ge(xT_in[par], 16 * (it + (1 if u == 0 else 2)))
                    for hh in range(2):
                        src = k.xT[:, par, :].rearrange("p (b r s c t) -> p b r s c t", b=GROUP, r=RESQ, s=2, c=RESQ)[:, :, :, 0, :, 0]
                        mm = nc.tensor.matmul(m_bank[0:AUG, hh * GTOK:(hh + 1) * GTOK], k.mh[:, 2 * m + hh, :],
                                              src, start=True, stop=True)
                    mm.then_inc(q_full, 1)
                elif kind == "o":
                    if m == 0:
                        at_least(pe, px_out, 2 * GROUP * (2 * it + u))
                    for jj in range(2):
                        for hh in range(2):
                            mm = nc.tensor.matmul(m_bank[64 * hh:64 * hh + 64, jj * GTOK:(jj + 1) * GTOK],
                                                  k.wv[:, 4 * m + 2 * jj + hh, :], px[:, par, 4 * m + 2 * jj + hh, :],
                                                  start=True, stop=True)
                    mm.then_inc(o_full, 1)
                else:
                    at_least(pe, o_hs, 3 * (2 * it + u - 1))
                    for t in range(2):
                        for j in range(6):
                            mm = nc.tensor.matmul(m_bank[0:ROWS, t * DIM:(t + 1) * DIM],
                                                  hs[:, par, j, t * ROWS:(t + 1) * ROWS], k.pw[:, j, :],
                                                  start=(j == 0), stop=(j == 5))
                    mm.then_inc(h_full, 1)

            def slot(it, j):
                u, i = rolled(j)
                s = BODY * it + j
                if live(it, j, 0):
                    if i == 0:
                        at_least(pe, q_out, 6 * (2 * it + u + 1))
                    for p, chunks in enumerate(PIECES):
                        if live(it, j, 1):
                            pe.wait_ge(s_max, 5 * (s - 1) + chunks[-1] + 1)
                        for n, c in enumerate(chunks):
                            mm = nc.tensor.matmul(s_bank[p][0:CH, n * KEYS:(n + 1) * KEYS],
                                                  qt[:, u, i, CHUNK_AT[c]:CHUNK_AT[c] + CH],
                                                  k.xT[:, u, i * KEYS:(i + 1) * KEYS], start=True, stop=True)
                        mm.then_inc(s_full, 1)
                def turn_piece(p, chunks):
                    if not live(it, j, 1):
                        return
                    par = (j - 1) % 2
                    pe.wait_ge(p_norm, 3 * (s - 1) + p + 1)
                    at_least(pe, t_out, 3 * (s - 1) + p - 1)
                    for n, c in enumerate(chunks):
                        for kc in range(2):
                            mm = nc.tensor.transpose(
                                t_bank[(3 * (j - 1) + p) % 2][0:KHALF, (2 * n + kc) * CH:(2 * n + kc + 1) * CH],
                                prob[:, par, c, kc * KHALF:(kc + 1) * KHALF], k.ident[0:CH, 0:CH])
                    mm.then_inc(t_full, 1)

                def weigh(half):
                    if not live(it, j, 2):
                        return
                    bu, bi = rolled((j - 2) % BODY)
                    if half == 0:
                        if bi == 0:
                            pe.wait_ge(xn_in[bu], 16 * (it + 1))
                        pe.wait_ge(t_out, 3 * (s - 1))
                    at_least(pe, px_out, 2 * (s - 3) + half + 1)
                    for kc in range(2):
                        mm = nc.tensor.matmul(px_bank[half][0:AUG, 0:HQ // 2], k.xn[:, bu, bi, kc, :],
                                              pt[:, j % 2, kc, half * (HQ // 2):(half + 1) * (HQ // 2)],
                                              start=(kc == 0), stop=(kc == 1))
                    mm.then_inc(px_full, 1)

                weigh(0)
                for n in range(3):
                    if n < len(SHARED[i]):
                        shared(it, u, i, n, *SHARED[i][n])
                    if n == 0:
                        weigh(1)
                    turn_piece(n, PIECES[n])

            pe.wait_ge(xT_in[0], 16)
            for m in range(6):
                at_least(pe, q_out, m)
                for hh in range(2):
                    src = k.xT[:, 0, :].rearrange("p (b r s c t) -> p b r s c t", b=GROUP, r=RESQ, s=2, c=RESQ)[:, :, :, 0, :, 0]
                    mm = nc.tensor.matmul(m_bank[0:AUG, hh * GTOK:(hh + 1) * GTOK], k.mh[:, 2 * m + hh, :], src,
                                          start=True, stop=True)
                mm.then_inc(q_full, 1)
            run(pe, slot)

        @block.vector
        def _(dve):
            def slot(it, j):
                u, i = rolled(j)
                s = BODY * it + j
                if live(it, j, 1):
                    par = (j - 1) % 2
                    dve.wait_ge(p_exp, s)
                    nc.vector.reciprocal(inv[:, par, :], total[:, par, :]).then_inc(inv_done, 1)
                    dve.wait_ge(inv_done, s)
                    for p, chunks in enumerate(PIECES):
                        for c in chunks:
                            ins = nc.vector.tensor_scalar(prob[:, par, c, :], prob[:, par, c, :], inv[:, par, c:c + 1], None, ALU.mult)
                        ins.then_inc(p_norm, 1)
                if live(it, j, 0):
                    par = j % 2
                    for p, chunks in enumerate(PIECES):
                        dve.wait_ge(s_full, 3 * s + p + 1)
                        if p == 0 and live(it, j, 2):
                            dve.wait_ge(p_exp, s - 1)
                        carry_waits(dve, tally)
                        for n, c in enumerate(chunks):
                            nc.vector.tensor_tensor_reduce(
                                sbias[:, par, c, :], s_bank[p][0:CH, n * KEYS:(n + 1) * KEYS], k.bias[:, c, :],
                                -1.0, 3e38, ALU.add, ALU.min, low[:, par, c:c + 1]).then_inc(s_max, 1)
                if live(it, j, 2):
                    bu, bi = rolled((j - 2) % BODY)
                    if bi == 0:
                        at_least(dve, o_full, 3 * ((2 * it + (u if i >= 2 else u - 1)) - 1))
                    for half in range(2):
                        dve.wait_ge(px_full, 2 * (s - 2) + half + 1)
                        nc.vector.tensor_copy(px[:, bu, 6 * half:6 * half + 6, bi * QUERIES:(bi + 1) * QUERIES],
                                                    px_bank[half][0:AUG, 0:HQ // 2].rearrange("p (h q) -> p h q", h=6)).then_inc(px_out, 1)
                for kind, m in SHARED[i]:
                    if kind == "h" and group_live(it, u, 2):
                        dve.wait_ge(h_full, 2 * it + u - 1)
                        nc.vector.tensor_tensor(k.h[:, bass.ds(4 * it + 2 * u - 4, 2), :],
                                                m_bank[0:ROWS, 0:2 * DIM].rearrange("p (t d) -> p t d", t=2),
                                                bc(k.prow[0:ROWS, :].unsqueeze(1), [ROWS, 2, DIM]), ALU.add).then_inc(h_out, 1)
                    if kind == "o" and group_live(it, u, 1):
                        par = (u - 1) % 2
                        n = (3 * par + m) % 2
                        if m == 0:
                            at_least(dve, h_full, 2 * it + u - 1)
                        dve.wait_ge(o_relu, 3 * (2 * it + u - 1) + m + 1)
                        nc.vector.scalar_tensor_tensor(hs[:, par, 2 * m:2 * m + 2, :], shifted[:, n, :, :], 6.0,
                                                       m_bank[:, 0:2 * GTOK].rearrange("p (t d) -> p t d", t=2),
                                                       ALU.min, ALU.mult).then_inc(o_hs, 1)

            run(dve, slot)
            dve.wait_ge(h_out, GROUPS)

        @block.scalar
        def _(act):
            def evacuate_q(it, u, m, par):
                dst = qt[:, par, :, :].rearrange("p b (h q) -> p h b q", h=HEADS)
                for hh in range(2):
                    ins = nc.scalar.activation(dst[:, 2 * m + hh, :, :],
                                               m_bank[0:AUG, hh * GTOK:(hh + 1) * GTOK].rearrange("p (b q) -> p b q", b=GROUP),
                                               ACT.Copy, scale=KD ** -0.5)
                ins.then_inc(q_out, 1)

            def slot(it, j):
                u, i = rolled(j)
                s = BODY * it + j
                if live(it, j, 0):
                    par = j % 2
                    if live(it, j, 2):
                        act.wait_ge(t_full, 3 * (s - 1))
                    for c in range(CHUNKS):
                        act.wait_ge(s_max, 5 * s + c + 1)
                        ins = nc.scalar.activation(prob[:, par, c, :], sbias[:, par, c, :], ACT.Exp, bias=low[:, par, c:c + 1],
                                                   scale=-1.0, accum_out=total[:, par, c:c + 1])
                    ins.then_inc(p_exp, 1)
                def leave_shared(kind, m):
                    if kind == "q" and group_live(it, u, -1):
                        if m == 0:
                            at_least(act, s_full, 3 * GROUP * (2 * it + u))
                        act.wait_ge(q_full, 6 * (2 * it + u + 1) + m + 1)
                        evacuate_q(it, u, m, (u + 1) % 2)
                    if kind == "o" and group_live(it, u, 1):
                        par = (u - 1) % 2
                        n = (3 * par + m) % 2
                        at_least(act, o_hs, 3 * (2 * it + u - 1) + m - 1)
                        act.wait_ge(o_full, 3 * (2 * it + u - 1) + m + 1)
                        nc.scalar.activation(shifted[:, n, :, :], m_bank[:, 0:2 * GTOK].rearrange("p (t d) -> p t d", t=2),
                                             ACT.Relu, bias=k.three[:, 0:1]).then_inc(o_relu, 1)

                def leave_turned(p, chunks):
                    par = (j - 1) % 2
                    if p == 0 and live(it, j, 3):
                        act.wait_ge(px_full, 2 * (s - 2))
                    act.wait_ge(t_full, 3 * (s - 1) + p + 1)
                    src = t_bank[(3 * (j - 1) + p) % 2][0:KHALF, 0:2 * CH * len(chunks)].rearrange(
                        "p (n c r) -> p c n r", n=len(chunks), c=2)
                    at = CHUNK_AT[chunks[0]]
                    if p == 2:
                        act.wait_ge(t_out, 3 * (s - 1) + p)
                    nc.scalar.activation(pt[:, par, :, at:at + CH * len(chunks)].rearrange("p c (n r) -> p c n r", r=CH), src,
                                         ACT.Copy).then_inc(t_out, 1)

                for n in range(3):
                    if n < len(SHARED[i]):
                        leave_shared(*SHARED[i][n])
                    if live(it, j, 1):
                        leave_turned(n, PIECES[n])

            for m in range(6):
                act.wait_ge(q_full, m + 1)
                evacuate_q(0, 0, m, 0)
            run(act, slot)


def peeled(eng, steps, body):
    body(0)
    with eng.Fori(1, steps) as it:
        body(it)


class Norm:

    def __init__(self, nc, ctx, name):
        sb = lambda n, s: ctx.enter_context(nc.sbuf_tensor(f"{name}_{n}", s, F32))
        self.nc = nc
        self.raw = sb("raw", [ROWS, TILES, 6])
        self.mean, self.var, self.rstd = sb("mean", [ROWS, TILES]), sb("var", [ROWS, TILES]), sb("rstd", [ROWS, TILES])
        self.half, self.gap = sb("half", [ROWS, TILES]), sb("gap", [ROWS, TILES])
        self.rows_seen, self.chain, self.var_ready, self.root_done, self.rstd_ready = (
            ctx.semaphore(f"{name}_{n}") for n in ("rows_seen", "chain", "var_ready", "root_done", "rstd_ready"))

    def vector_part(self, dve, x):
        nc, n = self.nc, [0]

        def link(ins):
            n[0] += 1
            ins.then_inc(self.chain, 1)
            dve.wait_ge(self.chain, n[0])

        with dve.Fori(0, TILES // 4) as it:
            for t in range(4):
                nc.vector.bn_stats(self.raw[:, 4 * it + t, :], x[:, 4 * it + t, :]).then_inc(self.rows_seen, 1)
        dve.wait_ge(self.rows_seen, TILES)
        m0, c0, m1, c1 = self.raw[:, :, 1], self.raw[:, :, 2], self.raw[:, :, 4], self.raw[:, :, 5]
        link(nc.vector.tensor_tensor(self.half[:], m0, m1, ALU.add))
        link(nc.vector.tensor_scalar(self.mean[:], self.half[:], 0.5, None, ALU.mult))
        link(nc.vector.tensor_tensor(self.gap[:], m0, m1, ALU.subtract))
        link(nc.vector.tensor_tensor(self.gap[:], self.gap[:], self.gap[:], ALU.mult))
        link(nc.vector.tensor_tensor(self.half[:], c0, c1, ALU.add))
        link(nc.vector.tensor_scalar(self.half[:], self.half[:], 1.0 / DIM, EPS, ALU.mult, ALU.add))
        nc.vector.scalar_tensor_tensor(self.var[:], self.gap[:], 0.25, self.half[:], ALU.mult, ALU.add).then_inc(self.var_ready, 1)
        dve.wait_ge(self.root_done, 1)
        nc.vector.reciprocal(self.rstd[:], self.var[:]).then_inc(self.rstd_ready, 1)
        dve.wait_ge(self.rstd_ready, 1)

    def scalar_part(self, act):
        act.wait_ge(self.var_ready, 1)
        self.nc.scalar.activation(self.var[:], self.var[:], ACT.Sqrt).then_inc(self.root_done, 1)


BT = 4
BTOK = BT * ROWS


def band_stage(nc, a, k):
    with Stage(nc) as ctx:
        sb = lambda n, s, d=F32: ctx.enter_context(nc.sbuf_tensor(n, s, d))
        sem = lambda n: ctx.semaphore(n)
        norm_a, norm_b = Norm(nc, ctx, "band"), Norm(nc, ctx, "ffn")
        w = sb("band_w", [DIM, 4, DIM])
        uv = sb("uv", [DIM, 1])
        vv = sb("vv", [ROWS, DIM])
        trig = sb("trig", [DIM, 2, QUERIES])
        mask = sb("mask", [ROWS, ROWS])
        rows = sb("rows", [ROWS, 2, BT, DIM])
        xt = sb("xt", [DIM, 2, BTOK])
        turn = sb("turn", [DIM, 2, 4, BTOK])
        rot = sb("rot", [DIM, 2, 2, BTOK])
        sval = sb("sval", [DIM, 2, BTOK])
        smask = sb("smask", [ROWS, 2, BT, ROWS])
        prob = sb("bprob", [ROWS, 2, BT, ROWS])
        junk = sb("junk", [ROWS, 2, BT, ROWS])
        low, den, num = sb("blow", [ROWS, 2, BT]), sb("bden", [ROWS, 2, BT]), sb("bnum", [ROWS, 2, BT])
        tally = sem("b_tally")
        yrow = sb("yrow", [ROWS, 4, DIM])
        names = ("w_in", "rows_done", "tr", "xt_out", "proj", "s_out", "turned", "rotated", "s_full", "s_low", "p_exp",
                 "num_done", "inv_done", "ratio", "h_done", "y_done", "sum_done")
        (w_in, rows_done, tr, xt_out, proj, s_out, turned, rotated, s_full, s_low, p_exp, num_done, inv_done, ratio,
         h_done, y_done, sum_done) = (sem("b_" + n) for n in names)
        xt_bank, s_bank, v_bank, q_banks = k.banks[0], k.banks[6:8], k.banks[5], k.banks[1:5]
        STEPS = TILES // BT // 2
        block = ctx.enter_context(nc.Block())

        @block.sync
        def _(sp):
            sp.dma_start(w[:], a["band_w"]).then_inc(w_in, 16)
            sp.dma_start(uv[:], a["u_v"]).then_inc(w_in, 16)
            sp.dma_start(vv[:], a["v_v"].partition_broadcast(ROWS)).then_inc(w_in, 16)
            sp.dma_start(trig[:], a["trig"]).then_inc(w_in, 16)
            sp.dma_start(mask[:], a["band_mask"]).then_inc(w_in, 16)

        @block.vector
        def _(dve):
            norm_a.vector_part(dve, k.h)
            dve.wait_ge(w_in, 16 * 5)

            def make_rows(it, u):
                g = 2 * it + u
                at_least(dve, tr, g - 1)
                for t in range(BT):
                    tile = 4 * g + t
                    ins = nc.vector.tensor_scalar(rows[:, u, t, :], k.h[:, tile, :], norm_a.mean[:, bass.ds(tile, 1)],
                                                  norm_a.rstd[:, bass.ds(tile, 1)], ALU.subtract, ALU.mult)
                ins.then_inc(rows_done, 1)

            def rotate(it, u):
                g = 2 * it + u
                dve.wait_ge(proj, g + 1)
                at_least(dve, s_full, g - 1)
                for i in range(4):
                    ins = nc.vector.tensor_tensor(turn[:, u, i, :].rearrange("p (b q) -> p b q", q=QUERIES),
                                                  q_banks[i][:, 0:BTOK].rearrange("p (b q) -> p b q", q=QUERIES),
                                                  bc(trig[:, i % 2, :].unsqueeze(1), [DIM, BTOK // QUERIES, QUERIES]), ALU.mult)
                ins.then_inc(turned, 1)
                dve.wait_ge(turned, g + 1)
                for i in range(2):
                    ins = nc.vector.tensor_tensor(rot[:, u, i, :], turn[:, u, 2 * i, :], turn[:, u, 2 * i + 1, :], ALU.add)
                ins.then_inc(rotated, 1)

            def lowest(it, u):
                g = 2 * it + u
                dve.wait_ge(s_full, g + 1)
                at_least(dve, p_exp, g - 1)
                carry_waits(dve, tally)
                for t in range(BT):
                    ins = nc.vector.tensor_tensor_reduce(smask[:, u, t, :], s_bank[u][0:ROWS, t * ROWS:(t + 1) * ROWS], mask[:],
                                                         -(DIM ** -0.5), 3e38, ALU.add, ALU.min, low[:, u, t:t + 1])
                ins.then_inc(s_low, 1)

            def add_rows(it, u):
                g = 2 * it + u
                dve.wait_ge(p_exp, g + 1)
                dve.wait_ge(s_out, g + 1)
                for t in range(BT):
                    ins = nc.vector.tensor_tensor_reduce(junk[:, u, t, :], prob[:, u, t, :], sval[0:ROWS, u, t * ROWS:(t + 1) * ROWS],
                                                         1.0, 0.0, ALU.mult, ALU.add, num[:, u, t:t + 1])
                ins.then_inc(num_done, 1)
                nc.vector.reciprocal(den[:, u, :], den[:, u, :]).then_inc(inv_done, 1)
                dve.wait_ge(num_done, g + 1)
                dve.wait_ge(inv_done, g + 1)
                nc.vector.tensor_tensor(num[:, u, :], num[:, u, :], den[:, u, :], ALU.mult).then_inc(ratio, 1)
                dve.wait_ge(ratio, g + 1)
                for t in range(BT):
                    tile = 4 * g + t
                    ins = nc.vector.scalar_tensor_tensor(k.h[:, tile, :], vv[:], num[:, u, t:t + 1], k.h[:, tile, :],
                                                         ALU.mult, ALU.add)
                ins.then_inc(h_done, 1)

            def body(it):
                make_rows(it, 0)
                make_rows(it, 1)
                rotate(it, 0)
                lowest(it, 0)
                rotate(it, 1)
                add_rows(it, 0)
                lowest(it, 1)
                add_rows(it, 1)

            peeled(dve, STEPS, body)
            dve.wait_ge(h_done, 2 * STEPS)
            norm_b.vector_part(dve, k.h)

            def add_norm(it):
                at_least(dve, sum_done, it)
                for t in range(4):
                    tile = 4 * it + t
                    ins = nc.vector.tensor_scalar(yrow[:, t, :], k.h[:, tile, :], norm_b.mean[:, bass.ds(tile, 1)],
                                                  norm_b.rstd[:, bass.ds(tile, 1)], ALU.subtract, ALU.mult)
                ins.then_inc(y_done, 1)
                dve.wait_ge(y_done, it + 1)
                nc.vector.tensor_tensor(k.h[:, bass.ds(4 * it, 4), :], k.h[:, bass.ds(4 * it, 4), :], yrow[:], ALU.add).then_inc(sum_done, 1)

            peeled(dve, TILES // 4, add_norm)
            dve.wait_ge(sum_done, TILES // 4)

        @block.tensor
        def _(pe):
            pe.wait_ge(w_in, 16 * 5)

            def turn_rows(it, u):
                g = 2 * it + u
                pe.wait_ge(rows_done, g + 1)
                at_least(pe, xt_out, g)
                for t in range(BT):
                    mm = nc.tensor.transpose(xt_bank[:, t * ROWS:(t + 1) * ROWS], rows[:, u, t, :], k.ident[0:ROWS, 0:ROWS])
                mm.then_inc(tr, 1)

            def project(it, u):
                g = 2 * it + u
                pe.wait_ge(xt_out, g + 1)
                at_least(pe, turned, g)
                at_least(pe, s_out, g)
                for i in range(4):
                    nc.tensor.matmul(q_banks[i][:, 0:BTOK], w[:, i, :], xt[:, u, :], start=True, stop=True)
                nc.tensor.matmul(v_bank[:, 0:BTOK], bc(uv[:, 0:1], [DIM, DIM]), xt[:, u, :], start=True, stop=True).then_inc(proj, 1)

            def scores(it, u):
                g = 2 * it + u
                pe.wait_ge(rotated, g + 1)
                at_least(pe, s_low, g - 1)
                for t in range(BT):
                    mm = nc.tensor.matmul(s_bank[u][0:ROWS, t * ROWS:(t + 1) * ROWS], rot[:, u, 0, t * ROWS:(t + 1) * ROWS],
                                          rot[:, u, 1, t * ROWS:(t + 1) * ROWS], start=True, stop=True)
                mm.then_inc(s_full, 1)

            def body(it):
                turn_rows(it, 0)
                project(it, 0)
                turn_rows(it, 1)
                project(it, 1)
                scores(it, 0)
                scores(it, 1)

            peeled(pe, STEPS, body)

        @block.scalar
        def _(act):
            norm_a.scalar_part(act)

            def copy_x(it, u):
                g = 2 * it + u
                act.wait_ge(tr, g + 1)
                at_least(act, proj, g - 1)
                nc.scalar.activation(xt[:, u, :], xt_bank[:, 0:BTOK], ACT.Copy).then_inc(xt_out, 1)

            def copy_s(it, u):
                g = 2 * it + u
                act.wait_ge(proj, g + 1)
                at_least(act, num_done, g - 1)
                nc.scalar.activation(sval[:, u, :], v_bank[:, 0:BTOK], ACT.Copy).then_inc(s_out, 1)

            def expo(it, u):
                g = 2 * it + u
                act.wait_ge(s_low, g + 1)
                at_least(act, ratio, g - 1)
                for t in range(BT):
                    ins = nc.scalar.activation(prob[:, u, t, :], smask[:, u, t, :], ACT.Exp, bias=low[:, u, t:t + 1], scale=-1.0,
                                               accum_out=den[:, u, t:t + 1])
                ins.then_inc(p_exp, 1)

            def body(it):
                copy_x(it, 0)
                copy_s(it, 0)
                copy_x(it, 1)
                copy_s(it, 1)
                expo(it, 0)
                expo(it, 1)

            peeled(act, STEPS, body)
            norm_b.scalar_part(act)


XH, XE, SRC, LLM = 8, 16, 250, 1024
SHALF = SRC // 2
LCH = LLM // 128


def cross_stage(nc, a, k):
    with Stage(nc) as ctx:
        sb = lambda n, s, d=F32: ctx.enter_context(nc.sbuf_tensor(n, s, d))
        sem = lambda n: ctx.semaphore("c_" + n)
        norm = Norm(nc, ctx, "cross")
        srcT, valT = sb("srcT", [128, LCH, SRC]), sb("valT", [128, LCH, SRC])
        wk, wv = sb("cwk", [128, LCH, DIM]), sb("cwv", [128, LCH, DIM])
        wq, wo = sb("cwq", [DIM, DIM]), sb("cwo", [DIM, DIM])
        bq, bk = sb("cbq", [DIM, 1]), sb("cbk", [DIM, 1])
        own, bk_own = sb("own", [DIM, XH]), sb("bk_own", [DIM, XH])
        bv, bo, ones = sb("cbv", [SHALF, DIM]), sb("cbo", [1, DIM]), sb("cones", [1, ROWS])
        kT = sb("kT", [DIM, XH, SRC])
        v = sb("cv", [SHALF, 2, XH, DIM])
        rows = sb("crows", [ROWS, 2, DIM])
        turned = sb("turned", [DIM, 2, 2, ROWS])
        qT = sb("qT", [DIM, 2, ROWS])
        prob = sb("cprob", [ROWS, 2, XH, SRC])
        low, total, inv = sb("clow", [ROWS, 2, XH]), sb("ctotal", [ROWS, 2, XH]), sb("cinv", [ROWS, 2, DIM])
        pt = sb("cpt", [SHALF, 2, XH, 2, ROWS])
        one_by = sb("one_by", [ROWS, 2, XH])
        ot = sb("cot", [DIM, 2, ROWS])
        names = ("w_in", "kv_full", "kv_out", "bias_done", "rows_done", "tr", "tr_out", "q_full", "q_out", "s_full", "s_low",
                 "p_exp", "t_full", "t_out", "t_last", "one_by_done", "inv_done", "pv_full", "o_done", "wo_full", "h_done")
        (w_in, kv_full, kv_out, bias_done, rows_done, tr, tr_out, q_full, q_out, s_full, s_low,
         p_exp, t_full, t_out, t_last, one_by_done, inv_done, pv_full, o_done, wo_full, h_done) = (sem(n) for n in names)
        s_bank, t_bank, pv_bank, m_bank = k.banks[0:4], k.banks[4:6], k.banks[6], k.banks[7]
        STEPS = TILES // 4
        LOADS = 11
        table, gslope, cell = sb("table", [128, 4096]), sb("gslope", [128, 16, 128]), sb("cell", [128, 16])
        zeros = sb("zeros", [128, SLOTS // 512 * DIM])
        table_in, moe_in, zeroed, split = sem("table_in"), sem("moe_in"), sem("zeroed"), sem("split")

        def run(eng, slot):
            for it in (-1, 0):
                for j in range(4):
                    slot(it, j)
            with eng.Fori(1, STEPS - 1) as it:
                for j in range(4):
                    slot(it, j)
            for it in (STEPS - 1, STEPS):
                for j in range(4):
                    slot(it, j)

        def live(it, j, back):
            return not isinstance(it, int) or 0 <= 4 * it + j - back < TILES

        block = ctx.enter_context(nc.Block())

        @block.sync
        def _(sp):
            for dst, src in ((srcT, "srcT"), (wk, "x_wk"), (valT, "valT"), (wv, "x_wv"), (wq, "x_wq"), (wo, "x_wo"),
                             (bq, "x_bq"), (bk, "x_bk"), (bo, "x_bo"), (own, "own")):
                sp.dma_start(dst[:], a[src]).then_inc(w_in, 16)
            sp.dma_start(bv[:], a["x_bv"].partition_broadcast(SHALF)).then_inc(w_in, 16)
            sp.dma_start(table[:], a["spline"]).then_inc(table_in, 16)
            sp.dma_start(cell[:], a["cell"].partition_broadcast(128)).then_inc(table_in, 16)
            sp.dma_start(k.wd[:], a["wd"]).then_inc(moe_in, 16)
            sp.dma_start(k.wu[:], a["wu"]).then_inc(moe_in, 16)
            sp.wait_ge(zeroed, 1)
            slots = k.x_slots.rearrange("(n p r) d -> n p (r d)", n=4, p=128)
            for i in range(4):
                sp.dma_start(slots[i], zeros[:]).then_inc(moe_in, 16)
            sp.wait_ge(moe_in, 16 * 6)

        @block.gpsimd
        def _(pool):
            nc.gpsimd.memset(zeros[:], 0.0).then_inc(zeroed, 1)
            pool.wait_ge(zeroed, 1)
            nc.gpsimd.memset(k.lines_lo[EXPERTS:128, :], 0.0).then_inc(zeroed, 1)
            pool.wait_ge(zeroed, 2)
            pool.wait_ge(table_in, 32)
            tv = table[:].rearrange("p (g c h) -> p g c h", g=16, c=2)
            shape = [128, 16, 128]
            nc.gpsimd.tensor_tensor(gslope[:], tv[:, :, 1, :], bc(cell[:].unsqueeze(2), shape), ALU.mult).then_inc(split, 1)
            pool.wait_ge(split, 1)
            nc.gpsimd.tensor_tensor(tv[:, :, 0, :], tv[:, :, 0, :], gslope[:], ALU.subtract).then_inc(split, 1)
            pool.wait_ge(split, 2)
            nc.gpsimd.tensor_copy(k.lines_hi[:], table[:]).then_inc(split, 1)
            pool.wait_ge(split, 3)
            nc.gpsimd.tensor_tensor(table[:], table[:], k.lines_hi[:], ALU.subtract).then_inc(split, 1)
            pool.wait_ge(split, 4)
            nc.gpsimd.tensor_copy(k.lines_hi[64:128, :], table[64:128, :]).then_inc(split, 1)
            pool.wait_ge(split, 5)
            nc.gpsimd.tensor_copy(k.lines_lo[0:64, :], table[0:64, :]).then_inc(split, 1)
            pool.wait_ge(split, 6)
            nc.gpsimd.tensor_tensor(table[0:64, :], table[0:64, :], k.lines_lo[0:64, :], ALU.subtract).then_inc(split, 1)
            pool.wait_ge(split, 7)
            nc.gpsimd.tensor_copy(k.lines_lo[0:64, :], table[0:64, :]).then_inc(split, 1)


        def q_turn(it, j):
            return live(it, j, -1)

        def turn_live(it, j):
            return live(it, j, -2) or live(it, j, 1)

        @block.tensor
        def _(pe):
            pe.wait_ge(w_in, 16 * LOADS)
            for c in range(LCH):
                mm = nc.tensor.matmul(s_bank[0][:, 0:SRC], wk[:, c, :], srcT[:, c, :], start=(c == 0), stop=(c == LCH - 1))
            mm.then_inc(kv_full, 1)
            for kc in range(2):
                for c in range(LCH):
                    mm = nc.tensor.matmul(s_bank[2 + kc][0:SHALF, 0:DIM], valT[:, c, kc * SHALF:(kc + 1) * SHALF], wv[:, c, :],
                                          start=(c == 0), stop=(c == LCH - 1))
                mm.then_inc(kv_full, 1)

            def scores(it, j, b):
                t = 4 * it + j
                if live(it, j, 0):
                    if b == 0:
                        pe.wait_ge(q_out, t + 1)
                    if live(it, j, 1):
                        pe.wait_ge(p_exp, 4 * (t - 1) + b + 1)
                    elif b == 0:
                        pe.wait_ge(kv_out, 3 * XH)
                    for n in range(2):
                        mm = nc.tensor.matmul(s_bank[b][0:ROWS, n * SRC:(n + 1) * SRC], qT[:, j % 2, :], kT[:, 2 * b + n, :],
                                              start=True, stop=True)
                    mm.then_inc(s_full, 1)

            def turn_probs(it, j, b):
                t = 4 * it + j
                if live(it, j, 1):
                    pe.wait_ge(p_exp, 4 * (t - 1) + b + 1)
                    if b == 1:
                        at_least(pe, t_last, t - 1)
                    else:
                        at_least(pe, t_out, 3 * (t - 1) + max(b - 1, 0))
                    for n in range(2):
                        for kc in range(2):
                            mm = nc.tensor.transpose(t_bank[b % 2][0:SHALF, (2 * n + kc) * ROWS:(2 * n + kc + 1) * ROWS],
                                                     prob[:, (j - 1) % 2, 2 * b + n, kc * SHALF:(kc + 1) * SHALF], k.ident[0:ROWS, 0:ROWS])
                    mm.then_inc(t_full, 1)

            def values(it, j, b):
                t = 4 * it + j
                if live(it, j, 2):
                    if b == 0:
                        pe.wait_ge(t_out, 3 * (t - 1))
                        pe.wait_ge(t_last, t - 1)
                        at_least(pe, o_done, t - 2)
                    for n in range(2):
                        for kc in range(2):
                            half = slice(64 * (b // 2), 64 * (b // 2) + 64)
                            mm = nc.tensor.matmul(pv_bank[half, 0:ROWS], v[:, kc, 2 * b + n, half], pt[:, j % 2, 2 * b + n, kc, :],
                                                  start=(b % 2 == 0 and n == 0 and kc == 0), stop=(b % 2 == 1 and n == 1 and kc == 1))
                    if b == 3:
                        mm.then_inc(pv_full, 1)

            def queries(it, j):
                t = 4 * it + j
                if q_turn(it, j):
                    pe.wait_ge(tr_out, t + 2)
                    nc.tensor.matmul(m_bank[:, 0:ROWS], wq[:], turned[:, (j - 1) % 2, 0, :], start=True, stop=True).then_inc(q_full, 1)

            def out_rows(it, j):
                t = 4 * it + j
                if live(it, j, 3):
                    pe.wait_ge(o_done, t - 2)
                    if q_turn(it, j):
                        pe.wait_ge(q_out, t + 2)
                    else:
                        pe.wait_ge(tr_out, min(t + 2, TILES + 3))
                        pe.wait_ge(h_done, t - 3)
                    nc.tensor.matmul(m_bank[0:ROWS, 0:DIM], ot[:, (j - 3) % 2, :], wo[:], start=True, stop=False)
                    nc.tensor.matmul(m_bank[0:ROWS, 0:DIM], ones[:], bo[:], start=False, stop=True).then_inc(wo_full, 1)

            def turn(it, j):
                t = 4 * it + j
                if turn_live(it, j):
                    if live(it, j, 3):
                        pe.wait_ge(h_done, t - 2)
                    elif q_turn(it, j):
                        pe.wait_ge(q_out, t + 2)
                    if live(it, j, -2):
                        pe.wait_ge(rows_done, t + 3)
                        mm = nc.tensor.transpose(m_bank[:, 0:ROWS], rows[:, j % 2, :], k.ident[0:ROWS, 0:ROWS])
                    if live(it, j, 1):
                        pe.wait_ge(inv_done, t)
                        mm = nc.tensor.transpose(m_bank[:, ROWS:2 * ROWS], inv[:, (j - 1) % 2, :], k.ident[0:ROWS, 0:ROWS])
                    mm.then_inc(tr, 1)

            def slot(it, j):
                scores(it, j, 0)
                turn_probs(it, j, 0)
                queries(it, j)
                values(it, j, 0)
                scores(it, j, 1)
                turn_probs(it, j, 1)
                out_rows(it, j)
                values(it, j, 1)
                scores(it, j, 2)
                turn_probs(it, j, 2)
                values(it, j, 2)
                scores(it, j, 3)
                turn(it, j)
                turn_probs(it, j, 3)
                values(it, j, 3)

            run(pe, slot)

        @block.vector
        def _(dve):
            nc.vector.memset(ones[:], 1.0).then_inc(bias_done, 1)
            nc.vector.memset(v[:], 0.0).then_inc(bias_done, 1)
            norm.vector_part(dve, k.h)
            dve.wait_ge(w_in, 16 * LOADS)
            dve.wait_ge(bias_done, 2)
            nc.vector.tensor_scalar(bq[:], bq[:], XE ** -0.5, None, ALU.mult).then_inc(bias_done, 1)
            nc.vector.tensor_scalar(bk_own[:], own[:], bk[:, 0:1], None, ALU.mult).then_inc(bias_done, 1)
            for kc in range(2):
                dve.wait_ge(kv_full, 2 + kc)
                for h in range(XH):
                    at = slice(h * XE, (h + 1) * XE)
                    nc.vector.tensor_tensor(v[:, kc, h, at], s_bank[2 + kc][0:SHALF, at], bv[:, at], ALU.add).then_inc(kv_out, 1)

            def make_rows(it, j):
                t = 4 * it + j
                if live(it, j, -3):
                    at_least(dve, tr, t + 2)
                    nc.vector.tensor_scalar(rows[:, (j + 1) % 2, :].unsqueeze(1), k.h[:, bass.ds(t + 3, 1), :],
                                            norm.mean[:, bass.ds(t + 3, 1)], norm.rstd[:, bass.ds(t + 3, 1)],
                                            ALU.subtract, ALU.mult).then_inc(rows_done, 1)

            def slot(it, j):
                t = 4 * it + j
                if live(it, j, 3):
                    dve.wait_ge(pv_full, t - 2)
                    dve.wait_ge(tr_out, t + 1)
                    if live(it, j, 5):
                        dve.wait_ge(wo_full, t - 4)
                    nc.vector.tensor_tensor(ot[:, (j - 3) % 2, :], pv_bank[:, 0:ROWS], turned[:, j % 2, 1, :], ALU.mult).then_inc(o_done, 1)
                for b in range(4):
                    if live(it, j, 0):
                        dve.wait_ge(s_full, 4 * t + b + 1)
                        if b == 0 and live(it, j, 2):
                            dve.wait_ge(p_exp, 4 * (t - 1))
                        nc.vector.tensor_reduce(low[:, j % 2, 2 * b:2 * b + 2],
                                                s_bank[b][0:ROWS, 0:2 * SRC].rearrange("p (h s) -> p h s", h=2),
                                                AX_X, ALU.max, negate=True).then_inc(s_low, 1)
                    if live(it, j, 1) and b < 3:
                        dve.wait_ge(t_full, 4 * (t - 1) + b + 1)
                        if b == 0 and live(it, j, 3):
                            dve.wait_ge(pv_full, t - 2)
                        nc.vector.tensor_copy(pt[:, (j - 1) % 2, 2 * b:2 * b + 2, :, :].rearrange("p h c r -> p (h c r)"),
                                              t_bank[b % 2][0:SHALF, 0:4 * ROWS]).then_inc(t_out, 1)
                    if live(it, j, 1) and b == 0:
                        dve.wait_ge(p_exp, 4 * t)
                        at_least(dve, tr, t + 1)
                        nc.vector.reciprocal(one_by[:, (j - 1) % 2, :], total[:, (j - 1) % 2, :]).then_inc(one_by_done, 1)
                        dve.wait_ge(one_by_done, t)
                        nc.vector.tensor_copy(inv[:, (j - 1) % 2, :].rearrange("p (h e) -> p h e", h=XH),
                                              bc(one_by[:, (j - 1) % 2, :].unsqueeze(2), [ROWS, XH, XE])).then_inc(inv_done, 1)
                    if live(it, j, 3) and b == 1:
                        dve.wait_ge(wo_full, t - 2)
                        nc.vector.tensor_tensor(k.h[:, bass.ds(t - 3, 1), :], m_bank[0:ROWS, 0:DIM].unsqueeze(1),
                                                k.h[:, bass.ds(t - 3, 1), :], ALU.add).then_inc(h_done, 1)
                    if b == 2:
                        make_rows(it, j)

            run(dve, slot)
            dve.wait_ge(h_done, TILES)

        @block.scalar
        def _(act):
            norm.scalar_part(act)
            act.wait_ge(w_in, 16 * LOADS)
            act.wait_ge(bias_done, 4)
            act.wait_ge(kv_full, 1)
            for h in range(XH):
                nc.scalar.activation(kT[:, h, :], s_bank[0][:, 0:SRC], ACT.Identity, bias=bk_own[:, h:h + 1],
                                     scale=own[:, h:h + 1]).then_inc(kv_out, 1)

            def exps(it, j, b):
                t = 4 * it + j
                if live(it, j, 0):
                    if b == 0 and live(it, j, 2):
                        act.wait_ge(t_full, 4 * (t - 1))
                        act.wait_ge(inv_done, t - 1)
                    act.wait_ge(s_low, 4 * t + b + 1)
                    for n in range(2):
                        h = 2 * b + n
                        ins = nc.scalar.activation(prob[:, j % 2, h, :], s_bank[b][0:ROWS, n * SRC:(n + 1) * SRC], ACT.Exp,
                                                   bias=low[:, j % 2, h:h + 1], accum_out=total[:, j % 2, h:h + 1])
                    ins.then_inc(p_exp, 1)

            def slot(it, j):
                t = 4 * it + j
                if q_turn(it, j):
                    act.wait_ge(q_full, t + 2)
                    at_least(act, s_full, 4 * t)
                    nc.scalar.activation(qT[:, (j + 1) % 2, :], m_bank[:, 0:ROWS], ACT.Identity, bias=bq[:, 0:1],
                                         scale=XE ** -0.5).then_inc(q_out, 1)
                for b in range(3):
                    exps(it, j, b)
                if turn_live(it, j):
                    act.wait_ge(tr, t + 3)
                    if live(it, j, -2) and live(it, j, 1):
                        if live(it, j, 3):
                            act.wait_ge(o_done, t - 2)
                        at_least(act, q_full, t + 1)
                        ins = nc.scalar.activation(turned[:, j % 2, :, :].rearrange("p a r -> p (a r)"), m_bank[:, 0:2 * ROWS], ACT.Copy)
                    elif live(it, j, -2):
                        at_least(act, q_full, t + 1)
                        ins = nc.scalar.activation(turned[:, j % 2, 0, :], m_bank[:, 0:ROWS], ACT.Copy)
                    else:
                        act.wait_ge(o_done, t - 2)
                        ins = nc.scalar.activation(turned[:, j % 2, 1, :], m_bank[:, ROWS:2 * ROWS], ACT.Copy)
                    ins.then_inc(tr_out, 1)
                if live(it, j, 1):
                    if live(it, j, 3):
                        act.wait_ge(pv_full, t - 2)
                    act.wait_ge(t_full, 4 * (t - 1) + 4)
                    nc.scalar.activation(pt[:, (j - 1) % 2, 6:8, :, :].rearrange("p h c r -> p (h c r)"),
                                         t_bank[1][0:SHALF, 0:4 * ROWS], ACT.Copy).then_inc(t_last, 1)
                exps(it, j, 3)

            run(act, slot)


EXPERTS, CLUSTERS, GRID = 64, 8, 16
PER_CLUSTER = EXPERTS // CLUSTERS
SLOT = 64
BLOCKS = (TOKENS + EXPERTS * (SLOT - 1)) // SLOT
SLOTS = BLOCKS * SLOT
LOAD = 8


def route_stage(nc, a, k):
    with Stage(nc) as ctx:
        sb = lambda n, s, d=F32: ctx.enter_context(nc.sbuf_tensor(n, s, d))
        sem = lambda n: ctx.semaphore("r_" + n)
        norm_x, norm_f = Norm(nc, ctx, "outer"), Norm(nc, ctx, "inner")
        gamma, beta, scale_row = sb("gamma", [ROWS, DIM]), sb("beta", [ROWS, DIM]), sb("scale_row", [ROWS, EXPERTS])
        tie = sb("tie", [ROWS, CLUSTERS + EXPERTS])
        tri, all_one, ident16 = sb("tri", [ROWS, ROWS], BF16), sb("all_one", [ROWS, BLOCKS], BF16), sb("ident16", [ROWS, ROWS], BF16)
        tri32, ident32, block_col = sb("tri32", [ROWS, ROWS]), sb("ident32", [ROWS, ROWS]), sb("block_col", [BLOCKS, 1])
        x5 = sb("x5", [ROWS, TILES, DIM])
        sgn = sb("sgn", [ROWS, TILES, DIM], BF16)
        sgT = sb("sgT", [DIM, TILES, ROWS], BF16)
        sums, csum = sb("sums", [DIM, EXPERTS]), sb("csum", [DIM, CLUSTERS])
        sneg, cneg = sb("sneg", [DIM, EXPERTS]), sb("cneg", [DIM, CLUSTERS])
        sig = sb("sig", [DIM, CLUSTERS + EXPERTS], BF16)
        keys = sb("keys", [ROWS, TILES, CLUSTERS + EXPERTS])
        cmax, tmax = sb("cmax", [ROWS, TILES]), sb("tmax", [ROWS, TILES])
        pen = sb("pen", [ROWS, TILES, CLUSTERS])
        tkey = sb("tkey", [ROWS, TILES, EXPERTS])
        oh = sb("oh", [ROWS, TILES, 2, EXPERTS], BF16)
        cum = sb("cum", [ROWS, TILES + 1, EXPERTS], BF16)
        count_i, nb_i = sb("count_i", [BLOCKS, EXPERTS], I32), sb("nb_i", [BLOCKS, EXPERTS], I32)
        nb, upto, start = sb("nb", [BLOCKS, EXPERTS]), sb("upto", [BLOCKS, EXPERTS]), sb("start", [BLOCKS, EXPERTS])
        one_row = sb("one_row", [BLOCKS, EXPERTS])
        owner, owner_i = sb("owner", [BLOCKS, 1]), sb("owner_i", [BLOCKS, 1], I32)
        posf = sb("posf", [ROWS, TILES])
        names = ("w_in", "link", "x_done", "f_done", "sgn_done", "sT", "sT_out", "sig_done", "sc_full", "key_done", "oh_done",
                 "cum_done", "pre_full", "oT", "oT_out", "owner_done", "owner_out", "owner_in", "pos_done", "scattered", "consts")
        (w_in, chain, x_done, f_done, sgn_done, sT, sT_out, sig_done, sc_full, key_done, oh_done, cum_done, pre_full, oT,
         oT_out, owner_done, owner_out, owner_in, pos_done, scattered, consts) = (sem(n) for n in names)
        block = ctx.enter_context(nc.Block())
        tb = [k.banks[6][:].bitcast(BF16), k.banks[7][:].bitcast(BF16)]
        LOADS = 7

        @block.sync
        def _(sp):
            for dst, name, p in ((gamma, "gamma", ROWS), (beta, "beta", ROWS), (scale_row, "scale", ROWS), (tie, "tie", ROWS)):
                sp.dma_start(dst[:], a[name].partition_broadcast(p)).then_inc(w_in, 16)
            for dst, name in ((tri32, "tri"), (ident32, "ident98"), (block_col, "block_col")):
                sp.dma_start(dst[:], a[name]).then_inc(w_in, 16)
            sp.wait_ge(owner_done, 1)
            sp.dma_start(k.owner_dram, owner_i[:]).then_inc(owner_out, 16)
            sp.wait_ge(owner_out, 16)
            sp.dma_start(k.owner_row[:], k.owner_dram.rearrange("b o -> o b")).then_inc(owner_in, 16)
            sp.wait_ge(owner_in, 16)

        @block.vector
        def _(dve):
            n = [0]

            def link(ins):
                n[0] += 1
                ins.then_inc(chain, 1)
                dve.wait_ge(chain, n[0])

            def sign(out, x, below, done=None):
                link(nc.vector.tensor_scalar(below, x, 0.0, None, ALU.is_lt))
                return nc.vector.scalar_tensor_tensor(out, x, 0.0, below, ALU.is_gt, ALU.subtract)

            link(nc.vector.tensor_reduce(sums[:], k.wd[:].rearrange("p (e h) -> p e h", e=EXPERTS), AX_X, ALU.add))
            link(sign(sig[:, CLUSTERS:], sums[:], sneg[:]))
            link(nc.vector.tensor_reduce(csum[:], sig[:, CLUSTERS:].rearrange("p (c t) -> p c t", c=CLUSTERS), AX_X, ALU.add))
            sign(sig[:, 0:CLUSTERS], csum[:], cneg[:]).then_inc(sig_done, 1)
            link(nc.vector.memset(all_one[:], 1.0))
            link(nc.vector.memset(one_row[:], 1.0))
            link(nc.vector.memset(cum[:, 0, :], 0.0))
            norm_x.vector_part(dve, k.h)
            dve.wait_ge(w_in, 16 * LOADS)
            link(nc.vector.tensor_copy(tri[:], tri32[:]))
            nc.vector.tensor_copy(ident16[:], ident32[:]).then_inc(consts, 1)

            def outer(it):
                for t in range(4):
                    tile = 4 * it + t
                    nc.vector.tensor_scalar(x5[:, tile, :], k.h[:, tile, :], norm_x.mean[:, bass.ds(tile, 1)],
                                            norm_x.rstd[:, bass.ds(tile, 1)], ALU.subtract, ALU.mult).then_inc(x_done, 1)

            def inner(it):
                for t in range(4):
                    tile = 4 * it + t
                    nc.vector.tensor_scalar(k.xf[:, tile, :], x5[:, tile, :], norm_f.mean[:, bass.ds(tile, 1)],
                                            norm_f.rstd[:, bass.ds(tile, 1)], ALU.subtract, ALU.mult).then_inc(f_done, 1)

            with dve.Fori(0, TILES // 4) as it:
                outer(it)
            dve.wait_ge(x_done, TILES)
            norm_f.vector_part(dve, x5)
            with dve.Fori(0, TILES // 4) as it:
                inner(it)
            dve.wait_ge(f_done, TILES)
            wide = [ROWS, TILES, DIM]
            link(nc.vector.tensor_tensor(k.xf[:], k.xf[:], bc(gamma[:].unsqueeze(1), wide), ALU.mult))
            link(nc.vector.tensor_tensor(k.xf[:], k.xf[:], bc(beta[:].unsqueeze(1), wide), ALU.add))
            sign(sgn[:], k.xf[:], tkey[:].rearrange("p t e -> p (t e)").bitcast(BF16)).then_inc(sgn_done, 1)
            dve.wait_ge(sgn_done, 1)
            link(nc.vector.tensor_tensor(k.h[:], k.h[:], x5[:], ALU.add))
            for g in range(TILES // 4):
                dve.wait_ge(sc_full, g + 1)
                nc.vector.scalar_tensor_tensor(keys[:, 4 * g:4 * g + 4, :],
                                               k.banks[g % 4][0:ROWS, 0:4 * 72].rearrange("p (t e) -> p t e", t=4), 16.0,
                                               bc(tie[:].unsqueeze(1), [ROWS, 4, 72]), ALU.mult, ALU.add).then_inc(key_done, 1)
            dve.wait_ge(key_done, TILES // 4)
            ck = keys[:, :, 0:CLUSTERS]
            link(nc.vector.tensor_reduce(cmax[:], ck, AX_X, ALU.max))
            link(nc.vector.tensor_tensor(pen[:], ck, bc(cmax[:].unsqueeze(2), [ROWS, TILES, CLUSTERS]), ALU.is_equal))
            link(nc.vector.tensor_scalar(pen[:], pen[:], -1.0, 1e5, ALU.add, ALU.mult))
            link(nc.vector.tensor_tensor(tkey[:].rearrange("p t (c j) -> p t c j", c=CLUSTERS),
                                         keys[:, :, CLUSTERS:].rearrange("p t (c j) -> p t c j", c=CLUSTERS),
                                         bc(pen[:].unsqueeze(3), [ROWS, TILES, CLUSTERS, PER_CLUSTER]), ALU.add))
            link(nc.vector.tensor_reduce(tmax[:], tkey[:], AX_X, ALU.max))
            for half in range(2):
                ins = nc.vector.tensor_tensor(oh[:, :, half, :], tkey[:], bc(tmax[:].unsqueeze(2), [ROWS, TILES, EXPERTS]), ALU.is_equal)
                ins.then_inc(oh_done, 1)
            dve.wait_ge(oh_done, 2)
            for t in range(TILES):
                link(nc.vector.tensor_tensor(cum[:, t + 1, :], cum[:, t, :], oh[:, t, 0, :], ALU.add))
            nc.vector.tensor_copy(one_row[:], one_row[:]).then_inc(cum_done, 1)
            dve.wait_ge(pre_full, 1)
            link(nc.vector.tensor_scalar(count_i[:], k.banks[4][0:BLOCKS, 0:EXPERTS], float(SLOT - 1), None, ALU.add))
            link(nc.vector.tensor_scalar(nb_i[:], count_i[:], SLOT.bit_length() - 1, None, ALU.arith_shift_right))
            link(nc.vector.tensor_copy(nb[:], nb_i[:]))
            link(nc.vector.tensor_tensor_scan(upto[:], one_row[:], nb[:], 0.0, ALU.mult, ALU.add))
            link(nc.vector.tensor_tensor(start[:], upto[:], nb[:], ALU.subtract))
            link(nc.vector.tensor_scalar(start[:], start[:], float(SLOT), None, ALU.mult))
            link(nc.vector.tensor_scalar(nb[:], upto[:], block_col[:, 0:1], None, ALU.is_le))
            link(nc.vector.tensor_reduce(owner[:], nb[:], AX_X, ALU.add))
            nc.vector.tensor_scalar(owner_i[:], owner[:], float(EXPERTS - 1), None, ALU.min).then_inc(owner_done, 1)
            for g in range(4):
                link(nc.vector.tensor_tensor(tkey[:, 8 * g:8 * g + 8, :], k.banks[g][0:ROWS, :].rearrange("p (t e) -> p t e", t=8),
                                             bc(start[0:ROWS, :].unsqueeze(1), [ROWS, 8, EXPERTS]), ALU.add))
            link(nc.vector.tensor_tensor(tkey[:], tkey[:], oh[:, :, 0, :], ALU.mult))
            link(nc.vector.tensor_reduce(posf[:], tkey[:], AX_X, ALU.add))
            nc.vector.tensor_copy(k.pos[:], posf[:]).then_inc(pos_done, 1)
            link(nc.vector.tensor_tensor(x5[:, :, 0:EXPERTS], oh[:, :, 0, :], bc(scale_row[:].unsqueeze(1), [ROWS, TILES, EXPERTS]), ALU.mult))
            link(nc.vector.tensor_reduce(k.scale[:], x5[:, :, 0:EXPERTS], AX_X, ALU.add))

        @block.scalar
        def _(act):
            norm_x.scalar_part(act)
            norm_f.scalar_part(act)
            for g in range(TILES // 4):
                act.wait_ge(sT, g + 1)
                nc.scalar.activation(sgT[:, 4 * g:4 * g + 4, :], tb[g % 2][:, 0:4 * ROWS].rearrange("p (t r) -> p t r", t=4),
                                     ACT.Copy).then_inc(sT_out, 1)
            for g in range(TILES // 4):
                act.wait_ge(oT, g + 1)
                nc.scalar.activation(k.ohT[:, 4 * g:4 * g + 4, :], tb[g % 2][:, 0:4 * ROWS].rearrange("p (t r) -> p t r", t=4),
                                     ACT.Copy).then_inc(oT_out, 1)

        def score(pe, g):
            pe.wait_ge(sT_out, g + 1)
            if g >= 4:
                pe.wait_ge(key_done, g - 3)
            for t in range(4):
                mm = nc.tensor.matmul(k.banks[g % 4][0:ROWS, 72 * t:72 * t + 72], sgT[:, 4 * g + t, :], sig[:], start=True, stop=True)
            mm.then_inc(sc_full, 1)

        @block.tensor
        def _(pe):
            pe.wait_ge(sgn_done, 1)
            pe.wait_ge(consts, 1)
            pe.wait_ge(sig_done, 1)
            for g in range(TILES // 4):
                if g >= 2:
                    pe.wait_ge(sT_out, g - 1)
                for t in range(4):
                    mm = nc.tensor.transpose(tb[g % 2][:, t * ROWS:(t + 1) * ROWS], sgn[:, 4 * g + t, :], ident16[:])
                mm.then_inc(sT, 1)
                if g >= 1:
                    score(pe, g - 1)
            score(pe, TILES // 4 - 1)
            pe.wait_ge(cum_done, 1)
            for g in range(4):
                nc.tensor.matmul(k.banks[g][0:ROWS, :], tri[:], oh[:, 8 * g:8 * g + 8, 0, :], start=True, stop=False)
                nc.tensor.matmul(k.banks[g][0:ROWS, :], all_one[:, 0:ROWS], cum[:, 8 * g:8 * g + 8, :], start=False, stop=True)
            nc.tensor.matmul(k.banks[4][0:BLOCKS, 0:EXPERTS], all_one[:], cum[:, TILES, :], start=True, stop=True).then_inc(pre_full, 1)
            pe.wait_ge(sT_out, TILES // 4)
            for g in range(TILES // 4):
                if g >= 2:
                    pe.wait_ge(oT_out, g - 1)
                for t in range(4):
                    mm = nc.tensor.transpose(tb[g % 2][:, t * ROWS:(t + 1) * ROWS], oh[:, 4 * g + t, :, :].rearrange("p a e -> p (a e)"),
                                             ident16[:])
                mm.then_inc(oT, 1)

        @block.gpsimd
        def _(pool):
            pool.wait_ge(pos_done, 1)
            for t in range(TILES):
                nc.gpsimd.indirect_dma_start(out=k.x_slots, out_offset=bass.IndirectOffsetOnAxis(ap=k.pos[:, t:t + 1], axis=0),
                                             in_=k.xf[:, t, :], in_offset=None).then_inc(scattered, 16)
            pool.wait_ge(scattered, 16 * TILES)


def expert_stage(nc, k, name, weights, src, dst):
    with Stage(nc) as ctx:
        sb = lambda n, s, d=F32: ctx.enter_context(nc.sbuf_tensor(f"{name}_{n}", s, d))
        sem = lambda n: ctx.semaphore(f"{name}_{n}")
        rows, out = sb("rows", [SLOT, 2, LOAD, DIM]), sb("out", [SLOT, 2, LOAD, DIM])
        xt = sb("xt", [DIM, 2, 4 * SLOT])
        rows_in, stored = [sem("rows_in0"), sem("rows_in1")], [sem("stored0"), sem("stored1")]
        t_full, t_out, y_full, y_out = sem("t_full"), sem("t_out"), sem("y_full"), sem("y_out")
        t_bank, y_bank = k.banks[0:2], k.banks[2:4]
        tally = sem("tally")
        STEPS = BLOCKS // LOAD // 2
        src_v = src.rearrange("(b s) d -> s b d", s=SLOT)
        dst_v = dst.rearrange("(b s) d -> s b d", s=SLOT)
        block = ctx.enter_context(nc.Block())

        @block.sync
        def _(sp):
            def body(it):
                for u in range(2):
                    at_least(sp, t_full, 4 * it + 2 * u - 2)
                    sp.dma_start(rows[:, u, :, :], src_v[:, bass.ds((2 * it + u) * LOAD, LOAD), :]).then_inc(rows_in[u], 16)
            peeled(sp, STEPS, body)

        @block.tensor
        def _(pe):
            def turn(it, v):
                u = v // 2
                if v % 2 == 0:
                    pe.wait_ge(rows_in[u], 16 * (it + 1))
                at_least(pe, t_out, 4 * it + v - 1)
                carry_waits(pe, tally)
                for b in range(4):
                    mm = nc.tensor.transpose(t_bank[v % 2][:, b * SLOT:(b + 1) * SLOT], rows[:, u, 4 * (v % 2) + b, :],
                                             k.ident[0:SLOT, 0:SLOT])
                mm.then_inc(t_full, 1)

            def owners_of(it, u):
                return nc.values_load_multi_w_load_instructions(k.owner_row[0:1, bass.ds(2 * LOAD * it + LOAD * u, LOAD)],
                                                                engines=[mybir.EngineType.PE], min_val=0, max_val=EXPERTS - 1)[1]

            def product(it, v, owners):
                pe.wait_ge(t_out, 4 * it + v + 1)
                at_least(pe, y_out, 4 * it + v - 1)
                for b, e in enumerate(owners):
                    mm = nc.tensor.matmul(y_bank[v % 2][0:SLOT, b * DIM:(b + 1) * DIM], xt[:, v % 2, b * SLOT:(b + 1) * SLOT],
                                          weights[:, bass.ds(e * DIM, DIM)], start=True, stop=True)
                mm.then_inc(y_full, 1)

            def body(it):
                turn(it, 0)
                for v in range(4):
                    if v % 2 == 0:
                        owners = owners_of(it, v // 2)
                    if v < 3:
                        turn(it, v + 1)
                    product(it, v, owners[4 * (v % 2):4 * (v % 2) + 4])

            peeled(pe, STEPS, body)

        @block.vector
        def _(dve):
            def body(it):
                for v in range(4):
                    dve.wait_ge(t_full, 4 * it + v + 1)
                    at_least(dve, y_full, 4 * it + v - 1)
                    nc.vector.tensor_copy(xt[:, v % 2, :], t_bank[v % 2][:, 0:4 * SLOT]).then_inc(t_out, 1)
            peeled(dve, STEPS, body)

        @block.scalar
        def _(act):
            def body(it):
                for v in range(4):
                    act.wait_ge(y_full, 4 * it + v + 1)
                    if v % 2 == 0:
                        at_least(act, stored[v // 2], 16 * it)
                    nc.scalar.activation(out[:, v // 2, 4 * (v % 2):4 * (v % 2) + 4, :].rearrange("p b d -> p (b d)"),
                                         y_bank[v % 2][0:SLOT, :], ACT.Copy).then_inc(y_out, 1)
                    if v % 2 == 1:
                        act.wait_ge(y_out, 4 * it + v + 1)
                        act.dma_start(dst_v[:, bass.ds((2 * it + v // 2) * LOAD, LOAD), :], out[:, v // 2, :, :]).then_inc(stored[v // 2], 16)
            peeled(act, STEPS, body)
            for u in range(2):
                act.wait_ge(stored[u], 16 * STEPS)


def spline_stage(nc, a, k):
    with Stage(nc) as ctx:
        sb = lambda n, s, d=F32: ctx.enter_context(nc.sbuf_tensor(n, s, d))
        sem = lambda n: ctx.semaphore("s_" + n)
        edge = sb("edge", [ROWS, GRID])
        below = sb("below", [ROWS, 2, GRID, 2, DIM], BF16)
        line = sb("line", [ROWS, 2, 2, 2, DIM])
        hn = sb("hn", [ROWS, TILES, DIM])
        slope_u = sb("slope_u", [ROWS, 2, 2, DIM])
        gathered = [sem(f"gathered{i}") for i in range(4)]
        edge_in, sig_done, mask_done, tab_full, pick, mul_done, hs_done, scattered = (
            sem(n) for n in ("edge_in", "sig_done", "mask_done", "tab_full", "pick", "mul_done", "hs_done", "scattered"))
        PAIRS = TILES // 2
        tally = sem("tally")
        block = ctx.enter_context(nc.Block())

        @block.sync
        def _(sp):
            sp.dma_start(edge[:], a["edge"].partition_broadcast(ROWS)).then_inc(edge_in, 16)

        @block.gpsimd
        def _(pool):
            for t in range(TILES):
                nc.gpsimd.indirect_dma_start(out=k.xf[:, t, :], out_offset=None, in_=k.y_slots,
                                             in_offset=bass.IndirectOffsetOnAxis(ap=k.pos[:, t:t + 1], axis=0)).then_inc(gathered[t // 8], 16)
            for t in range(TILES):
                pool.wait_ge(hs_done, t + 1)
                nc.gpsimd.indirect_dma_start(out=k.x_slots, out_offset=bass.IndirectOffsetOnAxis(ap=k.pos[:, t:t + 1], axis=0),
                                             in_=k.xf[:, t, :], in_offset=None).then_inc(scattered, 16)
            pool.wait_ge(scattered, 16 * TILES)

        @block.scalar
        def _(act):
            act.wait_ge(edge_in, 16)

            def sigmoid(q):
                act.wait_ge(gathered[q], 16 * 8)
                nc.scalar.activation(hn[:, 8 * q:8 * q + 8, :], k.xf[:, 8 * q:8 * q + 8, :], ACT.Sigmoid).then_inc(sig_done, 1)
                act.wait_ge(sig_done, q + 1)

            def body(it):
                for v in range(2):
                    at_least(act, pick, 32 * (2 * it + v - 1))
                    for i in range(1, GRID):
                        ins = nc.scalar.activation(below[:, v, i, :, :], hn[:, bass.ds(4 * it + 2 * v, 2), :], ACT.Relu,
                                                   bias=edge[:, i:i + 1], scale=-float(GRID))
                    ins.then_inc(mask_done, 1)
            sigmoid(0)
            body(0)
            body(1)
            for q in range(1, 4):
                sigmoid(q)
                with act.Fori(2 * q, 2 * q + 2) as it:
                    body(it)

        @block.tensor
        def _(pe):
            def body(it):
                for v in range(2):
                    for p in range(8):
                        for t in range(2):
                            n = (2 * p + t) % 8
                            at_least(pe, pick, 32 * (2 * it + v) + 4 * (p - 4) + 3 + t)
                            lhs = k.ohT[:, bass.ds(4 * it + 2 * v + t, 1), :].rearrange("p a r -> p (a r)")
                            nc.tensor.matmul(k.banks[n][0:ROWS, :], lhs, k.lines_hi[:, 512 * p:512 * (p + 1)], start=True, stop=False)
                            nc.tensor.matmul(k.banks[n][0:ROWS, :], lhs, k.lines_lo[:, 512 * p:512 * (p + 1)], start=False, stop=True).then_inc(tab_full, 1)
            peeled(pe, PAIRS // 2, body)

        @block.vector
        def _(dve):
            def body(it):
                for v in range(2):
                    base = 32 * (2 * it + v)
                    dve.wait_ge(mask_done, 2 * it + v + 1)
                    for p in range(8):
                        for n in range(2):
                            i = 2 * p + n
                            for t in range(2):
                                src = k.banks[(2 * p + t) % 8][0:ROWS, 256 * n:256 * n + 256].rearrange("p (c d) -> p c d", c=2)
                                if n == 0:
                                    dve.wait_ge(tab_full, 16 * (2 * it + v) + 2 * p + t + 1)
                                if i == 0:
                                    at_least(dve, hs_done, 2 * (2 * it + v) - 2)
                                    ins = nc.vector.tensor_copy(line[:, v, t, :, :], src)
                                else:
                                    dve.wait_ge(pick, base + 2 * i + t - 1)
                                    carry_waits(dve, tally)
                                    ins = nc.vector.copy_predicated(line[:, v, t, :, :],
                                                                    bc(below[:, v, i, t, :].bitcast(U16).unsqueeze(1), [ROWS, 2, DIM]), src)
                                ins.then_inc(pick, 1)
                    dve.wait_ge(pick, base + 32)
                    tile = 4 * it + 2 * v
                    nc.vector.scalar_tensor_tensor(slope_u[:, v, :, :], hn[:, bass.ds(tile, 2), :], float(GRID), line[:, v, :, 1, :],
                                                   ALU.mult, ALU.mult).then_inc(mul_done, 1)
                    dve.wait_ge(mul_done, 2 * it + v + 1)
                    for t in range(2):
                        nc.vector.tensor_tensor(k.xf[:, bass.ds(tile + t, 1), :], slope_u[:, v, t, :].unsqueeze(1), line[:, v, t, 0, :].unsqueeze(1),
                                                ALU.add).then_inc(hs_done, 1)
            peeled(dve, PAIRS // 2, body)


def final_stage(nc, k, out):
    with Stage(nc) as ctx:
        sem = lambda n: ctx.semaphore("f_" + n)
        gathered = [sem(f"gathered{i}") for i in range(8)]
        done, stored = sem("done"), sem("stored")
        out_v = out.rearrange("b q d -> (b q) d").rearrange("(t r) d -> r t d", r=ROWS)
        block = ctx.enter_context(nc.Block())

        @block.gpsimd
        def _(pool):
            for t in range(TILES):
                nc.gpsimd.indirect_dma_start(out=k.xf[:, t, :], out_offset=None, in_=k.y_slots,
                                             in_offset=bass.IndirectOffsetOnAxis(ap=k.pos[:, t:t + 1], axis=0)).then_inc(gathered[t // 4], 16)

        @block.vector
        def _(dve):
            for g in range(8):
                dve.wait_ge(gathered[g], 16 * 4)
                for t in range(4 * g, 4 * g + 4):
                    ins = nc.vector.scalar_tensor_tensor(k.h[:, t, :], k.xf[:, t, :], k.scale[:, t:t + 1], k.h[:, t, :], ALU.mult, ALU.add)
                    ins.then_inc(done, 1)

        @block.sync
        def _(sp):
            for g in range(8):
                sp.wait_ge(done, 4 * g + 4)
                sp.dma_start(out_v[:, 4 * g:4 * g + 4, :], k.h[:, 4 * g:4 * g + 4, :]).then_inc(stored, 16)
            sp.wait_ge(stored, 16 * 8)


class Store:
    pass


def tower_program(nc, a, out, stop=None, dbg=None):
    with ExitStack() as ctx:
        sb = lambda n, s, d=F32: ctx.enter_context(nc.sbuf_tensor(n, s, d))
        k = Store()
        k.banks = [ctx.enter_context(nc.psum_tensor(f"bank{i}", [128, 512], F32)) for i in range(8)]
        k.ident = sb("ident", [128, 128])
        k.h = sb("h", [ROWS, TILES, DIM])
        k.bias_dram = nc.dram_tensor("bias_dram", (HEADS, QUERIES * KEYS), F32, kind="Internal").ap()
        k.three = sb("three", [128, 1])
        with ExitStack() as first:
            sb1 = lambda n, s, d=F32: first.enter_context(nc.sbuf_tensor(n, s, d))
            k.mh = sb1("mh", [AUG, HEADS, AUG])
            k.wv = sb1("wv", [AUG, HEADS, VD])
            k.pw = sb1("pw", [128, 6, DIM])
            k.prow = sb1("prow", [128, DIM])
            k.bias = sb1("bias", [CH, CHUNKS, KEYS])
            k.xT = sb1("xT", [AUG, 2, GROUP * KEYS])
            k.xn = sb1("xn", [KHALF, 2, GROUP, 2, AUG])
            setup_stage(nc, a, k, ctx)
            token_stage(nc, a, k)
        if stop == "token":
            return dump(nc, k.h, dbg)
        band_stage(nc, a, k)
        if stop == "band":
            return dump(nc, k.h, dbg)
        k.wd = sb("wd", [DIM, EXPERTS * DIM])
        k.wu = sb("wu", [DIM, EXPERTS * DIM])
        k.lines_hi, k.lines_lo = sb("lines_hi", [128, 4096], BF16), sb("lines_lo", [128, 4096], BF16)
        k.x_slots = nc.dram_tensor("x_slots", (SLOTS, DIM), F32, kind="Internal").ap()
        k.y_slots = nc.dram_tensor("y_slots", (SLOTS, DIM), F32, kind="Internal").ap()
        k.owner_dram = nc.dram_tensor("owner_dram", (BLOCKS, 1), I32, kind="Internal").ap()
        cross_stage(nc, a, k)
        if stop == "cross":
            return dump(nc, k.h, dbg)
        k.owner_row = sb("owner_row", [1, BLOCKS], I32)
        k.pos = sb("pos", [ROWS, TILES], I32)
        k.scale = sb("scale", [ROWS, TILES])
        k.ohT = sb("ohT", [128, TILES, ROWS], BF16)
        k.xf = sb("xf", [ROWS, TILES, DIM])
        route_stage(nc, a, k)
        if stop == "route":
            return dump(nc, k.xf, dbg)
        expert_stage(nc, k, "down", k.wd[:], k.x_slots, k.y_slots)
        spline_stage(nc, a, k)
        if stop == "spline":
            return dump(nc, k.xf, dbg)
        expert_stage(nc, k, "up", k.wu[:], k.x_slots, k.y_slots)
        final_stage(nc, k, out)


def dump(nc, buf, dbg):
    with nc.semaphore("dumped") as dumped, nc.Block() as block:
        @block.sync
        def _(sp):
            sp.dma_start(dbg, buf[:]).then_inc(dumped, 16)
            sp.wait_ge(dumped, 16)


def layouts(i):
    import numpy as np
    f = {n: np.asarray(v) for n, v in i.items()}
    x = f["x"]
    kvw = f["L0_tok_kv_w"].reshape(HEADS, KD + VD, DIM_IN)
    kv_bn = np.stack([f[f"L0_tok_kv_{c}"] for c in "gbmv"]).reshape(4, HEADS, KD + VD)
    o = {
        "xT": x.transpose(2, 0, 1).reshape(DIM_IN, BATCH * KEYS),
        "xn": x.reshape(BATCH, 2, KHALF, DIM_IN).transpose(2, 0, 1, 3).reshape(KHALF, BATCH * 2, DIM_IN),
        "q_w": f["L0_tok_q_w"].reshape(HEADS, KD, DIM_IN).transpose(1, 0, 2),
        "k_w": kvw[:, :KD].transpose(1, 0, 2),
        "v_w": kvw[:, KD:].transpose(1, 0, 2),
        "q_bn": np.stack([f[f"L0_tok_q_{c}"] for c in "gbmv"]).reshape(4, HEADS, KD).transpose(2, 0, 1),
        "k_bn": kv_bn[:, :, :KD].transpose(2, 0, 1),
        "v_bn": kv_bn[:, :, KD:].transpose(2, 0, 1),
        "proj_w": f["L0_tok_proj_w"].T.reshape(6, 128, DIM).transpose(1, 0, 2),
        "proj_bn": np.stack([f[f"L0_tok_proj_{c}"] for c in "gbmv"]),
        "bias_t": f["L0_tok_attention_biases"].T.reshape(2, KHALF, HEADS).transpose(1, 0, 2),
        "bias_idx": f["L0_tok_bias_idxs"].reshape(-1),
        "off_col": (np.arange(KHALF)[:, None] + KHALF * np.arange(2)[None, :]).astype(np.float32),
        "ident": np.eye(128, dtype=np.float32),
    }
    half = np.arange(DIM // 2, dtype=np.float32)
    theta = np.float32(10000.0) ** (np.float32(-2.0) * (half - np.float32(1.0)) / np.float32(DIM))
    angle = np.arange(QUERIES, dtype=np.float32)[:, None] * theta[None, :]
    cos, sin = np.repeat(np.cos(angle).T, 2, axis=0), np.repeat(np.sin(angle).T, 2, axis=0)
    sin[1::2] *= -1.0
    swap = np.arange(DIM) ^ 1
    q, kk = np.arange(ROWS)[:, None], np.arange(ROWS)[None, :]
    wq, wk = f["L0_attn_W_q"], f["L0_attn_W_k"]
    o |= {
        "band_w": np.stack([wq, wq[:, swap], wk, wk[:, swap]], axis=1),
        "u_v": f["L0_attn_u_v"],
        "v_v": f["L0_attn_v_v"].reshape(DIM),
        "trig": np.stack([cos, sin], axis=1).astype(np.float32),
        "band_mask": np.where((kk <= q) & (kk // QUERIES == q // QUERIES), 0.0, -1e30).astype(np.float32),
    }

    g = lambda n: f["L1_attn_" + n]
    o |= {
        "srcT": g("source_embedding").T.reshape(LCH, 128, SRC).transpose(1, 0, 2),
        "valT": g("value_embedding").T.reshape(LCH, 128, SRC).transpose(1, 0, 2),
        "x_wk": g("Wk").reshape(LCH, 128, DIM).transpose(1, 0, 2),
        "x_wv": g("Wv").reshape(LCH, 128, DIM).transpose(1, 0, 2),
        "x_wq": g("Wq"),
        "x_wo": g("Wo"),
        "x_bq": g("bq")[:, None],
        "x_bk": g("bk")[:, None],
        "own": (np.arange(DIM)[:, None] // XE == np.arange(XH)[None, :]).astype(np.float32),
        "x_bv": g("bv"),
        "x_bo": g("bo")[None],
    }
    g = lambda n: f["L1_ffn_" + n]
    cells = np.arange(GRID - 1, -1, -1)
    lines = np.stack([g("spline_bases"), g("spline_slopes")], axis=3)[:, :, cells]
    lines = lines.transpose(0, 2, 3, 1).reshape(EXPERTS, 4096)
    o |= {
        "gamma": g("gamma"), "beta": g("beta"), "scale": g("scale"),
        "wd": g("Wd").transpose(2, 0, 1).reshape(DIM, EXPERTS * DIM),
        "wu": g("Wu").transpose(2, 0, 1).reshape(DIM, EXPERTS * DIM),
        "spline": np.concatenate([lines, lines]),
        "cell": cells.astype(np.float32),
        "edge": (GRID - np.arange(GRID)).astype(np.float32),
        "tie": -np.concatenate([np.arange(CLUSTERS), np.arange(EXPERTS) % PER_CLUSTER]).astype(np.float32),
        "tri": np.triu(np.ones((ROWS, ROWS), np.float32), 1),
        "ident98": np.eye(ROWS, dtype=np.float32),
        "block_col": np.arange(BLOCKS, dtype=np.float32)[:, None],
    }
    return {n: np.ascontiguousarray(v) for n, v in o.items()}


def kernel(**inputs):
    import numpy as np
    import concourse.bacc as bacc
    from concourse.bass_utils import run_bass_kernel_spmd

    arrays = {f"in_{n}": v for n, v in layouts(inputs).items()}
    nc = bacc.Bacc("TRN2", target_bir_lowering=False, num_devices=1)
    a = {n[3:]: nc.dram_tensor(n, v.shape, mybir.dt.from_np(v.dtype), kind="ExternalInput").ap() for n, v in arrays.items()}
    out = nc.dram_tensor("out", (BATCH, QUERIES, DIM), F32, kind="ExternalOutput").ap()
    tower_program(nc, a, out)
    r = run_bass_kernel_spmd(nc, [arrays], core_ids=[0])
    return np.asarray(r.results[0]["out"])
```

```python
from contextlib import ExitStack

import concourse.bass as bass
from concourse import mybir

ALU = mybir.AluOpType
ACT = mybir.ActivationFunctionType
AX_X = mybir.AxisListType.X
F32 = mybir.dt.float32
BF16 = mybir.dt.bfloat16
I32 = mybir.dt.int32
U16 = mybir.dt.uint16
U32 = mybir.dt.uint32

EPS = 1e-5
BATCH, RES, RESQ, DIM_IN, DIM = 64, 14, 7, 96, 128
KEYS, QUERIES = RES * RES, RESQ * RESQ
HEADS, KD, VD = 12, 32, 64
AUG = DIM_IN + 1
TOKENS = BATCH * QUERIES
ROWS = 2 * QUERIES
TILES = TOKENS // ROWS
KHALF = KEYS // 2
GROUP = 4
GROUPS = BATCH // GROUP
GTOK = GROUP * QUERIES
HQ = HEADS * QUERIES
CH = 118
CHUNKS = 5
CHUNK_AT = [0, CH, 2 * CH, 3 * CH, HQ - CH]
PIECES = [(0, 1), (2, 3), (4,)]


def at_least(eng, sem, count):
    if isinstance(count, int) and count <= 0:
        return
    eng.wait_ge(sem, count)


def carry_waits(eng, tally):
    eng.sem_inc(tally, 1)


class Stage(ExitStack):

    def __init__(self, nc):
        super().__init__()
        self.nc, self.sems = nc, []

    def semaphore(self, name):
        self.sems.append(self.nc.alloc_semaphore(name))
        return self.sems[-1]

    def __exit__(self, *error):
        handled = super().__exit__(*error)
        if error[0] is None:
            self.nc.clear_and_free_semaphores(self.sems)
            self.nc.all_engine_barrier(sem_only=True)
        return handled


def bc(ap, shape):
    return ap.to_broadcast(shape)


def setup_stage(nc, a, k, outer):
    with Stage(nc) as ctx:
        sb = lambda n, s, d=F32: ctx.enter_context(nc.sbuf_tensor(n, s, d))
        sem = lambda n: ctx.semaphore(n)
        qw, kw = sb("qw", [KD, HEADS, DIM_IN]), sb("kw", [KD, HEADS, DIM_IN])
        vw = sb("vw", [VD, HEADS, DIM_IN])
        qp, kp, vp = sb("qp", [KD, 4, HEADS]), sb("kp", [KD, 4, HEADS]), sb("vp", [VD, 4, HEADS])
        pp = sb("pp", [128, 4, DIM])
        qaug, kaug, vaug = sb("qaug", [KD, HEADS, AUG]), sb("kaug", [KD, HEADS, AUG]), sb("vaug", [VD, HEADS, AUG])
        rt_q, rt_k, rt_v, rt_p = sb("rt_q", [KD, HEADS]), sb("rt_k", [KD, HEADS]), sb("rt_v", [VD, HEADS]), sb("rt_p", [128, DIM])
        sc_q, sc_k, sc_v, sc_p = sb("sc_q", [KD, HEADS]), sb("sc_k", [KD, HEADS]), sb("sc_v", [VD, HEADS]), sb("sc_p", [128, DIM])
        tm_q, tm_k, tm_v, tm_p = sb("tm_q", [KD, HEADS]), sb("tm_k", [KD, HEADS]), sb("tm_v", [VD, HEADS]), sb("tm_p", [128, DIM])
        PIECE = KEYS * QUERIES // 7
        STRIP = PIECE // 4
        idx = sb("idx", [KHALF, 2, PIECE], I32)
        onehot = sb("onehot", [KHALF, 2, 2, PIECE], BF16)
        ab, ab_rest = sb("ab", [KHALF, 2, HEADS]), sb("ab_rest", [KHALF, 2, 2, HEADS])
        ab_parts = sb("ab_parts", [KHALF, 3, 2, HEADS], BF16)
        off_col = sb("off_col", [KHALF, 2])
        brow = sb("brow", [HEADS, 2, PIECE])

        loaded, idx_in = sem("loaded"), [sem("idx_in0"), sem("idx_in1")]
        chain, root, ready, m_full, m_out = sem("chain"), sem("root"), sem("ready"), sem("m_full"), sem("m_out")
        hot, b_full, b_out, v_full, table_in = sem("hot"), sem("b_full"), sem("b_out"), sem("v_full"), sem("table_in")
        b_stored = [sem("b_stored0"), sem("b_stored1")]
        bank = k.banks
        idx_src = a["bias_idx"]
        sets = [(qw, qp, qaug, rt_q, sc_q, tm_q), (kw, kp, kaug, rt_k, sc_k, tm_k), (vw, vp, vaug, rt_v, sc_v, tm_v)]
        LOADS = 9
        bias_in, ab_split = sem("bias_in"), sem("ab_split")
        block = ctx.enter_context(nc.Block())

        @block.sync
        def _(sp):
            def load_idx(p):
                sp.dma_start(idx[:, p % 2, :], idx_src[p * PIECE:(p + 1) * PIECE].partition_broadcast(KHALF)).then_inc(idx_in[p % 2], 16)

            for dst, src in ((off_col, "off_col"), (ab, "bias_t")):
                sp.dma_start(dst[:], a[src]).then_inc(bias_in, 16)
            load_idx(0)
            load_idx(1)
            for dst, src in ((qp, "q_bn"), (kp, "k_bn"), (vp, "v_bn"), (qw, "q_w"), (kw, "k_w"), (vw, "v_w"),
                             (k.ident, "ident"), (k.pw, "proj_w")):
                sp.dma_start(dst[:], a[src]).then_inc(loaded, 16)
            sp.dma_start(pp[:], a["proj_bn"].partition_broadcast(128)).then_inc(loaded, 16)
            for p in range(9):
                if 2 <= p < 7:
                    sp.wait_ge(hot, 2 * (p - 1))
                    load_idx(p)
                if p >= 2:
                    sp.wait_ge(b_out, 4 * (p - 1))
                    sp.dma_start(k.bias_dram[:, (p - 2) * PIECE:(p - 1) * PIECE], brow[:, p % 2, :]).then_inc(b_stored[p % 2], 16)
            sp.wait_ge(b_stored[0], 16 * 4)
            sp.wait_ge(b_stored[1], 16 * 3)
            flat = k.bias_dram.rearrange("h (q n) -> (h q) n", n=KEYS)
            sp.dma_start(k.bias[:, 0:4, :], flat[0:4 * CH, :].rearrange("(c r) n -> r c n", c=4)).then_inc(table_in, 16)
            sp.dma_start(k.bias[:, 4, :], flat[HQ - CH:HQ, :]).then_inc(table_in, 16)
            sp.wait_ge(table_in, 32)

        @block.vector
        def _(dve):
            n = [0]

            def link(ins):
                n[0] += 1
                ins.then_inc(chain, 1)
                dve.wait_ge(chain, n[0])

            def one_hots(p):
                dve.wait_ge(idx_in[p % 2], 16 * (p // 2 + 1))
                if p >= 2:
                    dve.wait_ge(b_full, 4 * (p - 1))
                for c in range(2):
                    nc.vector.tensor_scalar(onehot[:, p % 2, c, :], idx[:, p % 2, :], off_col[:, c:c + 1], None,
                                            ALU.is_equal).then_inc(hot, 1)

            dve.wait_ge(bias_in, 32)
            link(nc.vector.tensor_copy(ab_parts[:, 0], ab[:]))
            link(nc.vector.tensor_tensor(ab_rest[:, 0], ab[:], ab_parts[:, 0], ALU.subtract))
            link(nc.vector.tensor_copy(ab_parts[:, 1], ab_rest[:, 0]))
            link(nc.vector.tensor_tensor(ab_rest[:, 1], ab_rest[:, 0], ab_parts[:, 1], ALU.subtract))
            nc.vector.tensor_copy(ab_parts[:, 2], ab_rest[:, 1]).then_inc(ab_split, 1)
            one_hots(0)
            one_hots(1)
            for u in range(2):
                nc.vector.memset(k.xT[DIM_IN:AUG, u, :], 1.0)
                nc.vector.memset(k.xn[:, u, :, :, DIM_IN:AUG], 1.0)
            nc.vector.memset(k.three[:], 3.0)
            dve.wait_ge(loaded, 16 * LOADS)
            for i, (w, p, aug, rt, sc, tm) in enumerate(sets):
                nc.vector.tensor_scalar(rt[:], p[:, 3, :], EPS, None, ALU.add).then_inc(ready, 1)
            nc.vector.tensor_scalar(rt_p[:], pp[:, 3, :], EPS, None, ALU.add).then_inc(ready, 1)
            dve.wait_ge(root, 4)
            for i, (w, p, aug, rt, sc, tm) in enumerate(sets):
                link(nc.vector.reciprocal(tm[:], rt[:]))
                link(nc.vector.tensor_tensor(sc[:], tm[:], p[:, 0, :], ALU.mult))
                link(nc.vector.tensor_tensor(tm[:], p[:, 2, :], sc[:], ALU.mult))
                link(nc.vector.tensor_tensor(aug[:, :, DIM_IN], p[:, 1, :], tm[:], ALU.subtract))
                link(nc.vector.tensor_tensor(aug[:, :, 0:DIM_IN], w[:], bc(sc[:].unsqueeze(2), list(w.shape)), ALU.mult))
            nc.vector.tensor_copy(tm_q[:], sc_q[:]).then_inc(ready, 1)
            one_hots(2)
            link(nc.vector.reciprocal(tm_p[:], rt_p[:]))
            link(nc.vector.tensor_tensor(sc_p[:], tm_p[:], pp[:, 0, :], ALU.mult))
            link(nc.vector.tensor_tensor(tm_p[:], pp[:, 2, :], sc_p[:], ALU.mult))
            link(nc.vector.tensor_tensor(k.prow[:], pp[:, 1, :], tm_p[:], ALU.subtract))
            link(nc.vector.tensor_scalar(sc_p[:], sc_p[:], 1.0 / 6.0, None, ALU.mult))
            link(nc.vector.tensor_tensor(k.pw[:], k.pw[:], bc(sc_p[:].unsqueeze(1), [128, 6, DIM]), ALU.mult))
            for j in range(3):
                dve.wait_ge(m_full, j + 1)
                nc.vector.tensor_copy(k.mh[:, 4 * j:4 * j + 4, :],
                                      bank[j][0:AUG, 0:4 * AUG].rearrange("p (h r) -> p h r", h=4))
            for j in range(2):
                dve.wait_ge(v_full, j + 1)
                nc.vector.tensor_copy(k.wv[:, 6 * j:6 * j + 6, :],
                                      bank[3 + j][0:AUG, 0:6 * VD].rearrange("p (h r) -> p h r", h=6))
            for p in range(3, 7):
                one_hots(p)

        @block.scalar
        def _(act):
            def store_rows(p):
                if p >= 2:
                    act.wait_ge(b_stored[p % 2], 16 * (p // 2))
                for t in range(4):
                    act.wait_ge(b_full, 4 * p + t + 1)
                    nc.scalar.activation(brow[:, p % 2, t * STRIP:(t + 1) * STRIP],
                                         bank[5 + (4 * p + t) % 3][0:HEADS, 0:STRIP], ACT.Copy).then_inc(b_out, 1)

            store_rows(0)
            act.wait_ge(ready, 4)
            for rt in (rt_q, rt_k, rt_v, rt_p):
                nc.scalar.activation(rt[:], rt[:], ACT.Sqrt).then_inc(root, 1)
            for p in range(1, 7):
                store_rows(p)

        @block.tensor
        def _(pe):
            def bias_piece(p):
                pe.wait_ge(hot, 2 * (p + 1))
                for t in range(4):
                    if 4 * p + t >= 3:
                        pe.wait_ge(b_out, 4 * p + t - 2)
                    for part in range(3):
                        for c in range(2):
                            mm = nc.tensor.matmul(bank[5 + (4 * p + t) % 3][0:HEADS, 0:STRIP], ab_parts[:, part, c, :],
                                                  onehot[:, p % 2, c, t * STRIP:(t + 1) * STRIP],
                                                  start=(part == 0 and c == 0), stop=(part == 2 and c == 1))
                    mm.then_inc(b_full, 1)

            pe.wait_ge(ab_split, 1)
            bias_piece(0)
            bias_piece(1)
            pe.wait_ge(ready, 5)
            for h in range(HEADS):
                mm = nc.tensor.matmul(bank[h // 4][0:AUG, (h % 4) * AUG:(h % 4 + 1) * AUG], qaug[:, h, :], kaug[:, h, :],
                                      start=True, stop=True)
                if h % 4 == 3:
                    mm.then_inc(m_full, 1)
            for h in range(HEADS):
                mm = nc.tensor.transpose(bank[3 + h // 6][0:AUG, (h % 6) * VD:(h % 6 + 1) * VD], vaug[:, h, :],
                                         k.ident[0:VD, 0:VD])
                if h % 6 == 5:
                    mm.then_inc(v_full, 1)
            for p in range(2, 7):
                bias_piece(p)


def token_stage(nc, a, k):
    with Stage(nc) as ctx:
        sb = lambda n, s, d=F32: ctx.enter_context(nc.sbuf_tensor(n, s, d))
        sem = lambda n: ctx.semaphore(n)
        qt = sb("qt", [AUG, 2, GROUP, HQ])
        sbias = sb("sbias", [CH, 2, CHUNKS, KEYS])
        prob = sb("prob", [CH, 2, CHUNKS, KEYS])
        low = sb("low", [CH, 2, CHUNKS])
        tally = sem("tally")
        total = sb("total", [CH, 2, CHUNKS])
        inv = sb("inv", [CH, 2, CHUNKS])
        pt = sb("pt", [KHALF, 2, 2, HQ])
        px = sb("px", [AUG, 2, HEADS, GTOK])
        shifted = sb("shifted", [128, 2, 2, GTOK])
        hs = sb("hs", [128, 2, 6, GTOK])
        xT_in, xn_in = [sem("xT_in0"), sem("xT_in1")], [sem("xn_in0"), sem("xn_in1")]
        s_full, s_max, p_exp, inv_done, p_norm = sem("s_full"), sem("s_max"), sem("p_exp"), sem("inv_done"), sem("p_norm")
        t_full, t_out, px_full, px_out = sem("t_full"), sem("t_out"), sem("px_full"), sem("px_out")
        q_full, q_out, o_full, o_relu, o_hs = sem("q_full"), sem("q_out"), sem("o_full"), sem("o_relu"), sem("o_hs")
        h_full, h_out, source_in = sem("h_full"), sem("h_out"), sem("source_in")
        s_bank, t_bank, px_bank, m_bank = k.banks[0:3], k.banks[3:5], k.banks[5:7], k.banks[7]
        BODY = 2 * GROUP
        STEPS = BATCH // BODY

        def run(eng, slot):
            slot_range = range(BODY)
            for j in slot_range:
                slot(0, j)
            with eng.Fori(1, STEPS - 1) as it:
                for j in slot_range:
                    slot(it, j)
            for it in (STEPS - 1, STEPS):
                for j in slot_range:
                    slot(it, j)
            slot(STEPS + 1, 0)

        def live(it, j, back, count=BATCH):
            return not isinstance(it, int) or 0 <= BODY * it + j - back < count

        def group_live(it, u, back):
            return not isinstance(it, int) or 0 <= 2 * it + u - back < GROUPS

        SHARED = [[("h", 0)], [("q", 0), ("q", 1), ("q", 2)], [("q", 3), ("q", 4), ("o", 0)], [("q", 5), ("o", 1), ("o", 2)]]
        BACK = {"q": -1, "h": 2, "o": 1}
        PER = {"q": 6, "h": 1, "o": 3}

        def shared_before(it, u, i, n):
            seen = {"q": 0, "h": 0, "o": 0}
            for ii in range(i + 1):
                for nn, (kind, _) in enumerate(SHARED[ii]):
                    if (ii, nn) < (i, n):
                        seen[kind] += 1
            out = {}
            for kind, c in seen.items():
                count = PER[kind] * (2 * it + u - BACK[kind]) + c
                if isinstance(it, int):
                    count = min(max(count, 0), PER[kind] * GROUPS)
                out[kind] = count
            return out

        order = [x for row in SHARED for x in row]

        @(block := ctx.enter_context(nc.Block())).sync
        def _(sp):
            def load_keys(g, u):
                sp.dma_start(k.xT[0:DIM_IN, u, :], a["xT"][:, bass.ds(g * GROUP * KEYS, GROUP * KEYS)]).then_inc(xT_in[u], 16)

            def load_rows(g, u):
                sp.dma_start(k.xn[:, u, :, :, 0:DIM_IN].rearrange("p b c i -> p (b c) i"),
                             a["xn"][:, bass.ds(g * GROUP * 2, GROUP * 2), :]).then_inc(xn_in[u], 16)

            for u in range(2):
                load_keys(u, u)
                load_rows(u, u)
            for dst, src in ((k.wk, "x_wk"), (k.srcT, "srcT"), (k.wv_x, "x_wv"), (k.valT, "valT"), (k.wq, "x_wq"), (k.wo, "x_wo"),
                             (k.bq, "x_bq"), (k.bk, "x_bk"), (k.own, "own")):
                sp.dma_start(dst[:], a[src]).then_inc(source_in, 16)
            sp.dma_start(k.bv[:], a["x_bv"].partition_broadcast(SHALF)).then_inc(source_in, 16)
            sp.dma_start(k.bo[:], a["x_bo"].partition_broadcast(ROWS)).then_inc(source_in, 16)
            with sp.Fori(0, STEPS - 1) as it:
                for u in range(2):
                    sp.wait_ge(s_full, 3 * (BODY * it + GROUP * (u + 1)))
                    load_keys(2 * it + 2 + u, u)
                    sp.wait_ge(px_full, 2 * (BODY * it + GROUP * (u + 1)))
                    load_rows(2 * it + 2 + u, u)
            sp.wait_ge(source_in, 16 * 11)

        def rolled(j):
            return j // GROUP, j % GROUP

        @block.tensor
        def _(pe):
            def shared(it, u, i, n, kind, m):
                if not group_live(it, u, BACK[kind]):
                    return
                done = {"q": q_out, "h": h_out, "o": o_hs}
                before = shared_before(it, u, i, n)
                if isinstance(it, int):
                    for name, c in before.items():
                        at_least(pe, done[name], c)
                else:
                    prev = order[order.index((kind, m)) - 1][0]
                    at_least(pe, done[prev], before[prev])
                par = (u - BACK[kind]) % 2
                if kind == "q":
                    if m == 0:
                        pe.wait_ge(xT_in[par], 16 * (it + (1 if u == 0 else 2)))
                    for hh in range(2):
                        src = k.xT[:, par, :].rearrange("p (b r s c t) -> p b r s c t", b=GROUP, r=RESQ, s=2, c=RESQ)[:, :, :, 0, :, 0]
                        mm = nc.tensor.matmul(m_bank[0:AUG, hh * GTOK:(hh + 1) * GTOK], k.mh[:, 2 * m + hh, :],
                                              src, start=True, stop=True)
                    mm.then_inc(q_full, 1)
                elif kind == "o":
                    if m == 0:
                        at_least(pe, px_out, 2 * GROUP * (2 * it + u))
                    for jj in range(2):
                        for hh in range(2):
                            mm = nc.tensor.matmul(m_bank[64 * hh:64 * hh + 64, jj * GTOK:(jj + 1) * GTOK],
                                                  k.wv[:, 4 * m + 2 * jj + hh, :], px[:, par, 4 * m + 2 * jj + hh, :],
                                                  start=True, stop=True)
                    mm.then_inc(o_full, 1)
                else:
                    at_least(pe, o_hs, 3 * (2 * it + u - 1))
                    for t in range(2):
                        for j in range(6):
                            mm = nc.tensor.matmul(m_bank[0:ROWS, t * DIM:(t + 1) * DIM],
                                                  hs[:, par, j, t * ROWS:(t + 1) * ROWS], k.pw[:, j, :],
                                                  start=(j == 0), stop=(j == 5))
                    mm.then_inc(h_full, 1)

            def slot(it, j):
                u, i = rolled(j)
                s = BODY * it + j
                if live(it, j, 0):
                    if i == 0:
                        at_least(pe, q_out, 6 * (2 * it + u + 1))
                    for p, chunks in enumerate(PIECES):
                        if live(it, j, 1):
                            pe.wait_ge(s_max, 5 * (s - 1) + chunks[-1] + 1)
                        for n, c in enumerate(chunks):
                            mm = nc.tensor.matmul(s_bank[p][0:CH, n * KEYS:(n + 1) * KEYS],
                                                  qt[:, u, i, CHUNK_AT[c]:CHUNK_AT[c] + CH],
                                                  k.xT[:, u, i * KEYS:(i + 1) * KEYS], start=True, stop=True)
                        mm.then_inc(s_full, 1)
                def turn_piece(p, chunks):
                    if not live(it, j, 1):
                        return
                    par = (j - 1) % 2
                    pe.wait_ge(p_norm, 3 * (s - 1) + p + 1)
                    at_least(pe, t_out, 3 * (s - 1) + p - 1)
                    for n, c in enumerate(chunks):
                        for kc in range(2):
                            mm = nc.tensor.transpose(
                                t_bank[(3 * (j - 1) + p) % 2][0:KHALF, (2 * n + kc) * CH:(2 * n + kc + 1) * CH],
                                prob[:, par, c, kc * KHALF:(kc + 1) * KHALF], k.ident[0:CH, 0:CH])
                    mm.then_inc(t_full, 1)

                def weigh(half):
                    if not live(it, j, 2):
                        return
                    bu, bi = rolled((j - 2) % BODY)
                    if half == 0:
                        if bi == 0:
                            pe.wait_ge(xn_in[bu], 16 * (it + 1))
                        pe.wait_ge(t_out, 3 * (s - 1))
                    at_least(pe, px_out, 2 * (s - 3) + half + 1)
                    for kc in range(2):
                        mm = nc.tensor.matmul(px_bank[half][0:AUG, 0:HQ // 2], k.xn[:, bu, bi, kc, :],
                                              pt[:, j % 2, kc, half * (HQ // 2):(half + 1) * (HQ // 2)],
                                              start=(kc == 0), stop=(kc == 1))
                    mm.then_inc(px_full, 1)

                for n in range(3):
                    if n < len(SHARED[i]):
                        shared(it, u, i, n, *SHARED[i][n])
                    if n < 2:
                        weigh(n)
                    turn_piece(n, PIECES[n])

            pe.wait_ge(xT_in[0], 16)
            for m in range(6):
                at_least(pe, q_out, m)
                for hh in range(2):
                    src = k.xT[:, 0, :].rearrange("p (b r s c t) -> p b r s c t", b=GROUP, r=RESQ, s=2, c=RESQ)[:, :, :, 0, :, 0]
                    mm = nc.tensor.matmul(m_bank[0:AUG, hh * GTOK:(hh + 1) * GTOK], k.mh[:, 2 * m + hh, :], src,
                                          start=True, stop=True)
                mm.then_inc(q_full, 1)
            run(pe, slot)

        @block.vector
        def _(dve):
            def slot(it, j):
                u, i = rolled(j)
                s = BODY * it + j
                if live(it, j, 1):
                    par = (j - 1) % 2
                    dve.wait_ge(p_exp, s)
                    nc.vector.reciprocal(inv[:, par, :], total[:, par, :]).then_inc(inv_done, 1)
                    dve.wait_ge(inv_done, s)
                    for p, chunks in enumerate(PIECES):
                        for c in chunks:
                            ins = nc.vector.tensor_scalar(prob[:, par, c, :], prob[:, par, c, :], inv[:, par, c:c + 1], None, ALU.mult)
                        ins.then_inc(p_norm, 1)
                if live(it, j, 0):
                    par = j % 2
                    for p, chunks in enumerate(PIECES):
                        dve.wait_ge(s_full, 3 * s + p + 1)
                        if p == 0 and live(it, j, 2):
                            dve.wait_ge(p_exp, s - 1)
                        carry_waits(dve, tally)
                        for n, c in enumerate(chunks):
                            nc.vector.tensor_tensor_reduce(
                                sbias[:, par, c, :], s_bank[p][0:CH, n * KEYS:(n + 1) * KEYS], k.bias[:, c, :],
                                -1.0, 3e38, ALU.add, ALU.min, low[:, par, c:c + 1]).then_inc(s_max, 1)
                for n in range(3):
                    if n < len(SHARED[i]):
                        leave_shared(it, u, *SHARED[i][n])
                    if n < 2 and live(it, j, 2):
                        bu, bi = rolled((j - 2) % BODY)
                        if bi == 0 and n == 0:
                            at_least(dve, o_full, 3 * ((2 * it + (u if i >= 2 else u - 1)) - 1))
                        dve.wait_ge(px_full, 2 * (s - 2) + n + 1)
                        nc.vector.tensor_copy(px[:, bu, 6 * n:6 * n + 6, bi * QUERIES:(bi + 1) * QUERIES],
                                              px_bank[n][0:AUG, 0:HQ // 2].rearrange("p (h q) -> p h q", h=6)).then_inc(px_out, 1)

            def leave_shared(it, u, kind, m):
                if kind == "h" and group_live(it, u, 2):
                    dve.wait_ge(h_full, 2 * it + u - 1)
                    nc.vector.tensor_tensor(k.h[:, bass.ds(4 * it + 2 * u - 4, 2), :],
                                            m_bank[0:ROWS, 0:2 * DIM].rearrange("p (t d) -> p t d", t=2),
                                            bc(k.prow[0:ROWS, :].unsqueeze(1), [ROWS, 2, DIM]), ALU.add).then_inc(h_out, 1)
                    dve.wait_ge(h_out, 2 * it + u - 1)
                    carry_waits(dve, tally)
                    row_stats(nc, k, k.h, 4 * it + 2 * u - 4, 2)
                if kind == "o" and group_live(it, u, 1):
                    par = (u - 1) % 2
                    n = (3 * par + m) % 2
                    if m == 0:
                        at_least(dve, h_full, 2 * it + u - 1)
                    dve.wait_ge(o_relu, 3 * (2 * it + u - 1) + m + 1)
                    nc.vector.scalar_tensor_tensor(hs[:, par, 2 * m:2 * m + 2, :], shifted[:, n, :, :], 6.0,
                                                   m_bank[:, 0:2 * GTOK].rearrange("p (t d) -> p t d", t=2),
                                                   ALU.min, ALU.mult).then_inc(o_hs, 1)

            run(dve, slot)
            dve.wait_ge(h_out, GROUPS)

        @block.scalar
        def _(act):
            def evacuate_q(it, u, m, par):
                dst = qt[:, par, :, :].rearrange("p b (h q) -> p h b q", h=HEADS)
                for hh in range(2):
                    ins = nc.scalar.activation(dst[:, 2 * m + hh, :, :],
                                               m_bank[0:AUG, hh * GTOK:(hh + 1) * GTOK].rearrange("p (b q) -> p b q", b=GROUP),
                                               ACT.Copy, scale=KD ** -0.5)
                ins.then_inc(q_out, 1)

            def slot(it, j):
                u, i = rolled(j)
                s = BODY * it + j
                def leave_shared(kind, m):
                    if kind == "q" and group_live(it, u, -1):
                        if m == 0:
                            at_least(act, s_full, 3 * GROUP * (2 * it + u))
                        act.wait_ge(q_full, 6 * (2 * it + u + 1) + m + 1)
                        evacuate_q(it, u, m, (u + 1) % 2)
                    if kind == "o" and group_live(it, u, 1):
                        par = (u - 1) % 2
                        n = (3 * par + m) % 2
                        at_least(act, o_hs, 3 * (2 * it + u - 1) + m - 1)
                        act.wait_ge(o_full, 3 * (2 * it + u - 1) + m + 1)
                        nc.scalar.activation(shifted[:, n, :, :], m_bank[:, 0:2 * GTOK].rearrange("p (t d) -> p t d", t=2),
                                             ACT.Relu, bias=k.three[:, 0:1]).then_inc(o_relu, 1)

                def leave_turned(p, chunks):
                    par = (j - 1) % 2
                    if p == 0 and live(it, j, 3):
                        act.wait_ge(px_full, 2 * (s - 2))
                    act.wait_ge(t_full, 3 * (s - 1) + p + 1)
                    src = t_bank[(3 * (j - 1) + p) % 2][0:KHALF, 0:2 * CH * len(chunks)].rearrange(
                        "p (n c r) -> p c n r", n=len(chunks), c=2)
                    at = CHUNK_AT[chunks[0]]
                    if p == 2:
                        act.wait_ge(t_out, 3 * (s - 1) + p)
                    nc.scalar.activation(pt[:, par, :, at:at + CH * len(chunks)].rearrange("p c (n r) -> p c n r", r=CH), src,
                                         ACT.Copy).then_inc(t_out, 1)

                early = live(it, j, 0) and SHARED[i][0][0] == "q"
                if live(it, j, 0):
                    par = j % 2
                    if live(it, j, 2):
                        act.wait_ge(t_full, 3 * (s - 1))
                    for c in range(CHUNKS):
                        if early and c == 2:
                            leave_shared(*SHARED[i][0])
                        act.wait_ge(s_max, 5 * s + c + 1)
                        ins = nc.scalar.activation(prob[:, par, c, :], sbias[:, par, c, :], ACT.Exp, bias=low[:, par, c:c + 1],
                                                   scale=-1.0, accum_out=total[:, par, c:c + 1])
                    ins.then_inc(p_exp, 1)
                for n in range(3):
                    if n < len(SHARED[i]) and not (early and n == 0):
                        leave_shared(*SHARED[i][n])
                    if live(it, j, 1):
                        leave_turned(n, PIECES[n])

            for m in range(6):
                act.wait_ge(q_full, m + 1)
                evacuate_q(0, 0, m, 0)
            run(act, slot)


def peeled(eng, steps, body):
    body(0)
    with eng.Fori(1, steps) as it:
        body(it)


def row_stats(nc, k, x, tile, count=1):
    for t in range(count):
        ins = nc.vector.bn_stats(k.raw[:, tile + t, :], x[:, tile + t, :])
    return ins


class Norm:

    def __init__(self, nc, ctx, name, k):
        sb = lambda n, s: ctx.enter_context(nc.sbuf_tensor(f"{name}_{n}", s, F32))
        self.nc, self.raw = nc, k.raw
        self.mean, self.var, self.rstd = sb("mean", [ROWS, TILES]), sb("var", [ROWS, TILES]), sb("rstd", [ROWS, TILES])
        self.half, self.gap, self.shift = sb("half", [ROWS, TILES]), sb("gap", [ROWS, TILES]), sb("shift", [ROWS, TILES])
        self.chain, self.var_ready, self.root_done, self.rstd_ready = (
            ctx.semaphore(f"{name}_{n}") for n in ("chain", "var_ready", "root_done", "rstd_ready"))

    def vector_part(self, dve):
        nc, n = self.nc, [0]

        def link(ins):
            n[0] += 1
            ins.then_inc(self.chain, 1)
            dve.wait_ge(self.chain, n[0])

        m0, c0, m1, c1 = self.raw[:, :, 1], self.raw[:, :, 2], self.raw[:, :, 4], self.raw[:, :, 5]
        link(nc.vector.tensor_tensor(self.gap[:], m0, m1, ALU.subtract))
        link(nc.vector.tensor_tensor(self.half[:], c0, c1, ALU.add))
        link(nc.vector.tensor_tensor(self.gap[:], self.gap[:], self.gap[:], ALU.mult))
        link(nc.vector.tensor_scalar(self.half[:], self.half[:], 1.0 / DIM, EPS, ALU.mult, ALU.add))
        nc.vector.scalar_tensor_tensor(self.var[:], self.gap[:], 0.25, self.half[:], ALU.mult, ALU.add).then_inc(self.var_ready, 1)
        link(nc.vector.tensor_tensor(self.rstd[:], m0, m1, ALU.add))
        link(nc.vector.tensor_scalar(self.mean[:], self.rstd[:], 0.5, None, ALU.mult))
        dve.wait_ge(self.root_done, 1)
        nc.vector.reciprocal(self.rstd[:], self.var[:]).then_inc(self.rstd_ready, 1)
        dve.wait_ge(self.rstd_ready, 1)

    def vector_shift(self, dve):
        self.nc.vector.scalar_tensor_tensor(self.shift[:], self.mean[:], -1.0, self.rstd[:], ALU.mult, ALU.mult).then_inc(self.rstd_ready, 1)
        dve.wait_ge(self.rstd_ready, 2)

    def scalar_rows(self, act, out, x, done, tiles):
        act.wait_ge(self.rstd_ready, 2)
        with act.Fori(0, TILES // 8) as it:
            for t in range(tiles):
                tile = 8 * it + t
                self.nc.scalar.activation(out[:, tile, :], x[:, tile, :], ACT.Identity, bias=self.shift[:, bass.ds(tile, 1)],
                                          scale=self.rstd[:, bass.ds(tile, 1)]).then_inc(done, 1)

    def scalar_part(self, act):
        act.wait_ge(self.var_ready, 1)
        self.nc.scalar.activation(self.var[:], self.var[:], ACT.Sqrt).then_inc(self.root_done, 1)


XH, XE, SRC, LLM = 8, 16, 250, 1024
SHALF = SRC // 2
LCH = LLM // 128

BT = 4
BTOK = BT * ROWS


def band_stage(nc, a, k):
    with Stage(nc) as ctx:
        sb = lambda n, s, d=F32: ctx.enter_context(nc.sbuf_tensor(n, s, d))
        sem = lambda n: ctx.semaphore(n)
        norm_a, norm_b = Norm(nc, ctx, "band", k), Norm(nc, ctx, "ffn", k)
        w = sb("band_w", [DIM, 4, DIM])
        uv = sb("uv", [DIM, 1])
        vv = sb("vv", [ROWS, DIM])
        trig = sb("trig", [DIM, 2, QUERIES])
        mask = sb("mask", [ROWS, ROWS])
        rows = sb("rows", [ROWS, 2, BT, DIM])
        xt = sb("xt", [DIM, 2, BTOK])
        turn = sb("turn", [DIM, 2, 4, BTOK])
        rot = sb("rot", [DIM, 2, 2, BTOK])
        sval = sb("sval", [DIM, 2, BTOK])
        smask = sb("smask", [ROWS, 2, BT, ROWS])
        prob = sb("bprob", [ROWS, 2, BT, ROWS])
        junk = sb("junk", [ROWS, 2, BT, ROWS])
        low, den, num = sb("blow", [ROWS, 2, BT]), sb("bden", [ROWS, 2, BT]), sb("bnum", [ROWS, 2, BT])
        tally, tally_pool, sum_act = sem("b_tally"), sem("b_tally_pool"), sem("b_sum_act")
        gain = sb("gain", [ROWS, TILES])
        names = ("w_in", "rows_done", "tr", "xt_out", "proj", "s_out", "turned", "rotated", "s_full", "s_low", "p_exp",
                 "num_done", "inv_done", "ratio", "h_done", "seen", "gain_done", "sum_done")
        (w_in, rows_done, tr, xt_out, proj, s_out, turned, rotated, s_full, s_low, p_exp, num_done, inv_done, ratio,
         h_done, seen, gain_done, sum_done) = (sem("b_" + n) for n in names)
        xt_bank, s_bank, v_bank, q_banks = k.banks[0], k.banks[6:8], k.banks[5], k.banks[1:5]
        STEPS = TILES // BT // 2
        kv_bias, kv_full, kv_out = (sem("b_" + n) for n in ("kv_bias", "kv_full", "kv_out"))
        block = ctx.enter_context(nc.Block())


        def run(eng, slot, after_two=None):
            for u in range(2):
                slot(-1, u)
            if after_two:
                after_two()
            for u in range(2):
                slot(0, u)
            with eng.Fori(1, STEPS - 1) as it:
                for u in range(2):
                    slot(it, u)
            for it in (STEPS - 1, STEPS):
                for u in range(2):
                    slot(it, u)

        def live(it, u, ahead):
            return not isinstance(it, int) or 0 <= 2 * it + u + ahead < 2 * STEPS

        @block.sync
        def _(sp):
            sp.dma_start(w[:], a["band_w"]).then_inc(w_in, 16)
            sp.dma_start(uv[:], a["u_v"]).then_inc(w_in, 16)
            sp.dma_start(vv[:], a["v_v"].partition_broadcast(ROWS)).then_inc(w_in, 16)
            sp.dma_start(trig[:], a["trig"]).then_inc(w_in, 16)
            sp.dma_start(mask[:], a["band_mask"]).then_inc(w_in, 16)

        @block.vector
        def _(dve):
            nc.vector.memset(k.v[:], 0.0).then_inc(kv_bias, 1)
            norm_a.vector_part(dve)
            norm_a.vector_shift(dve)
            nc.vector.tensor_scalar(k.bq[:], k.bq[:], XE ** -0.5, None, ALU.mult).then_inc(kv_bias, 1)
            nc.vector.tensor_scalar(k.bk_own[:], k.own[:], k.bk[:, 0:1], None, ALU.mult).then_inc(kv_bias, 1)
            dve.wait_ge(w_in, 16 * 5)

            def rotate(it, u):
                g = 2 * it + u
                dve.wait_ge(proj, g + 1)
                at_least(dve, rotated, g - 1)
                for i in range(4):
                    ins = nc.vector.tensor_tensor(turn[:, u, i, :].rearrange("p (b q) -> p b q", q=QUERIES),
                                                  q_banks[i][:, 0:BTOK].rearrange("p (b q) -> p b q", q=QUERIES),
                                                  bc(trig[:, i % 2, :].unsqueeze(1), [DIM, BTOK // QUERIES, QUERIES]), ALU.mult)
                ins.then_inc(turned, 1)

            def lowest(it, u):
                g = 2 * it + u
                dve.wait_ge(s_full, g + 1)
                at_least(dve, p_exp, g - 1)
                carry_waits(dve, tally)
                for t in range(BT):
                    ins = nc.vector.tensor_tensor_reduce(smask[:, u, t, :], s_bank[u][0:ROWS, t * ROWS:(t + 1) * ROWS], mask[:],
                                                         -(DIM ** -0.5), 3e38, ALU.add, ALU.min, low[:, u, t:t + 1])
                ins.then_inc(s_low, 1)

            def add_rows(it, u):
                g = 2 * it + u
                dve.wait_ge(p_exp, g + 1)
                dve.wait_ge(s_out, g + 1)
                for t in range(BT):
                    ins = nc.vector.tensor_tensor_reduce(junk[:, u, t, :], prob[:, u, t, :], sval[0:ROWS, u, t * ROWS:(t + 1) * ROWS],
                                                         1.0, 0.0, ALU.mult, ALU.add, num[:, u, t:t + 1])
                ins.then_inc(num_done, 1)
                nc.vector.reciprocal(den[:, u, :], den[:, u, :]).then_inc(inv_done, 1)
                dve.wait_ge(num_done, g + 1)
                dve.wait_ge(inv_done, g + 1)
                nc.vector.tensor_tensor(num[:, u, :], num[:, u, :], den[:, u, :], ALU.mult).then_inc(ratio, 1)
                dve.wait_ge(ratio, g + 1)
                for t in range(BT):
                    tile = 4 * g + t
                    ins = nc.vector.scalar_tensor_tensor(k.h[:, tile, :], vv[:], num[:, u, t:t + 1], k.h[:, tile, :],
                                                         ALU.mult, ALU.add)
                ins.then_inc(h_done, 1)
                dve.wait_ge(h_done, g + 1)
                carry_waits(dve, tally)
                row_stats(nc, k, k.h, 4 * g, BT).then_inc(seen, 1)

            def slot(it, u):
                if live(it, u, 0):
                    rotate(it, u)
                if live(it, u, -1):
                    add_rows(it - 1 + u, 1 - u)
                if live(it, u, 0):
                    lowest(it, u)

            def source_values():
                dve.wait_ge(kv_bias, 3)
                dve.wait_ge(kv_full, 2)
                for kc in range(2):
                    for h in range(XH):
                        at = slice(h * XE, (h + 1) * XE)
                        nc.vector.tensor_tensor(k.v[:, kc, h, at], s_bank[1][0:SHALF, kc * DIM + h * XE:kc * DIM + (h + 1) * XE],
                                                k.bv[:, at], ALU.add).then_inc(kv_out, 1)

            run(dve, slot, source_values)
            dve.wait_ge(seen, 2 * STEPS)
            norm_b.vector_part(dve)
            nc.vector.tensor_scalar(gain[:], norm_b.rstd[:], 1.0, None, ALU.add).then_inc(gain_done, 1)
            norm_b.vector_shift(dve)
            dve.wait_ge(gain_done, 1)

            def add_norm(it):
                for t in range(4):
                    tile = 8 * it + t
                    ins = nc.vector.tensor_scalar(k.h[:, tile, :], k.h[:, tile, :], gain[:, bass.ds(tile, 1)], norm_b.shift[:, bass.ds(tile, 1)],
                                                  ALU.mult, ALU.add)
                ins.then_inc(sum_done, 1)

            def stats(it):
                dve.wait_ge(sum_done, it + 1)
                dve.wait_ge(sum_act, it + 1)
                carry_waits(dve, tally)
                row_stats(nc, k, k.h, 8 * it, 8)

            add_norm(0)
            with dve.Fori(1, TILES // 8) as it:
                add_norm(it)
                stats(it - 1)
            stats(TILES // 8 - 1)

        @block.gpsimd
        def _(pool):
            def slot(it, u):
                g = 2 * it + u
                if live(it, u, 0):
                    pool.wait_ge(turned, g + 1)
                    at_least(pool, s_full, g - 1)
                    carry_waits(pool, tally_pool)
                    for i in range(2):
                        ins = nc.gpsimd.tensor_tensor(rot[:, u, i, :], turn[:, u, 2 * i, :], turn[:, u, 2 * i + 1, :], ALU.add)
                    ins.then_inc(rotated, 1)

            run(pool, slot)

        @block.tensor
        def _(pe):
            for c in range(LCH):
                mm = nc.tensor.matmul(s_bank[0][:, 0:SRC], k.wk[:, c, :], k.srcT[:, c, :], start=(c == 0), stop=(c == LCH - 1))
            mm.then_inc(kv_full, 1)
            for kc in range(2):
                for c in range(LCH):
                    mm = nc.tensor.matmul(s_bank[1][0:SHALF, kc * DIM:(kc + 1) * DIM], k.valT[:, c, kc * SHALF:(kc + 1) * SHALF],
                                          k.wv_x[:, c, :], start=(c == 0), stop=(c == LCH - 1))
            mm.then_inc(kv_full, 1)
            pe.wait_ge(w_in, 16 * 5)

            def turn_rows(it, u):
                g = 2 * it + u
                pe.wait_ge(rows_done, g + 1)
                at_least(pe, xt_out, g)
                for t in range(BT):
                    mm = nc.tensor.transpose(xt_bank[:, t * ROWS:(t + 1) * ROWS], rows[:, u, t, :], k.ident[0:ROWS, 0:ROWS])
                mm.then_inc(tr, 1)

            def project(it, u):
                g = 2 * it + u
                pe.wait_ge(xt_out, g + 1)
                at_least(pe, turned, g)
                at_least(pe, s_out, g)
                for i in range(4):
                    nc.tensor.matmul(q_banks[i][:, 0:BTOK], w[:, i, :], xt[:, u, :], start=True, stop=True)
                nc.tensor.matmul(v_bank[:, 0:BTOK], bc(uv[:, 0:1], [DIM, DIM]), xt[:, u, :], start=True, stop=True).then_inc(proj, 1)

            def scores(it, u):
                g = 2 * it + u
                pe.wait_ge(rotated, g + 1)
                if isinstance(g, int) and g == 0:
                    pe.wait_ge(kv_out, 3 * XH)
                at_least(pe, s_low, g - 1)
                for t in range(BT):
                    mm = nc.tensor.matmul(s_bank[u][0:ROWS, t * ROWS:(t + 1) * ROWS], rot[:, u, 0, t * ROWS:(t + 1) * ROWS],
                                          rot[:, u, 1, t * ROWS:(t + 1) * ROWS], start=True, stop=True)
                mm.then_inc(s_full, 1)

            def slot(it, u):
                if live(it, u, 1):
                    project(it + u, 1 - u)
                if live(it, u, 0):
                    scores(it, u)
                if live(it, u, 2):
                    turn_rows(it + 1, u)

            run(pe, slot)

        @block.scalar
        def _(act):
            norm_a.scalar_part(act)
            act.wait_ge(norm_a.rstd_ready, 2)

            def source_keys():
                act.wait_ge(kv_bias, 3)
                act.wait_ge(kv_full, 1)
                for h in range(XH):
                    nc.scalar.activation(k.kT[:, h, :], s_bank[0][:, 0:SRC], ACT.Identity, bias=k.bk_own[:, h:h + 1],
                                         scale=k.own[:, h:h + 1]).then_inc(kv_out, 1)

            def make_rows(it, u):
                g = 2 * it + u
                at_least(act, tr, g - 1)
                for t in range(BT):
                    tile = 4 * g + t
                    ins = nc.scalar.activation(rows[:, u, t, :], k.h[:, tile, :], ACT.Identity, bias=norm_a.shift[:, bass.ds(tile, 1)],
                                               scale=norm_a.rstd[:, bass.ds(tile, 1)])
                ins.then_inc(rows_done, 1)

            def copy_x(it, u):
                g = 2 * it + u
                act.wait_ge(tr, g + 1)
                at_least(act, proj, g - 1)
                nc.scalar.activation(xt[:, u, :], xt_bank[:, 0:BTOK], ACT.Copy).then_inc(xt_out, 1)

            def copy_s(it, u):
                g = 2 * it + u
                act.wait_ge(proj, g + 1)
                at_least(act, num_done, g - 1)
                nc.scalar.activation(sval[:, u, :], v_bank[:, 0:BTOK], ACT.Copy).then_inc(s_out, 1)

            def expo(it, u):
                g = 2 * it + u
                act.wait_ge(s_low, g + 1)
                at_least(act, ratio, g - 1)
                for t in range(BT):
                    ins = nc.scalar.activation(prob[:, u, t, :], smask[:, u, t, :], ACT.Exp, bias=low[:, u, t:t + 1], scale=-1.0,
                                               accum_out=den[:, u, t:t + 1])
                ins.then_inc(p_exp, 1)

            def slot(it, u):
                if live(it, u, 2):
                    make_rows(it + 1, u)
                if live(it, u, 0):
                    expo(it, u)
                if live(it, u, 1):
                    copy_s(it + u, 1 - u)
                if live(it, u, 2):
                    copy_x(it + 1, u)

            run(act, slot, source_keys)
            norm_b.scalar_part(act)
            act.wait_ge(gain_done, 1)
            act.wait_ge(norm_b.rstd_ready, 2)
            with act.Fori(0, TILES // 8) as it:
                for t in range(4, 8):
                    tile = 8 * it + t
                    ins = nc.scalar.activation(k.h[:, tile, :], k.h[:, tile, :], ACT.Identity, bias=norm_b.shift[:, bass.ds(tile, 1)],
                                               scale=gain[:, bass.ds(tile, 1)])
                ins.then_inc(sum_act, 1)


def cross_stage(nc, a, k):
    with Stage(nc) as ctx:
        sb = lambda n, s, d=F32: ctx.enter_context(nc.sbuf_tensor(n, s, d))
        sem = lambda n: ctx.semaphore("c_" + n)
        norm = Norm(nc, ctx, "cross", k)
        tally, tally_pool = sem("tally"), sem("tally_pool")
        kT, v, wq, wo, bq, bo = k.kT, k.v, k.wq, k.wo, k.bq, k.bo
        rows = sb("crows", [ROWS, 2, DIM])
        turned = sb("turned", [DIM, 2, 2, ROWS])
        qT = sb("qT", [DIM, 2, ROWS])
        prob = sb("cprob", [ROWS, 2, XH, SRC])
        low, total, inv = sb("clow", [ROWS, 2, XH]), sb("ctotal", [ROWS, 2, XH]), sb("cinv", [ROWS, 2, DIM])
        pt = sb("cpt", [SHALF, 2, XH, 2, ROWS])
        one_by = sb("one_by", [ROWS, 2, XH])
        ot = sb("cot", [DIM, 2, ROWS])
        names = ("bo_added", "rows_done", "tr", "tr_out", "q_full", "q_out", "s_full", "s_low",
                 "p_exp", "t_full", "t_out", "t_last", "one_by_done", "inv_done", "pv_full", "o_done", "wo_full", "h_done")
        (bo_added, rows_done, tr, tr_out, q_full, q_out, s_full, s_low,
         p_exp, t_full, t_out, t_last, one_by_done, inv_done, pv_full, o_done, wo_full, h_done) = (sem(n) for n in names)
        s_bank, t_bank, pv_bank, m_bank = k.banks[0:4], k.banks[4:6], k.banks[6], k.banks[7]
        STEPS = TILES // 4
        gslope, cell = sb("gslope", [128, EXPERTS, GRID]), sb("cell", [128, GRID])
        empty = sb("empty", [128, SLOTS // 512, ROW])
        spare = sb("spare", [128, 4, SLOTS // 512], I32)
        spare_in, numbered, slots_out = sem("spare_in"), sem("numbered"), sem("slots_out")
        table_in, wd_in, moe_in, zeroed, split = sem("table_in"), sem("wd_in"), sem("moe_in"), sem("zeroed"), sem("split")

        def run(eng, slot):
            for it in (-1, 0):
                for j in range(4):
                    slot(it, j)
            with eng.Fori(1, STEPS - 1) as it:
                for j in range(4):
                    slot(it, j)
            for it in (STEPS - 1, STEPS):
                for j in range(4):
                    slot(it, j)

        def live(it, j, back):
            return not isinstance(it, int) or 0 <= 4 * it + j - back < TILES

        block = ctx.enter_context(nc.Block())

        @block.sync
        def _(sp):
            sp.dma_start(spare[:], a["spare"]).then_inc(spare_in, 16)
            sp.dma_start(k.table[:], a["spline"]).then_inc(table_in, 16)
            sp.dma_start(cell[:], a["cell"].partition_broadcast(128)).then_inc(table_in, 16)
            sp.dma_start(k.wd[:], a["wd"]).then_inc(wd_in, 16)
            sp.dma_start(k.wu[:], a["wu"]).then_inc(moe_in, 16)
            slots = k.x_slots.rearrange("(n p r) d -> n p r d", n=4, p=128)
            for i in range(4):
                sp.wait_ge(numbered, i + 1)
                sp.dma_start(slots[i], empty[:]).then_inc(slots_out, 16)
            sp.wait_ge(slots_out, 16 * 4)
            sp.wait_ge(moe_in, 16)

        @block.gpsimd
        def _(pool):
            def slot(it, j):
                t = 4 * it + j
                if live(it, j, -3):
                    pool.wait_ge(rows_done, t + 4)
                    carry_waits(pool, tally_pool)
                    nc.gpsimd.tensor_tensor(k.h[:, bass.ds(t + 3, 1), :], k.h[:, bass.ds(t + 3, 1), :], bo[:].unsqueeze(1), ALU.add).then_inc(bo_added, 1)

            run(pool, slot)
            nc.gpsimd.memset(empty[:], 0.0).then_inc(zeroed, 1)
            pool.wait_ge(zeroed, 1)
            pool.wait_ge(spare_in, 16)
            for i in range(4):
                if i >= 1:
                    pool.wait_ge(slots_out, 16 * i)
                nc.gpsimd.tensor_copy(empty[:, :, DIM:ROW].bitcast(I32), spare[:, i, :].unsqueeze(2)).then_inc(numbered, 1)
            pool.wait_ge(table_in, 32)
            tv = k.table[:].rearrange("p (e g c) -> p e g c", g=GRID, c=2)
            nc.gpsimd.tensor_tensor(gslope[:], tv[:, :, :, 1], bc(cell[:].unsqueeze(1), [128, EXPERTS, GRID]), ALU.mult).then_inc(split, 1)
            pool.wait_ge(split, 1)
            nc.gpsimd.tensor_tensor(tv[:, :, :, 0], tv[:, :, :, 0], gslope[:], ALU.subtract)


        def q_turn(it, j):
            return live(it, j, -1)

        def turn_live(it, j):
            return live(it, j, -2) or live(it, j, 1)

        @block.tensor
        def _(pe):
            def scores(it, j, b):
                t = 4 * it + j
                if live(it, j, 0):
                    if b == 0:
                        pe.wait_ge(q_out, t + 1)
                    if live(it, j, 1):
                        pe.wait_ge(p_exp, 4 * (t - 1) + b + 1)
                    for n in range(2):
                        mm = nc.tensor.matmul(s_bank[b][0:ROWS, n * SRC:(n + 1) * SRC], qT[:, j % 2, :], kT[:, 2 * b + n, :],
                                              start=True, stop=True)
                    mm.then_inc(s_full, 1)

            def turn_probs(it, j, b):
                t = 4 * it + j
                if live(it, j, 1):
                    pe.wait_ge(p_exp, 4 * (t - 1) + b + 1)
                    if b == 1:
                        at_least(pe, t_last, t - 1)
                    else:
                        at_least(pe, t_out, 3 * (t - 1) + max(b - 1, 0))
                    for n in range(2):
                        for kc in range(2):
                            mm = nc.tensor.transpose(t_bank[b % 2][0:SHALF, (2 * n + kc) * ROWS:(2 * n + kc + 1) * ROWS],
                                                     prob[:, (j - 1) % 2, 2 * b + n, kc * SHALF:(kc + 1) * SHALF], k.ident[0:ROWS, 0:ROWS])
                    mm.then_inc(t_full, 1)

            def values(it, j, b):
                t = 4 * it + j
                if live(it, j, 2):
                    if b == 0:
                        pe.wait_ge(t_out, 3 * (t - 1))
                        pe.wait_ge(t_last, t - 1)
                        at_least(pe, o_done, t - 2)
                    for n in range(2):
                        for kc in range(2):
                            half = slice(64 * (b // 2), 64 * (b // 2) + 64)
                            mm = nc.tensor.matmul(pv_bank[half, 0:ROWS], v[:, kc, 2 * b + n, half], pt[:, j % 2, 2 * b + n, kc, :],
                                                  start=(b % 2 == 0 and n == 0 and kc == 0), stop=(b % 2 == 1 and n == 1 and kc == 1))
                    if b == 3:
                        mm.then_inc(pv_full, 1)

            def queries(it, j):
                t = 4 * it + j
                if q_turn(it, j):
                    pe.wait_ge(tr_out, t + 2)
                    nc.tensor.matmul(m_bank[:, 0:ROWS], wq[:], turned[:, (j - 1) % 2, 0, :], start=True, stop=True).then_inc(q_full, 1)

            def out_rows(it, j):
                t = 4 * it + j
                if live(it, j, 3):
                    pe.wait_ge(o_done, t - 2)
                    if q_turn(it, j):
                        pe.wait_ge(q_out, t + 2)
                    else:
                        pe.wait_ge(tr_out, min(t + 2, TILES + 3))
                        pe.wait_ge(h_done, t - 3)
                    nc.tensor.matmul(m_bank[0:ROWS, 0:DIM], ot[:, (j - 3) % 2, :], wo[:], start=True, stop=True).then_inc(wo_full, 1)

            def turn(it, j):
                t = 4 * it + j
                if turn_live(it, j):
                    if live(it, j, 3):
                        pe.wait_ge(h_done, t - 2)
                    elif q_turn(it, j):
                        pe.wait_ge(q_out, t + 2)
                    if live(it, j, -2):
                        pe.wait_ge(rows_done, t + 3)
                        mm = nc.tensor.transpose(m_bank[:, 0:ROWS], rows[:, j % 2, :], k.ident[0:ROWS, 0:ROWS])
                    if live(it, j, 1):
                        pe.wait_ge(inv_done, t)
                        mm = nc.tensor.transpose(m_bank[:, ROWS:2 * ROWS], inv[:, (j - 1) % 2, :], k.ident[0:ROWS, 0:ROWS])
                    mm.then_inc(tr, 1)

            def slot(it, j):
                scores(it, j, 0)
                turn_probs(it, j, 0)
                queries(it, j)
                values(it, j, 0)
                scores(it, j, 1)
                turn_probs(it, j, 1)
                out_rows(it, j)
                values(it, j, 1)
                scores(it, j, 2)
                turn_probs(it, j, 2)
                values(it, j, 2)
                scores(it, j, 3)
                turn(it, j)
                turn_probs(it, j, 3)
                values(it, j, 3)

            run(pe, slot)

        @block.vector
        def _(dve):
            norm.vector_part(dve)

            def make_rows(it, j):
                t = 4 * it + j
                if live(it, j, -3):
                    at_least(dve, tr, t + 2)
                    nc.vector.tensor_scalar(rows[:, (j + 1) % 2, :].unsqueeze(1), k.h[:, bass.ds(t + 3, 1), :],
                                            norm.mean[:, bass.ds(t + 3, 1)], norm.rstd[:, bass.ds(t + 3, 1)],
                                            ALU.subtract, ALU.mult).then_inc(rows_done, 1)

            def slot(it, j):
                t = 4 * it + j
                if live(it, j, 3):
                    dve.wait_ge(pv_full, t - 2)
                    dve.wait_ge(tr_out, t + 1)
                    if live(it, j, 5):
                        dve.wait_ge(wo_full, t - 4)
                    nc.vector.tensor_tensor(ot[:, (j - 3) % 2, :], pv_bank[:, 0:ROWS], turned[:, j % 2, 1, :], ALU.mult).then_inc(o_done, 1)
                for b in range(4):
                    if live(it, j, 0):
                        dve.wait_ge(s_full, 4 * t + b + 1)
                        if b == 0 and live(it, j, 2):
                            dve.wait_ge(p_exp, 4 * (t - 1))
                        nc.vector.tensor_reduce(low[:, j % 2, 2 * b:2 * b + 2],
                                                s_bank[b][0:ROWS, 0:2 * SRC].rearrange("p (h s) -> p h s", h=2),
                                                AX_X, ALU.max, negate=True).then_inc(s_low, 1)
                    if live(it, j, 1) and b < 3:
                        dve.wait_ge(t_full, 4 * (t - 1) + b + 1)
                        if b == 0 and live(it, j, 3):
                            dve.wait_ge(pv_full, t - 2)
                        nc.vector.tensor_copy(pt[:, (j - 1) % 2, 2 * b:2 * b + 2, :, :].rearrange("p h c r -> p (h c r)"),
                                              t_bank[b % 2][0:SHALF, 0:4 * ROWS]).then_inc(t_out, 1)
                    if live(it, j, 1) and b == 0:
                        dve.wait_ge(p_exp, 4 * t)
                        at_least(dve, tr, t + 1)
                        nc.vector.reciprocal(one_by[:, (j - 1) % 2, :], total[:, (j - 1) % 2, :]).then_inc(one_by_done, 1)
                        dve.wait_ge(one_by_done, t)
                        nc.vector.tensor_copy(inv[:, (j - 1) % 2, :].rearrange("p (h e) -> p h e", h=XH),
                                              bc(one_by[:, (j - 1) % 2, :].unsqueeze(2), [ROWS, XH, XE])).then_inc(inv_done, 1)
                    if live(it, j, 3) and b == 1:
                        dve.wait_ge(wo_full, t - 2)
                        dve.wait_ge(bo_added, t - 2)
                        nc.vector.tensor_tensor(k.h[:, bass.ds(t - 3, 1), :], m_bank[0:ROWS, 0:DIM].unsqueeze(1),
                                                k.h[:, bass.ds(t - 3, 1), :], ALU.add).then_inc(h_done, 1)
                    if live(it, j, 3) and b == 2:
                        dve.wait_ge(h_done, t - 2)
                        carry_waits(dve, tally)
                        row_stats(nc, k, k.h, t - 3)
                    if b == 2:
                        make_rows(it, j)
                if isinstance(it, int) and it == STEPS - 1:
                    dve.wait_ge(wd_in, 16)
                    part = slice(j * EXPERTS // 4 * DIM, (j + 1) * EXPERTS // 4 * DIM)
                    nc.vector.tensor_reduce(k.sums[:, j * EXPERTS // 4:(j + 1) * EXPERTS // 4],
                                            k.wd[:, part].rearrange("p (e h) -> p e h", h=DIM), AX_X, ALU.add)

            run(dve, slot)
            dve.wait_ge(h_done, TILES)

        @block.scalar
        def _(act):
            norm.scalar_part(act)
            def exps(it, j, b):
                t = 4 * it + j
                if live(it, j, 0):
                    if b == 0 and live(it, j, 2):
                        act.wait_ge(t_full, 4 * (t - 1))
                        act.wait_ge(inv_done, t - 1)
                    act.wait_ge(s_low, 4 * t + b + 1)
                    for n in range(2):
                        h = 2 * b + n
                        ins = nc.scalar.activation(prob[:, j % 2, h, :], s_bank[b][0:ROWS, n * SRC:(n + 1) * SRC], ACT.Exp,
                                                   bias=low[:, j % 2, h:h + 1], accum_out=total[:, j % 2, h:h + 1])
                    ins.then_inc(p_exp, 1)

            def slot(it, j):
                t = 4 * it + j
                if q_turn(it, j):
                    act.wait_ge(q_full, t + 2)
                    at_least(act, s_full, 4 * t)
                    nc.scalar.activation(qT[:, (j + 1) % 2, :], m_bank[:, 0:ROWS], ACT.Identity, bias=bq[:, 0:1],
                                         scale=XE ** -0.5).then_inc(q_out, 1)
                for b in range(3):
                    exps(it, j, b)
                if turn_live(it, j):
                    act.wait_ge(tr, t + 3)
                    if live(it, j, -2) and live(it, j, 1):
                        if live(it, j, 3):
                            act.wait_ge(o_done, t - 2)
                        at_least(act, q_full, t + 1)
                        ins = nc.scalar.activation(turned[:, j % 2, :, :].rearrange("p a r -> p (a r)"), m_bank[:, 0:2 * ROWS], ACT.Copy)
                    elif live(it, j, -2):
                        at_least(act, q_full, t + 1)
                        ins = nc.scalar.activation(turned[:, j % 2, 0, :], m_bank[:, 0:ROWS], ACT.Copy)
                    else:
                        act.wait_ge(o_done, t - 2)
                        ins = nc.scalar.activation(turned[:, j % 2, 1, :], m_bank[:, ROWS:2 * ROWS], ACT.Copy)
                    ins.then_inc(tr_out, 1)
                if live(it, j, 1):
                    if live(it, j, 3):
                        act.wait_ge(pv_full, t - 2)
                    act.wait_ge(t_full, 4 * (t - 1) + 4)
                    nc.scalar.activation(pt[:, (j - 1) % 2, 6:8, :, :].rearrange("p h c r -> p (h c r)"),
                                         t_bank[1][0:SHALF, 0:4 * ROWS], ACT.Copy).then_inc(t_last, 1)
                exps(it, j, 3)

            run(act, slot)


EXPERTS, CLUSTERS, GRID = 64, 8, 16
PER_CLUSTER = EXPERTS // CLUSTERS
SLOT = 32
BLOCKS = (TOKENS + EXPERTS * (SLOT - 1)) // SLOT
SLOTS = BLOCKS * SLOT
SPARE = TOKENS
ROW = DIM + 1
OWN_P = BLOCKS // 2


def route_stage(nc, a, k):
    with Stage(nc) as ctx:
        sb = lambda n, s, d=F32: ctx.enter_context(nc.sbuf_tensor(n, s, d))
        sem = lambda n: ctx.semaphore("r_" + n)
        norm_x, norm_f = Norm(nc, ctx, "outer", k), Norm(nc, ctx, "inner", k)
        tally = sem("tally")
        gamma, beta, scale_row = sb("gamma", [ROWS, DIM]), sb("beta", [ROWS, DIM]), sb("scale_row", [ROWS, EXPERTS])
        tie = sb("tie", [ROWS, CLUSTERS + EXPERTS])
        tri, all_one, ident16 = sb("tri", [ROWS, ROWS], BF16), sb("all_one", [ROWS, ROWS], BF16), sb("ident16", [ROWS, ROWS], BF16)
        tri32, ident32, block_col = sb("tri32", [ROWS, ROWS]), sb("ident32", [ROWS, ROWS]), sb("block_col", [ROWS, 2])
        x5 = sb("x5", [ROWS, TILES, DIM])
        sgn = sb("sgn", [ROWS, TILES, DIM], BF16)
        sgT = sb("sgT", [DIM, TILES, ROWS], BF16)
        csum = sb("csum", [DIM, CLUSTERS])
        sneg, cneg = sb("sneg", [DIM, EXPERTS]), sb("cneg", [DIM, CLUSTERS])
        sig = sb("sig", [DIM, CLUSTERS + EXPERTS], BF16)
        keys = sb("keys", [ROWS, TILES, CLUSTERS + EXPERTS])
        cmax, tmax = sb("cmax", [ROWS, TILES]), sb("tmax", [ROWS, TILES])
        pen = sb("pen", [ROWS, TILES, CLUSTERS])
        tkey = sb("tkey", [ROWS, TILES, EXPERTS])
        oh = sb("oh", [ROWS, TILES, EXPERTS], BF16)
        HALF = TILES // 2
        cum = sb("cum", [ROWS, 2, HALF + 1, EXPERTS], BF16)
        count_i, nb_i = sb("count_i", [ROWS, EXPERTS], I32), sb("nb_i", [ROWS, EXPERTS], I32)
        nb, upto, start = sb("nb", [ROWS, EXPERTS]), sb("upto", [ROWS, EXPERTS]), sb("start", [ROWS, EXPERTS])
        one_row, ended = sb("one_row", [ROWS, EXPERTS]), sb("ended", [ROWS, 2, EXPERTS])
        owner, owner_i = sb("owner", [ROWS, 2]), sb("owner_i", [ROWS, 2], I32)
        posf = sb("posf", [ROWS, TILES])
        number = sb("number", [ROWS, TILES], I32)
        names = ("w_in", "link", "seen", "x_two", "x_done", "f_done", "xf_ready", "h_added", "numbered", "sgn_done", "sT", "sT_out", "sig_done", "sc_full", "key_done", "oh_done",
                 "cum_step", "cum_done", "pre_full", "owner_done", "owner_out", "owner_in", "pos_done", "scattered", "consts")
        (w_in, chain, seen, x_two, x_done, f_done, xf_ready, h_added, numbered, sgn_done, sT, sT_out, sig_done, sc_full, key_done, oh_done, cum_step, cum_done, pre_full,
          owner_done, owner_out, owner_in, pos_done, scattered, consts) = (sem(n) for n in names)
        block = ctx.enter_context(nc.Block())
        tb = [k.banks[6][:].bitcast(BF16), k.banks[7][:].bitcast(BF16)]
        LOADS = 8

        @block.sync
        def _(sp):
            for dst, name, p in ((gamma, "gamma", ROWS), (beta, "beta", ROWS), (scale_row, "scale", ROWS), (tie, "tie", ROWS)):
                sp.dma_start(dst[:], a[name].partition_broadcast(p)).then_inc(w_in, 16)
            for dst, name in ((tri32, "tri"), (ident32, "ident98"), (block_col, "block_col")):
                sp.dma_start(dst[:], a[name]).then_inc(w_in, 16)
            sp.dma_start(number[:], a["number"]).then_inc(w_in, 16)
            sp.wait_ge(owner_done, 1)
            for c in range(2):
                sp.dma_start(k.owner_dram[c * OWN_P:(c + 1) * OWN_P, :], owner_i[0:OWN_P, c:c + 1]).then_inc(owner_out, 16)
            sp.wait_ge(owner_out, 32)
            sp.dma_start(k.owner_row[:], k.owner_dram.rearrange("b o -> o b")).then_inc(owner_in, 16)
            sp.wait_ge(owner_in, 16)

        @block.vector
        def _(dve):
            n = [0]

            def link(ins):
                n[0] += 1
                ins.then_inc(chain, 1)
                dve.wait_ge(chain, n[0])

            def sign(out, x, below, done=None):
                link(nc.vector.tensor_scalar(below, x, 0.0, None, ALU.is_lt))
                return nc.vector.scalar_tensor_tensor(out, x, 0.0, below, ALU.is_gt, ALU.subtract)

            link(sign(sig[:, CLUSTERS:], k.sums[:], sneg[:]))
            link(nc.vector.tensor_reduce(csum[:], sig[:, CLUSTERS:].rearrange("p (c t) -> p c t", c=CLUSTERS), AX_X, ALU.add))
            sign(sig[:, 0:CLUSTERS], csum[:], cneg[:]).then_inc(sig_done, 1)
            link(nc.vector.memset(all_one[:], 1.0))
            link(nc.vector.memset(one_row[:], 1.0))
            link(nc.vector.memset(cum[:, :, 0, :], 0.0))
            norm_x.vector_part(dve)
            norm_x.vector_shift(dve)
            dve.wait_ge(w_in, 16 * LOADS)
            link(nc.vector.tensor_copy(tri[:], tri32[:]))
            nc.vector.tensor_copy(ident16[:], ident32[:]).then_inc(consts, 1)

            with dve.Fori(0, TILES // 8) as it:
                for t in range(6, 8):
                    tile = 8 * it + t
                    ins = nc.vector.tensor_scalar(x5[:, tile, :], k.h[:, tile, :], norm_x.mean[:, bass.ds(tile, 1)],
                                                  norm_x.rstd[:, bass.ds(tile, 1)], ALU.subtract, ALU.mult)
                ins.then_inc(x_two, 1)
                dve.wait_ge(x_done, 6 * it + 6)
                dve.wait_ge(x_two, it + 1)
                carry_waits(dve, tally)
                row_stats(nc, k, x5, 8 * it, 8).then_inc(seen, 1)
            dve.wait_ge(seen, TILES // 8)
            norm_f.vector_part(dve)
            norm_f.vector_shift(dve)
            wide = [ROWS, 8, DIM]
            for q in range(TILES // 8):
                xf_q = k.xf[:, 8 * q:8 * q + 8, 0:DIM]
                dve.wait_ge(f_done, 8 * q + 8)
                link(nc.vector.tensor_tensor(xf_q, xf_q, bc(gamma[:].unsqueeze(1), wide), ALU.mult))
                nc.vector.tensor_tensor(xf_q, xf_q, bc(beta[:].unsqueeze(1), wide), ALU.add).then_inc(xf_ready, 1)
            for g in range(TILES // 4):
                dve.wait_ge(sc_full, g + 1)
                nc.vector.scalar_tensor_tensor(keys[:, 4 * g:4 * g + 4, :],
                                               k.banks[g % 4][0:ROWS, 0:4 * 72].rearrange("p (t e) -> p t e", t=4), 16.0,
                                               bc(tie[:].unsqueeze(1), [ROWS, 4, 72]), ALU.mult, ALU.add).then_inc(key_done, 1)
            dve.wait_ge(key_done, TILES // 4)
            ck = keys[:, :, 0:CLUSTERS]
            link(nc.vector.tensor_reduce(cmax[:], ck, AX_X, ALU.max))
            link(nc.vector.tensor_tensor(pen[:], ck, bc(cmax[:].unsqueeze(2), [ROWS, TILES, CLUSTERS]), ALU.is_equal))
            link(nc.vector.tensor_scalar(pen[:], pen[:], -1.0, 1e5, ALU.add, ALU.mult))
            link(nc.vector.tensor_tensor(tkey[:].rearrange("p t (c j) -> p t c j", c=CLUSTERS),
                                         keys[:, :, CLUSTERS:].rearrange("p t (c j) -> p t c j", c=CLUSTERS),
                                         bc(pen[:].unsqueeze(3), [ROWS, TILES, CLUSTERS, PER_CLUSTER]), ALU.add))
            link(nc.vector.tensor_reduce(tmax[:], tkey[:], AX_X, ALU.max))
            nc.vector.tensor_tensor(oh[:, :, :], tkey[:], bc(tmax[:].unsqueeze(2), [ROWS, TILES, EXPERTS]), ALU.is_equal).then_inc(oh_done, 1)
            dve.wait_ge(oh_done, 1)
            for t in range(HALF):
                for half in range(2):
                    if t >= 1:
                        dve.wait_ge(cum_step, 2 * t + half - 1)
                    nc.vector.tensor_tensor(cum[:, half, t + 1, :], cum[:, half, t, :], oh[:, half * HALF + t, :], ALU.add).then_inc(cum_step, 1)
            dve.wait_ge(cum_step, TILES)
            nc.vector.tensor_copy(one_row[:], one_row[:]).then_inc(cum_done, 1)
            dve.wait_ge(pre_full, 1)
            link(nc.vector.tensor_scalar(count_i[:], k.banks[4][0:ROWS, 0:EXPERTS], float(SLOT - 1), None, ALU.add))
            link(nc.vector.tensor_scalar(nb_i[:], count_i[:], SLOT.bit_length() - 1, None, ALU.arith_shift_right))
            link(nc.vector.tensor_copy(nb[:], nb_i[:]))
            link(nc.vector.tensor_tensor_scan(upto[:], one_row[:], nb[:], 0.0, ALU.mult, ALU.add))
            link(nc.vector.tensor_tensor(start[:], upto[:], nb[:], ALU.subtract))
            link(nc.vector.tensor_scalar(start[:], start[:], float(SLOT), None, ALU.mult))
            for c in range(2):
                link(nc.vector.tensor_scalar(ended[:, c, :], upto[:], block_col[:, c:c + 1], None, ALU.is_le))
            link(nc.vector.tensor_reduce(owner[:], ended[:], AX_X, ALU.add))
            nc.vector.tensor_scalar(owner_i[:], owner[:], float(EXPERTS - 1), None, ALU.min).then_inc(owner_done, 1)
            for g in range(4):
                part = slice(8 * g, 8 * g + 8)
                link(nc.vector.tensor_tensor(tkey[:, part, :], k.banks[g][0:ROWS, :].rearrange("p (t e) -> p t e", t=8),
                                             bc(start[:].unsqueeze(1), [ROWS, 8, EXPERTS]), ALU.add))
                link(nc.vector.tensor_tensor(tkey[:, part, :], tkey[:, part, :], oh[:, part, :], ALU.mult))
                link(nc.vector.tensor_reduce(posf[:, part], tkey[:, part, :], AX_X, ALU.add))
                nc.vector.tensor_copy(k.pos[:, part], posf[:, part]).then_inc(pos_done, 1)
            dve.wait_ge(h_added, 1)
            link(nc.vector.tensor_tensor(x5[:, :, 0:EXPERTS], oh[:, :, :], bc(scale_row[:].unsqueeze(1), [ROWS, TILES, EXPERTS]), ALU.mult))
            link(nc.vector.tensor_reduce(k.scale[:], x5[:, :, 0:EXPERTS], AX_X, ALU.add))

        @block.scalar
        def _(act):
            norm_x.scalar_part(act)
            norm_x.scalar_rows(act, x5, k.h, x_done, 6)
            act.wait_ge(x_done, 6 * TILES // 8)
            act.wait_ge(x_two, TILES // 8)
            norm_f.scalar_part(act)
            norm_f.scalar_rows(act, k.xf[:, :, 0:DIM], x5, f_done, 8)
            for q in range(TILES // 8):
                act.wait_ge(xf_ready, q + 1)
                nc.scalar.activation(sgn[:, 8 * q:8 * q + 8, :], k.xf[:, 8 * q:8 * q + 8, 0:DIM], ACT.Sign).then_inc(sgn_done, 1)
            for g in range(TILES // 4):
                act.wait_ge(sT, g + 1)
                nc.scalar.activation(sgT[:, 4 * g:4 * g + 4, :], tb[g % 2][:, 0:4 * ROWS].rearrange("p (t r) -> p t r", t=4),
                                     ACT.Copy).then_inc(sT_out, 1)

        def score(pe, g):
            pe.wait_ge(sT_out, g + 1)
            if g >= 4:
                pe.wait_ge(key_done, g - 3)
            for t in range(4):
                mm = nc.tensor.matmul(k.banks[g % 4][0:ROWS, 72 * t:72 * t + 72], sgT[:, 4 * g + t, :], sig[:], start=True, stop=True)
            mm.then_inc(sc_full, 1)

        @block.tensor
        def _(pe):
            pe.wait_ge(consts, 1)
            pe.wait_ge(sig_done, 1)
            for g in range(TILES // 4):
                if g % 2 == 0:
                    pe.wait_ge(sgn_done, g // 2 + 1)
                if g >= 2:
                    pe.wait_ge(sT_out, g - 1)
                for t in range(4):
                    mm = nc.tensor.transpose(tb[g % 2][:, t * ROWS:(t + 1) * ROWS], sgn[:, 4 * g + t, :], ident16[:])
                mm.then_inc(sT, 1)
                if g >= 1:
                    score(pe, g - 1)
            score(pe, TILES // 4 - 1)
            pe.wait_ge(cum_done, 1)
            for g in range(4):
                nc.tensor.matmul(k.banks[g][0:ROWS, :], tri[:], oh[:, 8 * g:8 * g + 8, :], start=True, stop=False)
                half, first = divmod(8 * g, HALF)
                if half:
                    nc.tensor.matmul(k.banks[g][0:ROWS, :], all_one[:], bc(cum[:, 0, HALF, :].unsqueeze(1), [ROWS, 8, EXPERTS]),
                                     start=False, stop=False)
                nc.tensor.matmul(k.banks[g][0:ROWS, :], all_one[:], cum[:, half, first:first + 8, :], start=False, stop=True)
            for half in range(2):
                mm = nc.tensor.matmul(k.banks[4][0:ROWS, 0:EXPERTS], all_one[:], cum[:, half, HALF, :], start=(half == 0), stop=(half == 1))
            mm.then_inc(pre_full, 1)

        @block.gpsimd
        def _(pool):
            pool.wait_ge(w_in, 16 * LOADS)
            nc.gpsimd.tensor_copy(k.xf[:, :, DIM:ROW].bitcast(I32), number[:].unsqueeze(2)).then_inc(numbered, 1)
            pool.wait_ge(numbered, 1)
            pool.wait_ge(x_done, 6 * TILES // 8)
            pool.wait_ge(x_two, TILES // 8)
            nc.gpsimd.tensor_tensor(k.h[:], k.h[:], x5[:], ALU.add).then_inc(h_added, 1)
            for t in range(TILES):
                if t % 8 == 0:
                    pool.wait_ge(pos_done, t // 8 + 1)
                nc.gpsimd.indirect_dma_start(out=k.x_slots, out_offset=bass.IndirectOffsetOnAxis(ap=k.pos[:, t:t + 1], axis=0),
                                             in_=k.xf[:, t, :], in_offset=None).then_inc(scattered, 16)
            pool.wait_ge(scattered, 16 * TILES)


def expert_stage(nc, a, k):
    with Stage(nc) as ctx:
        sb = lambda n, s, d=F32: ctx.enter_context(nc.sbuf_tensor(n, s, d))
        sem = lambda n: ctx.semaphore("e_" + n)
        NB = 16
        COLS = NB * SLOT
        STEPS = BLOCKS // NB
        CHUNK = COLS // 128
        edge = sb("edge", [128, GRID])
        rows = sb("e_rows", [128, 2, CHUNK, ROW])
        token = sb("token", [128, SLOTS // 128], I32)
        to_row = sb("to_row", [128, 2, CHUNK], I32)
        PITCH = 128 + SLOT
        xt = sb("e_xt", [DIM, 2, CHUNK, 4 * PITCH])
        sig = sb("e_sig", [128, 2, COLS])
        below = sb("below", [128, 2, GRID - 1, COLS], BF16)
        lines = sb("lines", [128, 2, NB, GRID, 2])
        line = sb("line", [128, 2, NB, 2, SLOT])
        hid = sb("hid", [128, 2, CHUNK, 4 * PITCH])
        hrow = sb("hrow", [128, 2, CHUNK, DIM])
        out = sb("e_out", [128, 2, CHUNK, DIM])
        names = ("edge_in", "x_full", "x_out", "r_full", "r_out", "d_full", "sig_done", "mask_done", "lines_in", "line_set", "pick", "mul_done",
                 "hid_done", "y_full", "y_out", "token_in", "to_row_set", "tally", "tally_pe", "tally_pool")
        (edge_in, x_full, x_out, r_full, r_out, d_full, sig_done, mask_done, lines_in, line_set, pick, mul_done,
         hid_done, y_full, y_out, token_in, to_row_set, tally, tally_pe, tally_pool) = (sem(n) for n in names)
        rows_in, stored = [sem("rows_in0"), sem("rows_in1")], [sem("stored0"), sem("stored1")]
        x_bank, r_bank, d_bank, y_bank = k.banks[0:2], k.banks[2:4], k.banks[4:6], k.banks[6:8]
        src_v = k.x_slots.rearrange("(n c p) d -> p n c d", p=128, c=CHUNK)
        cleared = sem("cleared")
        block = ctx.enter_context(nc.Block())

        def own_columns(buf, u):
            return buf[:, u, :, :].rearrange("p c (j w) -> p c j w", w=PITCH)[:, :, :, 0:SLOT]


        def owners_of(engine, it, u, half):
            return nc.values_load_multi_w_load_instructions(k.owner_row[0:1, bass.ds(2 * NB * it + NB * u + 8 * half, 8)],
                                                            engines=[engine], min_val=0, max_val=EXPERTS - 1)[1]

        @block.sync
        def _(sp):
            sp.dma_start(edge[:], a["edge"].partition_broadcast(128)).then_inc(edge_in, 16)

            def body(it):
                for u in range(2):
                    at_least(sp, x_full, 2 * it + u - 1)
                    at_least(sp, token_in, 2 * it + u - 1)
                    sp.dma_start(rows[:, u, :, :], src_v[:, bass.ds(2 * it + u, 1), :, :].rearrange("p n c d -> p (n c) d")).then_inc(rows_in[u], 16)
            peeled(sp, STEPS // 2, body)

        @block.tensor
        def _(pe):
            def products(it, u, bank, src, weights, filled, read):
                for half in range(2):
                    owners = owners_of(mybir.EngineType.PE, it, u, half)
                    if half == 0:
                        pe.wait_ge(*filled)
                        at_least(pe, *read)
                        carry_waits(pe, tally_pe)
                    for b, e in enumerate(owners):
                        c, j = divmod(8 * half + b, 4)
                        mm = nc.tensor.matmul(bank[:, c * DIM:(c + 1) * DIM], src[:, u, c, 128 * j:128 * j + 128],
                                              weights[:, bass.ds(e * DIM, DIM)], start=(j == 0), stop=(j == 3))
                return mm

            def down(it, u):
                n = 2 * it + u
                pe.wait_ge(rows_in[u], 16 * (it + 1))
                at_least(pe, x_out, n - 1)
                carry_waits(pe, tally_pe)
                for c in range(CHUNK):
                    mm = nc.tensor.transpose(x_bank[u][:, c * 128:(c + 1) * 128], rows[:, u, c, 0:DIM], k.ident[:])
                mm.then_inc(x_full, 1)
                products(it, u, r_bank[u], xt, k.wd, (x_out, n + 1), (r_out, n - 1)).then_inc(r_full, 1)
                pe.wait_ge(r_out, n + 1)
                at_least(pe, sig_done, n - 1)
                carry_waits(pe, tally_pe)
                for c in range(CHUNK):
                    mm = nc.tensor.transpose(d_bank[u][:, c * 128:(c + 1) * 128], hrow[:, u, c, :], k.ident[:])
                mm.then_inc(d_full, 1)

            def up(it, u):
                n = 2 * it + u
                products(it, u, y_bank[u], hid, k.wu, (hid_done, n + 1), (y_out, n - 1)).then_inc(y_full, 1)

            down(0, 0)
            down(0, 1)
            down(1, 0)
            up(0, 0)
            down(1, 1)
            up(0, 1)
            with pe.Fori(2, STEPS // 2) as it:
                for u in range(2):
                    down(it, u)
                    up(it - 1, u)
            up(STEPS // 2 - 1, 0)
            up(STEPS // 2 - 1, 1)

        @block.scalar
        def _(act):
            act.wait_ge(edge_in, 16)
            act.wait_ge(cleared, 2)

            def masks(it, u):
                n = 2 * it + u
                act.wait_ge(x_full, n + 1)
                at_least(act, r_full, n - 1)
                nc.scalar.activation(own_columns(xt, u), x_bank[u][:].rearrange("p (c j s) -> p c j s", c=CHUNK, j=4), ACT.Copy).then_inc(x_out, 1)
                act.wait_ge(r_full, n + 1)
                at_least(act, d_full, n - 1)
                nc.scalar.activation(hrow[:, u, :, :].rearrange("p c d -> p (c d)"), r_bank[u][:], ACT.Copy).then_inc(r_out, 1)
                act.wait_ge(d_full, n + 1)
                at_least(act, mul_done, n - 1)
                nc.scalar.activation(sig[:, u, :], d_bank[u][:], ACT.Sigmoid).then_inc(sig_done, 1)
                act.wait_ge(sig_done, n + 1)
                at_least(act, pick, (2 * GRID - 2) * (n - 1))
                for i in range(1, GRID):
                    nc.scalar.activation(below[:, u, i - 1, :], sig[:, u, :], ACT.Relu, bias=edge[:, i:i + 1],
                                         scale=-float(GRID)).then_inc(mask_done, 1)

            def results(it, u):
                n = 2 * it + u
                act.wait_ge(y_full, n + 1)
                at_least(act, stored[u], 16 * CHUNK * it)
                nc.scalar.activation(out[:, u, :, :].rearrange("p c d -> p (c d)"), y_bank[u][:], ACT.Copy).then_inc(y_out, 1)

            masks(0, 0)
            masks(0, 1)
            masks(1, 0)
            results(0, 0)
            masks(1, 1)
            results(0, 1)
            with act.Fori(2, STEPS // 2) as it:
                for u in range(2):
                    masks(it, u)
                    results(it - 1, u)
            results(STEPS // 2 - 1, 0)
            results(STEPS // 2 - 1, 1)
        @block.gpsimd
        def _(pool):
            def fetch(it, u):
                n = 2 * it + u
                pool.wait_ge(rows_in[u], 16 * (it + 1))
                carry_waits(pool, tally_pool)
                nc.gpsimd.tensor_copy(token[:, bass.ds(CHUNK * n, CHUNK)], rows[:, u, :, DIM:ROW].bitcast(I32)
                                      .rearrange("p c o -> p (c o)")).then_inc(token_in, 1)
                for half in range(2):
                    owners = owners_of(mybir.EngineType.Pool, it, u, half)
                    if half == 0:
                        at_least(pool, pick, (2 * GRID - 2) * (n - 1))
                        carry_waits(pool, tally_pool)
                    for b, e in enumerate(owners):
                        nc.gpsimd.tensor_copy(lines[:, u, 8 * half + b, :, :].rearrange("p i c -> p (i c)"),
                                              k.table[:, bass.ds(e * 2 * GRID, 2 * GRID)]).then_inc(lines_in, 1)
                pool.wait_ge(lines_in, NB * (n + 1))
                at_least(pool, hid_done, n - 1)
                carry_waits(pool, tally_pool)
                for t in range(2):
                    part = slice(8 * t, 8 * t + 8)
                    nc.gpsimd.tensor_copy(line[:, u, part, :, :], bc(lines[:, u, part, 0, :].unsqueeze(3), [128, 8, 2, SLOT])).then_inc(line_set, 1)

            def add(it, u):
                n = 2 * it + u
                pool.wait_ge(mul_done, n + 1)
                at_least(pool, y_full, n - 1)
                nc.gpsimd.tensor_tensor(own_columns(hid, u), line[:, u, :, 1, :].rearrange("p (c j) s -> p c j s", j=4),
                                        line[:, u, :, 0, :].rearrange("p (c j) s -> p c j s", j=4), ALU.add).then_inc(hid_done, 1)

            def store(it, u):
                n = 2 * it + u
                at_least(pool, stored[u], 16 * CHUNK * it)
                pool.wait_ge(token_in, n + 1)
                carry_waits(pool, tally_pool)
                nc.gpsimd.tensor_copy(to_row[:, u, :], token[:, bass.ds(CHUNK * n, CHUNK)]).then_inc(to_row_set, 1)
                pool.wait_ge(to_row_set, n + 1)
                pool.wait_ge(y_out, n + 1)
                carry_waits(pool, tally_pool)
                for c in range(CHUNK):
                    nc.gpsimd.indirect_dma_start(out=k.y_rows, out_offset=bass.IndirectOffsetOnAxis(ap=to_row[:, u, c:c + 1], axis=0),
                                                 in_=out[:, u, c, :], in_offset=None).then_inc(stored[u], 16)

            fetch(0, 0)
            fetch(0, 1)
            pool.wait_ge(cleared, 4)
            add(0, 0)
            fetch(1, 0)
            add(0, 1)
            store(0, 0)
            fetch(1, 1)
            add(1, 0)
            store(0, 1)
            with pool.Fori(2, STEPS // 2) as it:
                fetch(it, 0)
                add(it - 1, 1)
                store(it - 1, 0)
                fetch(it, 1)
                add(it, 0)
                store(it - 1, 1)
            add(STEPS // 2 - 1, 1)
            for u in range(2):
                store(STEPS // 2 - 1, u)
            for u in range(2):
                pool.wait_ge(stored[u], 16 * CHUNK * (STEPS // 2))

        @block.vector
        def _(dve):
            for buf in (xt, hid):
                for u in range(2):
                    nc.vector.memset(buf[:, u, :, :], 0.0).then_inc(cleared, 1)

            def body(it):
                for u in range(2):
                    n = 2 * it + u
                    base = (2 * GRID - 2) * n
                    dve.wait_ge(line_set, 2 * n + 2)
                    for i in range(1, GRID):
                        dve.wait_ge(mask_done, (GRID - 1) * n + i)
                        for t in range(2):
                            if i > 1:
                                dve.wait_ge(pick, base + 2 * i + t - 3)
                            carry_waits(dve, tally)
                            part = slice(8 * t, 8 * t + 8)
                            mask = below[:, u, i - 1, 256 * t:256 * t + 256].bitcast(U16).rearrange("p (b s) -> p b s", s=SLOT)
                            nc.vector.copy_predicated(line[:, u, part, :, :], bc(mask.unsqueeze(2), [128, 8, 2, SLOT]),
                                                      bc(lines[:, u, part, i, :].unsqueeze(3), [128, 8, 2, SLOT])).then_inc(pick, 1)
                    dve.wait_ge(pick, base + 2 * GRID - 2)
                    carry_waits(dve, tally)
                    nc.vector.scalar_tensor_tensor(line[:, u, :, 1, :],
                                                   sig[:, u, :].rearrange("p (b s) -> p b s", s=SLOT), float(GRID), line[:, u, :, 1, :],
                                                   ALU.mult, ALU.mult).then_inc(mul_done, 1)
            peeled(dve, STEPS // 2, body)


def final_stage(nc, k, out):
    with Stage(nc) as ctx:
        sem = lambda n: ctx.semaphore("f_" + n)
        back = ctx.enter_context(nc.sbuf_tensor("back", [ROWS, TILES, DIM], F32))
        loaded = [sem(f"loaded{i}") for i in range(8)]
        done, stored = sem("done"), sem("stored")
        out_v = out.rearrange("b q d -> (b q) d").rearrange("(t r) d -> r t d", r=ROWS)
        block = ctx.enter_context(nc.Block())

        y_v = k.y_rows[0:TOKENS, :].rearrange("(t r) d -> r t d", r=ROWS)

        @block.scalar
        def _(act):
            for g in range(8):
                act.dma_start(back[:, 4 * g:4 * g + 4, :], y_v[:, 4 * g:4 * g + 4, :]).then_inc(loaded[g], 16)

        @block.vector
        def _(dve):
            for g in range(8):
                dve.wait_ge(loaded[g], 16)
                for t in range(4 * g, 4 * g + 4):
                    ins = nc.vector.scalar_tensor_tensor(k.h[:, t, :], back[:, t, :], k.scale[:, t:t + 1], k.h[:, t, :], ALU.mult, ALU.add)
                    ins.then_inc(done, 1)

        @block.sync
        def _(sp):
            for g in range(8):
                sp.wait_ge(done, 4 * g + 4)
                sp.dma_start(out_v[:, 4 * g:4 * g + 4, :], k.h[:, 4 * g:4 * g + 4, :]).then_inc(stored, 16)
            sp.wait_ge(stored, 16 * 8)


class Store:
    pass


def tower_program(nc, a, out, stop=None, dbg=None):
    with ExitStack() as ctx:
        sb = lambda n, s, d=F32: ctx.enter_context(nc.sbuf_tensor(n, s, d))
        k = Store()
        k.banks = [ctx.enter_context(nc.psum_tensor(f"bank{i}", [128, 512], F32)) for i in range(8)]
        k.ident = sb("ident", [128, 128])
        k.h = sb("h", [ROWS, TILES, DIM])
        k.raw = sb("raw", [ROWS, TILES, 6])
        k.bias_dram = nc.dram_tensor("bias_dram", (HEADS, QUERIES * KEYS), F32, kind="Internal").ap()
        k.three = sb("three", [128, 1])
        k.kT, k.v = sb("kT", [DIM, XH, SRC]), sb("cv", [SHALF, 2, XH, DIM])
        k.wq, k.wo = sb("cwq", [DIM, DIM]), sb("cwo", [DIM, DIM])
        k.bq, k.bk, k.own, k.bk_own = sb("cbq", [DIM, 1]), sb("cbk", [DIM, 1]), sb("own", [DIM, XH]), sb("bk_own", [DIM, XH])
        k.bv, k.bo = sb("cbv", [SHALF, DIM]), sb("cbo", [ROWS, DIM])
        source = ctx.enter_context(ExitStack())
        sb0 = lambda n, s: source.enter_context(nc.sbuf_tensor(n, s, F32))
        k.srcT, k.valT = sb0("srcT", [128, LCH, SRC]), sb0("valT", [128, LCH, SRC])
        k.wk, k.wv_x = sb0("cwk", [128, LCH, DIM]), sb0("cwv", [128, LCH, DIM])
        with ExitStack() as first:
            sb1 = lambda n, s, d=F32: first.enter_context(nc.sbuf_tensor(n, s, d))
            k.mh = sb1("mh", [AUG, HEADS, AUG])
            k.wv = sb1("wv", [AUG, HEADS, VD])
            k.pw = sb1("pw", [128, 6, DIM])
            k.prow = sb1("prow", [128, DIM])
            k.bias = sb1("bias", [CH, CHUNKS, KEYS])
            k.xT = sb1("xT", [AUG, 2, GROUP * KEYS])
            k.xn = sb1("xn", [KHALF, 2, GROUP, 2, AUG])
            setup_stage(nc, a, k, ctx)
            token_stage(nc, a, k)
        if stop == "token":
            return dump(nc, k.h, dbg)
        band_stage(nc, a, k)
        if stop == "band":
            return dump(nc, k.h, dbg)
        source.close()
        k.wd = sb("wd", [DIM, EXPERTS * DIM])
        k.sums = sb("sums", [DIM, EXPERTS])
        k.wu = sb("wu", [DIM, EXPERTS * DIM])
        k.table = sb("table", [128, EXPERTS * GRID * 2])
        k.x_slots = nc.dram_tensor("x_slots", (SLOTS, ROW), F32, kind="Internal").ap()
        k.y_rows = nc.dram_tensor("y_rows", (SPARE + SLOTS, DIM), F32, kind="Internal").ap()
        k.owner_dram = nc.dram_tensor("owner_dram", (BLOCKS, 1), I32, kind="Internal").ap()
        cross_stage(nc, a, k)
        if stop == "cross":
            return dump(nc, k.h, dbg)
        k.owner_row = sb("owner_row", [1, BLOCKS], I32)
        k.pos = sb("pos", [ROWS, TILES], I32)
        k.scale = sb("scale", [ROWS, TILES])
        with nc.sbuf_tensor("xf", [ROWS, TILES, ROW], F32) as k.xf:
            route_stage(nc, a, k)
        expert_stage(nc, a, k)
        final_stage(nc, k, out)


def dump(nc, buf, dbg):
    with nc.semaphore("dumped") as dumped, nc.Block() as block:
        @block.sync
        def _(sp):
            sp.dma_start(dbg, buf[:]).then_inc(dumped, 16)
            sp.wait_ge(dumped, 16)


def layouts(i):
    import numpy as np
    f = {n: np.asarray(v) for n, v in i.items()}
    x = f["x"]
    kvw = f["L0_tok_kv_w"].reshape(HEADS, KD + VD, DIM_IN)
    kv_bn = np.stack([f[f"L0_tok_kv_{c}"] for c in "gbmv"]).reshape(4, HEADS, KD + VD)
    o = {
        "xT": x.transpose(2, 0, 1).reshape(DIM_IN, BATCH * KEYS),
        "xn": x.reshape(BATCH, 2, KHALF, DIM_IN).transpose(2, 0, 1, 3).reshape(KHALF, BATCH * 2, DIM_IN),
        "q_w": f["L0_tok_q_w"].reshape(HEADS, KD, DIM_IN).transpose(1, 0, 2),
        "k_w": kvw[:, :KD].transpose(1, 0, 2),
        "v_w": kvw[:, KD:].transpose(1, 0, 2),
        "q_bn": np.stack([f[f"L0_tok_q_{c}"] for c in "gbmv"]).reshape(4, HEADS, KD).transpose(2, 0, 1),
        "k_bn": kv_bn[:, :, :KD].transpose(2, 0, 1),
        "v_bn": kv_bn[:, :, KD:].transpose(2, 0, 1),
        "proj_w": f["L0_tok_proj_w"].T.reshape(6, 128, DIM).transpose(1, 0, 2),
        "proj_bn": np.stack([f[f"L0_tok_proj_{c}"] for c in "gbmv"]),
        "bias_t": f["L0_tok_attention_biases"].T.reshape(2, KHALF, HEADS).transpose(1, 0, 2),
        "bias_idx": f["L0_tok_bias_idxs"].reshape(-1),
        "off_col": (np.arange(KHALF)[:, None] + KHALF * np.arange(2)[None, :]).astype(np.float32),
        "ident": np.eye(128, dtype=np.float32),
    }
    half = np.arange(DIM // 2, dtype=np.float32)
    theta = np.float32(10000.0) ** (np.float32(-2.0) * (half - np.float32(1.0)) / np.float32(DIM))
    angle = np.arange(QUERIES, dtype=np.float32)[:, None] * theta[None, :]
    cos, sin = np.repeat(np.cos(angle).T, 2, axis=0), np.repeat(np.sin(angle).T, 2, axis=0)
    sin[1::2] *= -1.0
    swap = np.arange(DIM) ^ 1
    q, kk = np.arange(ROWS)[:, None], np.arange(ROWS)[None, :]
    wq, wk = f["L0_attn_W_q"], f["L0_attn_W_k"]
    o |= {
        "band_w": np.stack([wq, wq[:, swap], wk, wk[:, swap]], axis=1),
        "u_v": f["L0_attn_u_v"],
        "v_v": f["L0_attn_v_v"].reshape(DIM),
        "trig": np.stack([cos, sin], axis=1).astype(np.float32),
        "band_mask": np.where((kk <= q) & (kk // QUERIES == q // QUERIES), 0.0, -1e30).astype(np.float32),
    }

    g = lambda n: f["L1_attn_" + n]
    o |= {
        "srcT": g("source_embedding").T.reshape(LCH, 128, SRC).transpose(1, 0, 2),
        "valT": g("value_embedding").T.reshape(LCH, 128, SRC).transpose(1, 0, 2),
        "x_wk": g("Wk").reshape(LCH, 128, DIM).transpose(1, 0, 2),
        "x_wv": g("Wv").reshape(LCH, 128, DIM).transpose(1, 0, 2),
        "x_wq": g("Wq"),
        "x_wo": g("Wo"),
        "x_bq": g("bq")[:, None],
        "x_bk": g("bk")[:, None],
        "own": (np.arange(DIM)[:, None] // XE == np.arange(XH)[None, :]).astype(np.float32),
        "x_bv": g("bv"),
        "x_bo": g("bo"),
    }
    g = lambda n: f["L1_ffn_" + n]
    cells = np.arange(GRID - 1, -1, -1)
    lines = np.stack([g("spline_bases"), g("spline_slopes")], axis=3)[:, :, cells]
    lines = lines.transpose(1, 0, 2, 3).reshape(DIM, EXPERTS * GRID * 2)
    o |= {
        "gamma": g("gamma"), "beta": g("beta"), "scale": g("scale"),
        "wd": g("Wd").transpose(2, 0, 1).reshape(DIM, EXPERTS * DIM),
        "wu": g("Wu").transpose(2, 0, 1).reshape(DIM, EXPERTS * DIM),
        "spline": lines,
        "cell": cells.astype(np.float32),
        "edge": (GRID - np.arange(GRID)).astype(np.float32),
        "tie": -np.concatenate([np.arange(CLUSTERS), np.arange(EXPERTS) % PER_CLUSTER]).astype(np.float32),
        "tri": np.triu(np.ones((ROWS, ROWS), np.float32), 1),
        "ident98": np.eye(ROWS, dtype=np.float32),
        "spare": (SPARE + np.arange(SLOTS)).reshape(4, 128, SLOTS // 512).transpose(1, 0, 2).astype(np.int32),
        "number": np.arange(TOKENS).reshape(TILES, ROWS).T.astype(np.int32),
        "block_col": (np.arange(ROWS)[:, None] + OWN_P * np.arange(2)[None, :]).astype(np.float32),
    }
    return {n: np.ascontiguousarray(v) for n, v in o.items()}


def kernel(**inputs):
    import numpy as np
    import concourse.bacc as bacc
    from concourse.bass_utils import run_bass_kernel_spmd

    arrays = {f"in_{n}": v for n, v in layouts(inputs).items()}
    nc = bacc.Bacc("TRN2", target_bir_lowering=False, num_devices=1)
    a = {n[3:]: nc.dram_tensor(n, v.shape, mybir.dt.from_np(v.dtype), kind="ExternalInput").ap() for n, v in arrays.items()}
    out = nc.dram_tensor("out", (BATCH, QUERIES, DIM), F32, kind="ExternalOutput").ap()
    tower_program(nc, a, out)
    r = run_bass_kernel_spmd(nc, [arrays], core_ids=[0])
    return np.asarray(r.results[0]["out"])
```
